# Optimizing a Trainium2 kernel written in Bass

```python
import numpy as np
import jax
import jax.numpy as jnp

def _softmax(x, axis=-1):
    return jax.nn.softmax(x, axis=axis)

def _gelu(x):
    return jax.nn.gelu(x, approximate=True)

def _silu(x):
    return jax.nn.silu(x)

def _sigmoid(x):
    return jax.nn.sigmoid(x)

def _layernorm(x, axis=-1, eps=1e-05):
    m = jnp.mean(x, axis=axis, keepdims=True)
    v = jnp.var(x, axis=axis, keepdims=True)
    return (x - m) / jnp.sqrt(v + eps)

def _scatter_add(tgt, idx, src, axis=0):
    return tgt.at[idx].add(src)

def _segment_sum(src, seg, n):
    return jax.ops.segment_sum(src, seg, n)
kernel_name = 'mk_xattn_ffn_d2_seqx_r4_8cebcd'

def setup_inputs(seed: int=0):
    np.random.seed(seed)
    _w = jnp.asarray

    def _rec_inputs():
        import jax
        import jax.numpy as jnp
        _rk = jax.random.key(seed)
        x = -0.0002928 + 1 * jax.random.normal(jax.random.fold_in(_rk, 1), (4, 512, 256), jnp.float32)
        _lenS = 512 - jax.random.randint(jax.random.fold_in(_rk, 7), (4,), 0, max(1, 512 // 4) + 1, jnp.int32)
        _lenS2 = 512 - jax.random.randint(jax.random.fold_in(_rk, 8), (4,), 0, max(1, 512 // 4) + 1, jnp.int32)
        _ctx_1024P = jax.random.normal(jax.random.fold_in(_rk, 11), (4, 16, 256), jnp.float32)
        _ctx_1024c = jax.random.dirichlet(jax.random.fold_in(_rk, 511), 0.3 * jnp.ones((16,), jnp.float32), (4, 512))
        _ctx_1024t = jnp.einsum('bsk,bkd->bsd', _ctx_1024c, _ctx_1024P)
        _ctx_1024t = _ctx_1024t * jax.lax.rsqrt(jnp.mean(jnp.square(_ctx_1024t)) + 1e-12) * 0.953939
        ctx_1024 = -1.39393e-06 + 0.999914 * (_ctx_1024t + 0.3 * jax.random.normal(jax.random.fold_in(_rk, 611), (4, 512, 256), jnp.float32))
        fside_Bx16xSxS2_0 = 9.80324e-06 + 0.100009 * jax.random.normal(jax.random.fold_in(_rk, 13), (4, 16, 512, 512), jnp.float32)
        fside_SxS2_0 = -2.64403e-05 + 0.100002 * jax.random.normal(jax.random.fold_in(_rk, 15), (512, 512), jnp.float32)
        _validS = jnp.arange(512)[None, :] < _lenS[:, None]
        _validS2 = jnp.arange(512)[None, :] < _lenS2[:, None]
        _causal = jnp.tril(jnp.ones((512, 512), dtype=bool))
        mask_Bx1xSxS2_ik1 = jnp.where(jnp.broadcast_to(_validS2[:, None, None, :], (4, 1, 512, 512)), 1, 0).astype(jnp.int32)
        mask_BxS2_bf0 = jnp.logical_not(jnp.ones((4, 512), dtype=bool))
        return (x, ctx_1024, fside_Bx16xSxS2_0, fside_SxS2_0, mask_Bx1xSxS2_ik1, mask_BxS2_bf0)
    x, ctx_1024, fside_Bx16xSxS2_0, fside_SxS2_0, mask_Bx1xSxS2_ik1, mask_BxS2_bf0 = _rec_inputs()

    def _L0_xattn_setup():
        import jax, jax.numpy as jnp
        import numpy as np
        B, S, D, H = (2, 512, 256, 16)
        DK = D // H
        key = jax.random.key(seed)
        ks = jax.random.split(key, 8)
        inp = {'Q': jax.random.normal(ks[0], (B, S, D), dtype=jnp.float32), 'K': jax.random.normal(ks[1], (B, S, D), dtype=jnp.float32), 'V': jax.random.normal(ks[2], (B, S, D), dtype=jnp.float32), 'mask': jax.random.randint(ks[3], (B, 1, S, S), 0, 2, dtype=jnp.int32), 'Wq': jax.random.normal(ks[4], (D, D), dtype=jnp.float32) / np.sqrt(D), 'Wk': jax.random.normal(ks[5], (D, D), dtype=jnp.float32) / np.sqrt(D), 'Wv': jax.random.normal(ks[6], (D, D), dtype=jnp.float32) / np.sqrt(D), 'Wo': jax.random.normal(ks[7], (D, D), dtype=jnp.float32) / np.sqrt(D)}
        return inp
    _L0_xattn_all = _L0_xattn_setup()
    _L0_xattn_in = {k: v for k, v in _L0_xattn_all.items() if k in ('Wq', 'Wk', 'Wv', 'Wo')}
    del _L0_xattn_all

    def _L0_ffn_setup():
        import jax, jax.numpy as jnp
        import numpy as np
        D_MODEL = 256
        N_HEAD = 16
        HEAD_DIM = D_MODEL // N_HEAD
        D_FF = 1024
        N_EXPERTS = 4
        EPS = 1e-05

        def _layer_norm(x, gamma, beta):
            mu = jnp.mean(x, axis=-1, keepdims=True)
            var = jnp.mean((x - mu) ** 2, axis=-1, keepdims=True)
            return (x - mu) / jnp.sqrt(var + EPS) * gamma + beta
        key = jax.random.key(seed)
        ks = jax.random.split(key, 20)
        f32 = jnp.float32
        sc = 1.0 / np.sqrt(D_MODEL)
        scf = 1.0 / np.sqrt(D_FF)
        return {'src': jax.random.normal(ks[0], (4, 128, D_MODEL), f32), 'Wq': jax.random.normal(ks[1], (D_MODEL, D_MODEL), f32) * sc, 'bq': jnp.zeros((D_MODEL,), f32), 'Wk': jax.random.normal(ks[2], (D_MODEL, D_MODEL), f32) * sc, 'bk': jnp.zeros((D_MODEL,), f32), 'Wv': jax.random.normal(ks[3], (D_MODEL, D_MODEL), f32) * sc, 'bv': jnp.zeros((D_MODEL,), f32), 'Wo': jax.random.normal(ks[4], (D_MODEL, D_MODEL), f32) * sc, 'bo': jnp.zeros((D_MODEL,), f32), 'router_w': jax.random.normal(ks[5], (D_MODEL, 1), f32) * 0.05, 'router_b': jnp.zeros((1,), f32), 'W1': jax.random.normal(ks[6], (N_EXPERTS, D_MODEL, D_FF), f32) * sc, 'b1': jnp.zeros((N_EXPERTS, D_FF), f32), 'W2': jax.random.normal(ks[7], (N_EXPERTS, D_FF, D_MODEL), f32) * scf, 'b2': jnp.zeros((N_EXPERTS, D_MODEL), f32), 'ln1_g': jnp.ones((D_MODEL,), f32), 'ln1_b': jnp.zeros((D_MODEL,), f32), 'ln2_g': jnp.ones((D_MODEL,), f32), 'ln2_b': jnp.zeros((D_MODEL,), f32)}
    _L0_ffn_all = _L0_ffn_setup()
    _L0_ffn_in = {k: v for k, v in _L0_ffn_all.items() if k in ('Wq', 'bq', 'Wk', 'bk', 'Wv', 'bv', 'Wo', 'bo', 'router_w', 'router_b', 'W1', 'b1', 'W2', 'b2', 'ln1_g', 'ln1_b', 'ln2_g', 'ln2_b')}
    del _L0_ffn_all

    def _L1_xattn_setup():
        import jax, jax.numpy as jnp
        import numpy as np
        E = 256
        H = 16
        D = E // H
        key = jax.random.key(seed)
        ks = jax.random.split(key, 12)
        B, T, S = (2, 512, 512)
        inp = {'query': jax.random.normal(ks[0], (B, T, E), jnp.float32), 'key': jax.random.normal(ks[1], (B, S, E), jnp.float32), 'value': jax.random.normal(ks[2], (B, S, E), jnp.float32), 'spatial_bias': jax.random.normal(ks[3], (B, H, T, S), jnp.float32) * 0.1, 'directional_bias': jax.random.normal(ks[4], (B, H, T, S), jnp.float32) * 0.1, 'key_padding_mask': jnp.zeros((B, S), dtype=bool), 'attn_mask': jax.random.normal(ks[5], (T, S), jnp.float32) * 0.1, 'Wq': jax.random.normal(ks[6], (E, E), jnp.float32) / np.sqrt(E), 'bq': jnp.zeros((E,), jnp.float32), 'Wk': jax.random.normal(ks[7], (E, E), jnp.float32) / np.sqrt(E), 'bk': jnp.zeros((E,), jnp.float32), 'Wv': jax.random.normal(ks[8], (E, E), jnp.float32) / np.sqrt(E), 'bv': jnp.zeros((E,), jnp.float32), 'Wo': jax.random.normal(ks[9], (E, E), jnp.float32) / np.sqrt(E), 'bo': jnp.zeros((E,), jnp.float32)}
        return inp
    _L1_xattn_all = _L1_xattn_setup()
    _L1_xattn_in = {k: v for k, v in _L1_xattn_all.items() if k in ('Wq', 'bq', 'Wk', 'bk', 'Wv', 'bv', 'Wo', 'bo')}
    del _L1_xattn_all

    def _L1_ffn_setup():
        import math
        import jax, jax.numpy as jnp
        import numpy as np
        B, T, D, H, E, K, S = (4, 1024, 256, 512, 16, 2, 2)
        ROUTE_SCALE = 1.0

        def _swiglu(x, w1, w3, w2):
            return jax.nn.silu(x @ w1) * (x @ w3) @ w2
        key = jax.random.key(seed)
        ks = jax.random.split(key, 9)
        s = 0.02
        return {'x': jax.random.normal(ks[0], (B, T, D), jnp.float32), 'gate_w': jax.random.normal(ks[1], (D, E), jnp.float32) * s, 'gate_b': jnp.zeros((E,), jnp.float32), 'ew1': jax.random.normal(ks[2], (E, D, H), jnp.float32) * s, 'ew3': jax.random.normal(ks[3], (E, D, H), jnp.float32) * s, 'ew2': jax.random.normal(ks[4], (E, H, D), jnp.float32) * s, 'sw1': jax.random.normal(ks[5], (S, D, H), jnp.float32) * s, 'sw3': jax.random.normal(ks[6], (S, D, H), jnp.float32) * s, 'sw2': jax.random.normal(ks[7], (S, H, D), jnp.float32) * s}
    _L1_ffn_all = _L1_ffn_setup()
    _L1_ffn_in = {k: v for k, v in _L1_ffn_all.items() if k in ('gate_w', 'gate_b', 'ew1', 'ew3', 'ew2', 'sw1', 'sw3', 'sw2')}
    del _L1_ffn_all
    return {'x': x, 'ctx_1024': ctx_1024, 'fside_Bx16xSxS2_0': fside_Bx16xSxS2_0, 'fside_SxS2_0': fside_SxS2_0, 'mask_Bx1xSxS2_ik1': mask_Bx1xSxS2_ik1, 'mask_BxS2_bf0': mask_BxS2_bf0, 'L0_xattn_Wq': _L0_xattn_in['Wq'], 'L0_xattn_Wk': _L0_xattn_in['Wk'], 'L0_xattn_Wv': _L0_xattn_in['Wv'], 'L0_xattn_Wo': _L0_xattn_in['Wo'], 'L0_ffn_Wq': _L0_ffn_in['Wq'], 'L0_ffn_bq': _L0_ffn_in['bq'], 'L0_ffn_Wk': _L0_ffn_in['Wk'], 'L0_ffn_bk': _L0_ffn_in['bk'], 'L0_ffn_Wv': _L0_ffn_in['Wv'], 'L0_ffn_bv': _L0_ffn_in['bv'], 'L0_ffn_Wo': _L0_ffn_in['Wo'], 'L0_ffn_bo': _L0_ffn_in['bo'], 'L0_ffn_router_w': _L0_ffn_in['router_w'], 'L0_ffn_router_b': _L0_ffn_in['router_b'], 'L0_ffn_W1': _L0_ffn_in['W1'], 'L0_ffn_b1': _L0_ffn_in['b1'], 'L0_ffn_W2': _L0_ffn_in['W2'], 'L0_ffn_b2': _L0_ffn_in['b2'], 'L0_ffn_ln1_g': _L0_ffn_in['ln1_g'], 'L0_ffn_ln1_b': _L0_ffn_in['ln1_b'], 'L0_ffn_ln2_g': _L0_ffn_in['ln2_g'], 'L0_ffn_ln2_b': _L0_ffn_in['ln2_b'], 'L1_xattn_Wq': _L1_xattn_in['Wq'], 'L1_xattn_bq': _L1_xattn_in['bq'], 'L1_xattn_Wk': _L1_xattn_in['Wk'], 'L1_xattn_bk': _L1_xattn_in['bk'], 'L1_xattn_Wv': _L1_xattn_in['Wv'], 'L1_xattn_bv': _L1_xattn_in['bv'], 'L1_xattn_Wo': _L1_xattn_in['Wo'], 'L1_xattn_bo': _L1_xattn_in['bo'], 'L1_ffn_gate_w': _L1_ffn_in['gate_w'], 'L1_ffn_gate_b': _L1_ffn_in['gate_b'], 'L1_ffn_ew1': _L1_ffn_in['ew1'], 'L1_ffn_ew3': _L1_ffn_in['ew3'], 'L1_ffn_ew2': _L1_ffn_in['ew2'], 'L1_ffn_sw1': _L1_ffn_in['sw1'], 'L1_ffn_sw3': _L1_ffn_in['sw3'], 'L1_ffn_sw2': _L1_ffn_in['sw2']}

def reference(x, ctx_1024, fside_Bx16xSxS2_0, fside_SxS2_0, mask_Bx1xSxS2_ik1, mask_BxS2_bf0, L0_xattn_Wq, L0_xattn_Wk, L0_xattn_Wv, L0_xattn_Wo, L0_ffn_Wq, L0_ffn_bq, L0_ffn_Wk, L0_ffn_bk, L0_ffn_Wv, L0_ffn_bv, L0_ffn_Wo, L0_ffn_bo, L0_ffn_router_w, L0_ffn_router_b, L0_ffn_W1, L0_ffn_b1, L0_ffn_W2, L0_ffn_b2, L0_ffn_ln1_g, L0_ffn_ln1_b, L0_ffn_ln2_g, L0_ffn_ln2_b, L1_xattn_Wq, L1_xattn_bq, L1_xattn_Wk, L1_xattn_bk, L1_xattn_Wv, L1_xattn_bv, L1_xattn_Wo, L1_xattn_bo, L1_ffn_gate_w, L1_ffn_gate_b, L1_ffn_ew1, L1_ffn_ew3, L1_ffn_ew2, L1_ffn_sw1, L1_ffn_sw3, L1_ffn_sw2):
    import jax
    import jax.numpy as jnp

    def _L0_xattn_ref(Q, K, V, mask, Wq, Wk, Wv, Wo):
        import jax, jax.numpy as jnp
        import numpy as np
        B, S, D, H = (2, 512, 256, 16)
        DK = D // H
        b, s, d = Q.shape
        q = (Q @ Wq.T).reshape(b, s, H, DK).transpose(0, 2, 1, 3)
        k = (K @ Wk.T).reshape(b, -1, H, DK).transpose(0, 2, 1, 3)
        v = (V @ Wv.T).reshape(b, -1, H, DK).transpose(0, 2, 1, 3)
        score = jnp.einsum('bhqd,bhkd->bhqk', q, k) / jnp.sqrt(jnp.float32(DK))
        score = jnp.where(mask == 0, jnp.float32(1e-09), score)
        attn = jax.nn.softmax(score, axis=-1)
        out = jnp.einsum('bhqk,bhkd->bhqd', attn, v)
        out = out.transpose(0, 2, 1, 3).reshape(b, s, d)
        return out @ Wo.T

    def _L0_ffn_ref(src, Wq, bq, Wk, bk, Wv, bv, Wo, bo, router_w, router_b, W1, b1, W2, b2, ln1_g, ln1_b, ln2_g, ln2_b):
        import jax, jax.numpy as jnp
        import numpy as np
        D_MODEL = 256
        N_HEAD = 16
        HEAD_DIM = D_MODEL // N_HEAD
        D_FF = 1024
        N_EXPERTS = 4
        EPS = 1e-05

        def _layer_norm(x, gamma, beta):
            mu = jnp.mean(x, axis=-1, keepdims=True)
            var = jnp.mean((x - mu) ** 2, axis=-1, keepdims=True)
            return (x - mu) / jnp.sqrt(var + EPS) * gamma + beta
        B, T, _ = src.shape
        q = (src @ Wq + bq).reshape(B, T, N_HEAD, HEAD_DIM)
        k = (src @ Wk + bk).reshape(B, T, N_HEAD, HEAD_DIM)
        v = (src @ Wv + bv).reshape(B, T, N_HEAD, HEAD_DIM)
        scale = HEAD_DIM ** (-0.5)
        scores = jnp.einsum('bqhd,bkhd->bhqk', q, k) * scale
        probs = jax.nn.softmax(scores, axis=-1)
        attn = jnp.einsum('bhqk,bkhd->bqhd', probs, v).reshape(B, T, D_MODEL)
        attn = attn @ Wo + bo
        x = _layer_norm(src + attn, ln1_g, ln1_b)
        keys = (x @ router_w + router_b)[..., 0]
        expert_idx = jnp.remainder(jnp.floor(keys).astype(jnp.int32), N_EXPERTS)
        ff_out = jnp.zeros_like(x)
        for e in range(N_EXPERTS):
            h = jax.nn.relu(x @ W1[e] + b1[e])
            y = h @ W2[e] + b2[e]
            ff_out = ff_out + jnp.where((expert_idx == e)[..., None], y, 0.0)
        return _layer_norm(x + ff_out, ln2_g, ln2_b)

    def _L1_xattn_ref(query, key, value, spatial_bias, directional_bias, key_padding_mask, attn_mask, Wq, bq, Wk, bk, Wv, bv, Wo, bo):
        import jax, jax.numpy as jnp
        import numpy as np
        E = 256
        H = 16
        D = E // H
        B, T, _ = query.shape
        S = key.shape[1]
        scale = D ** (-0.5)
        q = (query @ Wq.T + bq).reshape(B, T, H, D).transpose(0, 2, 1, 3)
        k = (key @ Wk.T + bk).reshape(B, S, H, D).transpose(0, 2, 1, 3)
        v = (value @ Wv.T + bv).reshape(B, S, H, D).transpose(0, 2, 1, 3)
        scores = jnp.einsum('bhtd,bhsd->bhts', q, k) * scale
        scores = scores + attn_mask[None, None, :, :]
        pad = key_padding_mask[:, None, None, :]
        scores = jnp.where(pad, -jnp.inf, scores)
        if T == S:
            scores = scores + spatial_bias + directional_bias
        probs = jax.nn.softmax(scores, axis=-1)
        out = jnp.einsum('bhts,bhsd->bhtd', probs, v)
        out = out.transpose(0, 2, 1, 3).reshape(B, T, E)
        return out @ Wo.T + bo

    def _L1_ffn_ref(x, gate_w, gate_b, ew1, ew3, ew2, sw1, sw3, sw2):
        import math
        import jax, jax.numpy as jnp
        import numpy as np
        B, T, D, H, E, K, S = (4, 1024, 256, 512, 16, 2, 2)
        ROUTE_SCALE = 1.0

        def _swiglu(x, w1, w3, w2):
            return jax.nn.silu(x @ w1) * (x @ w3) @ w2
        Bx, Tx, Dx = x.shape
        flat = x.reshape(-1, Dx)
        N = flat.shape[0]
        n_experts = gate_w.shape[1]
        logits = flat @ gate_w
        scores = jax.nn.softmax(logits.astype(jnp.float32), -1) + gate_b
        _, topi = jax.lax.top_k(scores, K)
        weights = jnp.take_along_axis(logits, topi, axis=-1) * ROUTE_SCALE
        weights = weights.astype(flat.dtype)
        capacity = math.ceil(N * K / n_experts * 1.25)

        def per_expert(gid, w1, w3, w2):
            match = topi == gid
            assigned = match.any(-1)
            w_tok = jnp.sum(jnp.where(match, weights, 0.0), -1)
            wm = jnp.where(assigned, w_tok, -jnp.inf)
            vals, idx = jax.lax.top_k(wm, capacity)
            valid = assigned[idx]
            xs = flat[idx]
            y = _swiglu(xs, w1, w3, w2) * jnp.where(valid, vals, 0.0)[:, None]
            return (idx, y)
        idxs, ys = jax.vmap(per_expert)(jnp.arange(n_experts), ew1, ew3, ew2)
        out = jnp.zeros_like(flat).at[idxs.reshape(-1)].add(ys.reshape(-1, Dx))
        shared = jax.vmap(lambda w1, w3, w2: _swiglu(flat, w1, w3, w2))(sw1, sw3, sw2)
        out = out + shared.mean(0)
        return out.reshape(Bx, Tx, Dx)
    x = x + _L0_xattn_ref(_layernorm(x, axis=-1), ctx_1024, ctx_1024, mask_Bx1xSxS2_ik1, L0_xattn_Wq, L0_xattn_Wk, L0_xattn_Wv, L0_xattn_Wo)
    x = x + _L0_ffn_ref(_layernorm(x, axis=-1), L0_ffn_Wq, L0_ffn_bq, L0_ffn_Wk, L0_ffn_bk, L0_ffn_Wv, L0_ffn_bv, L0_ffn_Wo, L0_ffn_bo, L0_ffn_router_w, L0_ffn_router_b, L0_ffn_W1, L0_ffn_b1, L0_ffn_W2, L0_ffn_b2, L0_ffn_ln1_g, L0_ffn_ln1_b, L0_ffn_ln2_g, L0_ffn_ln2_b)
    x = x + _L1_xattn_ref(_layernorm(x, axis=-1), ctx_1024, ctx_1024, fside_Bx16xSxS2_0, fside_Bx16xSxS2_0, mask_BxS2_bf0, fside_SxS2_0, L1_xattn_Wq, L1_xattn_bq, L1_xattn_Wk, L1_xattn_bk, L1_xattn_Wv, L1_xattn_bv, L1_xattn_Wo, L1_xattn_bo)
    x = x + _L1_ffn_ref(_layernorm(x, axis=-1), L1_ffn_gate_w, L1_ffn_gate_b, L1_ffn_ew1, L1_ffn_ew3, L1_ffn_ew2, L1_ffn_sw1, L1_ffn_sw3, L1_ffn_sw2)
    return x

_drawn_inputs = setup_inputs


def setup_inputs(seed=0):
    import zlib

    import numpy as np

    out = dict(_drawn_inputs(seed))
    spreads = {'L0_ffn_bq': (0.0, 0.288),
     'L0_ffn_bk': (0.0, 0.8),
     'L0_ffn_bv': (0.0, 0.1),
     'L0_ffn_bo': (0.0, 0.1),
     'L0_ffn_b1': (0.0, 0.301),
     'L0_ffn_b2': (0.0, 0.1),
     'L0_ffn_ln1_g': (1.0, 0.2),
     'L0_ffn_ln1_b': (0.0, 0.1),
     'L0_ffn_ln2_g': (1.0, 0.2),
     'L0_ffn_ln2_b': (0.0, 0.1),
     'L1_xattn_bq': (0.0, 0.762),
     'L1_xattn_bk': (0.0, 0.8),
     'L1_xattn_bv': (0.0, 0.1),
     'L1_xattn_bo': (0.0, 0.1),
     'L1_ffn_gate_b': (0.0, 0.8)}
    factors = {'fside_Bx16xSxS2_0': 8.0,
     'fside_SxS2_0': 8.0,
     'L1_ffn_gate_w': 8.0,
     'L1_ffn_ew1': 8.0,
     'L1_ffn_ew3': 8.0,
     'L1_ffn_ew2': 8.0,
     'L1_ffn_sw1': 7.045,
     'L1_ffn_sw3': 6.971,
     'L1_ffn_sw2': 6.981}
    for name, (base, spread) in spreads.items():
        noise = np.random.default_rng([zlib.crc32(name.encode()), seed]).standard_normal(out[name].shape)
        drawn = base * np.exp(spread * noise) if base else spread * noise
        out[name] = jnp.asarray(drawn.astype(out[name].dtype))
    for name, factor in factors.items():
        out[name] = (out[name] * factor).astype(out[name].dtype)
    return out
```

```python
from contextlib import ExitStack

import concourse.bass as bass
from concourse import mybir
from concourse.alu_op_type import AluOpType as ALU

F32 = mybir.dt.float32
F32R = mybir.dt.float32r
BF16 = mybir.dt.bfloat16
I32 = mybir.dt.int32
U32 = mybir.dt.uint32
ACT = mybir.ActivationFunctionType
AX = mybir.AxisListType.X

P = 128
B, S, D, H = 4, 512, 256, 16
DK = D // H
N = B * S
NT = N // P
ST = S // P
KD = D // P
NBH = B * H
EPS = 1e-5
LOWEST = -3.0e38
E0, FF0 = 4, 1024
E1, FF1, TOPK = 16, 512, 2
CAP = -(-N * TOPK // E1 * 5 // 4)
NSH = 2
FSH = NSH * FF1

L0_TILES = 20
L0_SLOTS = L0_TILES * P
L1_SLOTS = E1 * CAP
ZERO_ROW = L1_SLOTS
DROP_ROW = L1_SLOTS + P
L1_ROWS = DROP_ROW + TOPK * N
CAP_TILES = [(s, min(P, CAP - s)) for s in range(0, CAP, P)]


def steps(eng, step, trips, ahead=4, behind=2):
    for i in range(ahead):
        step(i, i // 2, i % 2)
    with eng.Fori(ahead // 2, trips // 2) as u:
        step(u * 2, u, 0)
        step(u * 2 + 1, u, 1)
    for i in range(trips, trips + behind):
        step(i, i // 2, i % 2)


def need(eng, sem, value):
    if not isinstance(value, int) or value > 0:
        eng.wait_ge(sem, value)


def unfused(eng, spare, i):
    if not isinstance(i, int):
        eng.sem_inc(spare, 1)


def inside(i, trips):
    return not isinstance(i, int) or 0 <= i < trips


class Chain:

    def __init__(self, eng, sem):
        self.eng, self.sem, self.base, self.k, self.loop, self.rate = eng, sem, 0, 0, None, 0

    def __call__(self, ins):
        ins.then_inc(self.sem, 1)
        self.k += 1
        return ins

    def wait(self):
        self.eng.wait_ge(self.sem, self.value())

    def value(self):
        at = self.base + self.k
        return at if self.loop is None else self.loop * self.rate + at

    def enter(self, loop, rate):
        self.base, self.k, self.loop, self.rate = self.base + self.k, 0, loop, rate

    def leave(self, trips):
        assert self.k == self.rate, (self.k, self.rate)
        self.base, self.k, self.loop = self.base + trips * self.rate, 0, None


class Program:
    def __init__(self, nc, t, out):
        self.nc, self.t, self.out, self.ctx = nc, t, out, ExitStack()
        self.n_sem, self.used = 0, []

    def sem(self, name, ctx=None):
        self.n_sem += 1
        self.used.append(self.nc.alloc_semaphore(f"{name}_{self.n_sem}"))
        return self.used[-1]

    def recycle(self):
        self.nc.clear_and_free_semaphores(self.used)
        self.nc.all_engine_barrier()
        self.used = []

    def sb(self, name, shape, dt=F32, ctx=None):
        self.n_sem += 1
        return (ctx or self.ctx).enter_context(self.nc.sbuf_tensor(f"{name}_{self.n_sem}", shape, dt))

    def ps(self, name, shape, ctx):
        self.n_sem += 1
        return ctx.enter_context(self.nc.psum_tensor(f"{name}_{self.n_sem}", shape, F32))

    def dram(self, name, shape, dt=F32):
        return self.nc.dram_tensor(name, shape, dt, kind="Internal").ap()

    def load(self):
        nc = self.nc
        self.x = self.sb("x", [P, NT, D])
        self.ident = self.sb("ident", [P, P])
        self.zeros = self.sb("zeros", [P, 2048])
        s_x, s_c = self.sem("s_x"), self.sem("s_c")
        with nc.Block() as block:
            @block.sync
            def _(eng):
                eng.dma_start(self.x[:], self.t["x"].rearrange("b (t p) d -> p (b t) d", p=P)).then_inc(s_x, 16)
                eng.wait_ge(s_x, 16)

            @block.gpsimd
            def _(eng):
                eng.memset(self.ident[:], 0.0).then_inc(s_c, 1)
                eng.memset(self.zeros[:], 0.0)
                eng.wait_ge(s_c, 1)
                eng.affine_select(out=self.ident[:], in_=self.ident[:], compare_op=ALU.not_equal, fill=1.0,
                                  base=0, pattern=[[-1, P]], channel_multiplier=1)

    def normalise(self, block, chain_sem, s_mv, s_rs, s_z, dst, src, ctx, gain=None, shift=None):
        st = self.sb("bn", [P, NT, 6], ctx=ctx)
        mv = self.sb("mv", [P, NT, 2], ctx=ctx)
        rs = self.sb("rs", [P, NT], ctx=ctx)

        @block.vector
        def _(eng):
            chain = Chain(eng, chain_sem)
            for n in range(NT):
                chain(eng.bn_stats(st[:, n, :], src[:, n, :]))
            chain.wait()
            for n in range(NT):
                chain(eng.bn_aggr(mv[:, n, :], st[:, n, :]))
            chain.wait()
            eng.tensor_scalar(rs[:], mv[:, :, 1], EPS, None, ALU.add).then_inc(s_mv, 1)
            eng.wait_ge(s_rs, 1)
            chain(eng.reciprocal(rs[:], rs[:]))
            chain.wait()
            for b in range(B):
                for j in range(ST):
                    n = b * ST + j
                    chain(eng.tensor_scalar(dst[:, n, :], src[:, n, :], mv[:, n, 0:1], rs[:, n:n + 1],
                                            ALU.subtract, ALU.mult))
                if gain is not None:
                    rows = dst[:, b * ST:(b + 1) * ST, :]
                    chain.wait()
                    chain(eng.tensor_tensor(rows, rows, gain[:].unsqueeze(1).to_broadcast([P, ST, D]), ALU.mult))
                    chain.wait()
                    chain(eng.tensor_tensor(rows, rows, shift[:].unsqueeze(1).to_broadcast([P, ST, D]), ALU.add))
                chain.wait()
                eng.sem_inc(s_z, 1)

        return rs

    @staticmethod
    def deviations(eng, s_mv, s_rs, rs):
        eng.wait_ge(s_mv, 1)
        eng.activation(rs[:], rs[:], ACT.Sqrt).then_inc(s_rs, 1)

    def norm_and_transpose(self, src, nat, featT):
        nc = self.nc
        with ExitStack() as ctx:
            bank = self.ps("tp", [P, 4, 512], ctx)
            s_ch, s_mv, s_rs, s_z, s_tr, s_ev = (self.sem(n, ctx) for n in ("s_ch", "s_mv", "s_rs", "s_z", "s_tr", "s_ev"))
            with nc.Block() as block:
                rs = self.normalise(block, s_ch, s_mv, s_rs, s_z, nat, src, ctx)

                @block.tensor
                def _(eng):
                    for b in range(B):
                        eng.wait_ge(s_z, b + 1)
                        self.transposes(eng, nat, bank, b, s_tr, s_ev)

                @block.scalar
                def _(eng):
                    self.deviations(eng, s_mv, s_rs, rs)
                    for n in range(B * KD):
                        eng.wait_ge(s_tr, n + 1)
                        b, k = divmod(n, KD)
                        eng.copy(featT[:, k, b * S:(b + 1) * S], bank[:, n % 4, :]).then_inc(s_ev, 1)

    def transposes(self, eng, nat, bank, b, s_tr, s_ev):
        for k in range(KD):
            n = b * KD + k
            need(eng, s_ev, n - 3)
            for j in range(ST):
                ins = eng.transpose(bank[:, n % 4, j * P:(j + 1) * P], nat[:, b * ST + j, k * P:(k + 1) * P], self.ident[:])
            ins.then_inc(s_tr, 1)

    def project(self, qT, kvT, wq, wk, wv, bq, bk, bv, q_scale, QS, KS, V):
        nc = self.nc
        with ExitStack() as ctx:
            W = [self.sb(n, [P, KD, D], ctx=ctx) for n in ("wq", "wk", "wv")]
            bias = self.sb("bias", [P, 2, KD], ctx=ctx)
            bvr = self.sb("bvr", [P, D], ctx=ctx)
            whole = self.sb("whole", [P, 2, 512], ctx=ctx)
            hi = self.sb("hi", [P, 4, 512], F32R, ctx=ctx)
            lo = self.sb("lo", [P, 4, 512], F32R, ctx=ctx)
            pj = self.ps("pj", [P, 4, 512], ctx)
            pv = self.ps("pv", [P, 4, 512], ctx)
            names = ("s_w", "s_z", "s_p", "s_t", "s_hi", "s_lo", "s_pv", "s_v", "s_one")
            s_w, s_z, s_p, s_t, s_hi, s_lo, s_pv, s_v, s_one = (self.sem(n, ctx) for n in names)
            s_st = [self.sem("s_st", ctx) for _ in range(4)]
            jobs = [(x, c, m) for x in range(2) for c in range(B) for m in range(KD)]
            n_bias = 3 if bq is not None else 0
            with nc.Block() as block:
                @block.sync
                def _(eng):
                    for w, src in zip(W, (wq, wk, wv)):
                        eng.dma_start(w[:], src.rearrange("(k p) n -> p k n", p=P)).then_inc(s_w, 16)
                    if n_bias:
                        eng.dma_start(bias[:, 0, :], bq).then_inc(s_w, 16)
                        eng.dma_start(bias[:, 1, :], bk).then_inc(s_w, 16)
                        eng.dma_start(bvr[:], bv.partition_broadcast(P)).then_inc(s_w, 16)
                    for n, (x, c, m) in enumerate(jobs):
                        rows = slice(c * H + m * (P // DK), c * H + (m + 1) * (P // DK))
                        for part, (s, buf) in enumerate(((s_hi, hi), (s_lo, lo))):
                            eng.wait_ge(s, n + 1)
                            eng.dma_start((QS, KS)[x][part, rows].rearrange("h d s -> (h d) s"), buf[:, n % 4, :].bitcast(F32)).then_inc(s_st[n % 4], 16)
                    for s in s_st:
                        eng.wait_ge(s, 32 * len(jobs) // 4)

                @block.tensor
                def _(eng):
                    eng.wait_ge(s_w, 16 * (3 + n_bias))
                    for n, (x, c, m) in enumerate(jobs):
                        need(eng, s_t, n - 3)
                        src = (qT, kvT)[x]
                        for k in range(KD):
                            ins = eng.matmul(pj[:, n % 4, :], W[x][:, k, m * P:(m + 1) * P], src[:, k, c * S:(c + 1) * S],
                                             start=(k == 0), stop=(k == KD - 1))
                        ins.then_inc(s_p, 1)
                        need(eng, s_v, n - 3)
                        for k in range(KD):
                            ins = eng.matmul(pv[:, n % 4, 0:D], kvT[:, k, n * P:(n + 1) * P], W[2][:, k, :],
                                             start=(k == 0), stop=(k == KD - 1))
                        ins.then_inc(s_pv, 1)

                @block.vector
                def _(eng):
                    eng.memset(V[:, :, :, DK:DK + 1], 1.0).then_inc(s_one, 1)
                    if not n_bias:
                        eng.memset(bias[:], 0.0).then_inc(s_one, 1)
                        eng.memset(bvr[:], 0.0).then_inc(s_one, 1)
                        eng.wait_ge(s_one, 3)
                    eng.wait_ge(s_w, 16 * (3 + n_bias))

                    def rest(n):
                        eng.wait_ge(s_hi, n + 1)
                        need(eng, s_st[n % 4], 32 * (n // 4))
                        eng.tensor_tensor(lo[:, n % 4, :], whole[:, n % 2, :], hi[:, n % 4, :].bitcast(F32), ALU.subtract)\
                           .then_inc(s_lo, 1)

                    for n, (x, c, m) in enumerate(jobs):
                        eng.wait_ge(s_p, n + 1)
                        need(eng, s_lo, n - 1)
                        eng.tensor_scalar(whole[:, n % 2, :], pj[:, n % 4, :], bias[:, x, m:m + 1], q_scale if x == 0 else 1.0,
                                          ALU.add, ALU.mult).then_inc(s_t, 1)
                        eng.wait_ge(s_pv, n + 1)
                        b, j = divmod(n, ST)
                        eng.tensor_tensor(V[:, b * H:(b + 1) * H, j, 0:DK], pv[:, n % 4, 0:D].rearrange("p (h d) -> p h d", d=DK),
                                          bvr[:].rearrange("p (h d) -> p h d", d=DK), ALU.add).then_inc(s_v, 1)
                        rest(n)

                @block.scalar
                def _(eng):
                    for n in range(len(jobs)):
                        eng.wait_ge(s_t, n + 1)
                        need(eng, s_st[n % 4], 32 * (n // 4))
                        eng.copy(hi[:, n % 4, :], whole[:, n % 2, :]).then_inc(s_hi, 1)

    def attention(self, kind, QS, KS, V, O, exp_scale, mask=None, common=None, side=None, k_aux=0.0):
        nc = self.nc
        with ExitStack() as ctx:
            q = self.sb("q", [P, 2, S], F32R, ctx=ctx)
            k = self.sb("k", [P, 2, S], F32R, ctx=ctx)
            v = self.sb("v", [P, 2, ST, DK + 1], ctx=ctx)
            X = self.sb("X", [P, 2, ST, S], ctx=ctx)
            PT = self.sb("PT", [P, 2, ST, S], ctx=ctx)
            OT = self.sb("OT", [DK + 1, S], ctx=ctx)
            mx = self.sb("mx", [P, 2, ST], ctx=ctx)
            nm = self.sb("nm", [P, 2, ST], ctx=ctx)
            rec = self.sb("rec", [P, ST, 1], ctx=ctx)
            M = None if kind == "self" else self.sb("M", [P, 2, ST, S], BF16 if kind == "mask" else F32, ctx=ctx)
            pS = self.ps("pS", [P, 3, 512], ctx)
            pT = self.ps("pT", [P, 4, 512], ctx)
            pO = self.ps("pO", [P, 512], ctx)
            names = ("s_c", "s_s", "s_x", "s_nm", "s_p", "s_t", "s_ea", "s_ed", "s_v", "s_o", "s_oc", "s_b", "s_r", "s_n",
                     "s_m", "s_z", "s_spv", "s_spt", "s_spg")
            (s_c, s_s, s_x, s_nm, s_p, s_t, s_ea, s_ed, s_v, s_o, s_oc, s_b, s_r, s_n, s_m, s_z, s_spv, s_spt, s_spg) = (self.sem(n, ctx) for n in names)
            s_ld = [self.sem("s_ld", ctx) for _ in range(2)]
            s_f = [self.sem("s_f", ctx) for _ in range(2)]
            PER = 6 * 16
            s_free = s_p if kind == "self" else s_x

            with nc.Block() as block:
                @block.sync
                def _(eng):
                    eng.wait_ge(s_c, 4)

                    def step(i, u, par):
                        if not inside(i, NBH):
                            return
                        need(eng, s_s, (i - 1) * 4)
                        for r in range(4):
                            eng.dma_start(q[r * DK:(r + 1) * DK, par, :].bitcast(F32), QS[r // 2, bass.ds(i, 1)].rearrange("o d s -> (o d) s"))\
                               .then_inc(s_ld[par], 16)
                        for r in range(2):
                            eng.dma_start(k[r * 2 * DK:(r + 1) * 2 * DK, par, :].bitcast(F32), KS[:, bass.ds(i, 1)].rearrange("r o d s -> r (o d) s"))\
                               .then_inc(s_ld[par], 16)
                        if kind != "self":
                            need(eng, s_x, (i - 1) * 4)
                            src = side[bass.ds(i, 1)] if kind == "side" else mask[bass.ds(i // H, 1)]
                            eng.dma_start(M[:, par], src.rearrange("o p t k -> (o p) t k")).then_inc(s_f[par], 16)
                    steps(eng, step, NBH, behind=0)

                @block.gpsimd
                def _(eng):
                    def one(i, u, par, b):
                        if kind == "side":
                            eng.wait_ge(s_f[par], (u + 1) * 16)
                            unfused(eng, s_spg, i)
                            eng.tensor_tensor(M[:, par], M[:, par], common[:, bass.ds(b, 1)].rearrange("p o t k -> p (o t) k"),
                                              ALU.add).then_inc(s_m, 1)
                        need(eng, s_o, i - 1)
                        unfused(eng, s_spg, i)
                        eng.tensor_copy(v[:, par], V[:, bass.ds(i, 1)].rearrange("p o t d -> p (o t) d")).then_inc(s_v, 1)

                    eng.wait_ge(s_c, 4)
                    for i in range(4):
                        one(i, i // 2, i % 2, 0)
                    with eng.Fori(2, H // 2) as u:
                        for par in range(2):
                            one(u * 2 + par, u, par, 0)
                    with eng.Fori(1, B) as b:
                        with eng.Fori(0, H // 2) as w:
                            for par in range(2):
                                one(b * H + w * 2 + par, b * (H // 2) + w, par, b)

                @block.tensor
                def _(eng):
                    eng.wait_ge(s_c, 4)

                    def scores(i, u, par, qts):
                        for qt in qts:
                            if qt == 0:
                                eng.wait_ge(s_ld[par], (u + 1) * PER)
                            if qt == 3:
                                eng.wait_ge(s_free, i * 4 + 1)
                            elif qt == 0:
                                need(eng, s_free, i * 4)
                            else:
                                need(eng, s_free, (i - 1) * 4 + qt + 1)
                            eng.matmul(pS[:, qt % 3, :], q[:, par, qt * P:(qt + 1) * P], k[:, par, :], start=True, stop=True)\
                               .then_inc(s_s, 1)

                    def step(i, u, par):
                        if inside(i, NBH):
                            scores(i, u, par, (0, 1, 2))
                        a = i - 2
                        if inside(a, NBH):
                            eng.wait_ge(s_v, a + 1)
                            eng.wait_ge(s_ea, (a + 1) * 2)
                            eng.wait_ge(s_ed, (a + 1) * 2)
                            need(eng, s_n, a)
                            for kt in range(ST):
                                ins = eng.matmul(pO[0:DK + 1, :], v[:, par, kt, :], PT[:, par, kt, :],
                                                 start=(kt == 0), stop=(kt == ST - 1))
                            ins.then_inc(s_o, 1)
                        if inside(i, NBH):
                            scores(i, u, par, (3,))
                        t = i - 1
                        if inside(t, NBH):
                            eng.wait_ge(s_p, (t + 1) * 4)
                            for kt in range(ST):
                                if kt == 0:
                                    need(eng, s_ea, t * 2)
                                if kt == 1:
                                    need(eng, s_ed, t * 2)
                                for qt in range(ST):
                                    ins = eng.transpose(pT[:, kt, qt * P:(qt + 1) * P], X[:, 1 - par, qt, kt * P:(kt + 1) * P],
                                                        self.ident[:])
                                ins.then_inc(s_t, 1)
                        if inside(a, NBH):
                            eng.wait_ge(s_oc, a + 1)
                            unfused(eng, s_spt, i)
                            for qt in range(ST):
                                ins = eng.transpose(pO[:, qt * (DK + 1):(qt + 1) * (DK + 1)], OT[:, qt * P:(qt + 1) * P],
                                                    self.ident[0:DK + 1, 0:DK + 1])
                            ins.then_inc(s_b, 1)
                    steps(eng, step, NBH)

                @block.vector
                def _(eng):
                    eng.memset(q[64:128, :, :].bitcast(F32), 0.0).then_inc(s_z, 1)
                    eng.memset(k[64:128, :, :].bitcast(F32), 0.0).then_inc(s_z, 1)
                    eng.wait_ge(s_z, 2)
                    eng.memset(q[64:65, :, :].bitcast(F32), 1.0).then_inc(s_c, 2)
                    eng.memset(k[64:65, :, :].bitcast(F32), k_aux).then_inc(s_c, 2)

                    def step(i, u, par):
                        if inside(i, NBH):
                            for qt in range(ST):
                                eng.wait_ge(s_s, i * 4 + qt + 1)
                                if kind == "self":
                                    if qt == 0:
                                        need(eng, s_p, (i - 1) * 4)
                                    eng.tensor_reduce(nm[:, par, qt:qt + 1], pS[:, qt % 3, :], AX, ALU.max, negate=True)\
                                       .then_inc(s_x, 1)
                                    continue
                                if qt == 0:
                                    if kind == "side":
                                        eng.wait_ge(s_m, i + 1)
                                    else:
                                        eng.wait_ge(s_f[par], (u + 1) * 16)
                                    need(eng, s_t, (i - 1) * 4)
                                unfused(eng, s_spv, i)
                                eng.tensor_tensor_reduce(X[:, par, qt, :], pS[:, qt % 3, :], M[:, par, qt, :], 1.0, LOWEST,
                                                         ALU.mult if kind == "mask" else ALU.add, ALU.max,
                                                         mx[:, par, qt:qt + 1]).then_inc(s_x, 1)
                            if kind != "self":
                                eng.wait_ge(s_x, (i + 1) * 4)
                                eng.tensor_scalar(nm[:, par, :], mx[:, par, :], -exp_scale, None, ALU.mult).then_inc(s_nm, 1)
                        t = i - 1
                        if inside(t, NBH):
                            for kt in (1, 3):
                                eng.wait_ge(s_t, t * 4 + kt + 1)
                                if kt == 1:
                                    need(eng, s_o, t - 1)
                                eng.tensor_copy(PT[:, 1 - par, kt, :], pT[:, kt, :]).then_inc(s_ed, 1)
                        a = i - 2
                        if inside(a, NBH):
                            eng.wait_ge(s_b, a + 1)
                            o = pO[:, 0:ST * (DK + 1)].rearrange("p (t d) -> p t d", d=DK + 1)
                            need(eng, s_n, a)
                            eng.reciprocal(rec[:], o[:, :, DK:DK + 1]).then_inc(s_r, 1)
                            eng.wait_ge(s_r, a + 1)
                            eng.tensor_tensor(O[:, bass.ds(a, 1)].rearrange("p o t d -> p (o t) d"), o[:, :, 0:DK],
                                              rec[:].to_broadcast([P, ST, DK]), ALU.mult).then_inc(s_n, 1)
                    steps(eng, step, NBH)

                @block.scalar
                def _(eng):
                    def exps(i, par, qts):
                        for qt in qts:
                            if kind == "self":
                                if qt == 0:
                                    need(eng, s_t, (i - 1) * 4)
                                eng.wait_ge(s_x, i * 4 + qt + 1)
                            elif qt == 0:
                                eng.wait_ge(s_nm, i + 1)
                            eng.activation(X[:, par, qt, :], pS[:, qt % 3, :] if kind == "self" else X[:, par, qt, :], ACT.Exp,
                                           bias=nm[:, par, qt:qt + 1], scale=exp_scale).then_inc(s_p, 1)

                    def turned(a):
                        eng.wait_ge(s_o, a + 1)
                        need(eng, s_b, a)
                        eng.copy(OT[:], pO[0:DK + 1, :]).then_inc(s_oc, 1)

                    def step(i, u, par):
                        a, t = i - 2, i - 1
                        if kind == "self" and inside(i, NBH):
                            exps(i, par, (0, 1, 2))
                        if inside(a, NBH):
                            turned(a)
                        if kind == "self" and inside(i, NBH):
                            exps(i, par, (3,))
                        if inside(t, NBH):
                            for kt in (0, 2):
                                eng.wait_ge(s_t, t * 4 + kt + 1)
                                if kt == 0:
                                    need(eng, s_o, t - 1)
                                eng.copy(PT[:, 1 - par, kt, :], pT[:, kt, :]).then_inc(s_ea, 1)
                        if kind != "self" and inside(i, NBH):
                            exps(i, par, range(ST))
                    steps(eng, step, NBH)

    def output(self, O, wo, bo, base, dst):
        nc = self.nc
        with ExitStack() as ctx:
            w = self.sb("wo", [P, KD, D], ctx=ctx)
            brow = self.sb("bo", [P, D], ctx=ctx)
            OT = self.sb("oT", [P, 2, KD, S], ctx=ctx)
            nat = self.sb("nat", [P, 2, ST, D], ctx=ctx)
            bank = self.ps("tp", [P, 4, 512], ctx)
            py = self.ps("py", [P, 4, 512], ctx)
            s_w, s_g, s_tr, s_ev, s_y, s_a, s_b = (self.sem(n, ctx) for n in ("s_w", "s_g", "s_tr", "s_ev", "s_y", "s_a", "s_b"))
            with nc.Block() as block:
                @block.sync
                def _(eng):
                    eng.dma_start(w[:], wo.rearrange("(k p) n -> p k n", p=P)).then_inc(s_w, 16)
                    if bo is not None:
                        eng.dma_start(brow[:], bo.partition_broadcast(P)).then_inc(s_w, 16)

                @block.gpsimd
                def _(eng):
                    for b in range(B):
                        need(eng, s_tr, (b - 1) * KD)
                        eng.tensor_copy(nat[:, b % 2].rearrange("p t (h d) -> p t h d", d=DK),
                                        O[:, b * H:(b + 1) * H].rearrange("p h t d -> p t h d")).then_inc(s_g, 1)

                @block.tensor
                def _(eng):
                    eng.wait_ge(s_w, 16 if bo is None else 32)

                    def turn(b):
                        eng.wait_ge(s_g, b + 1)
                        for k in range(KD):
                            n = b * KD + k
                            need(eng, s_ev, n - 3)
                            for j in range(ST):
                                ins = eng.transpose(bank[:, n % 4, j * P:(j + 1) * P], nat[:, b % 2, j, k * P:(k + 1) * P],
                                                    self.ident[:])
                            ins.then_inc(s_tr, 1)

                    turn(0)
                    for b in range(B):
                        if b + 1 < B:
                            turn(b + 1)
                        eng.wait_ge(s_ev, (b + 1) * KD)
                        for j in range(ST):
                            n = b * ST + j
                            need(eng, s_a, n - 3)
                            for k in range(KD):
                                ins = eng.matmul(py[:, n % 4, 0:D], OT[:, b % 2, k, j * P:(j + 1) * P], w[:, k, :],
                                                 start=(k == 0), stop=(k == KD - 1))
                            ins.then_inc(s_y, 1)

                @block.scalar
                def _(eng):
                    for n in range(B * KD):
                        b, k = divmod(n, KD)
                        eng.wait_ge(s_tr, n + 1)
                        need(eng, s_y, (b - 1) * ST)
                        eng.copy(OT[:, b % 2, k, :], bank[:, n % 4, :]).then_inc(s_ev, 1)

                @block.vector
                def _(eng):
                    if bo is not None:
                        eng.wait_ge(s_w, 32)
                        for b in range(B):
                            rows = slice(b * ST, (b + 1) * ST)
                            eng.tensor_tensor(dst[:, rows, :], base[:, rows, :], brow[:].unsqueeze(1).to_broadcast([P, ST, D]),
                                              ALU.add).then_inc(s_b, 1)
                        eng.wait_ge(s_b, B)
                    src = base if bo is None else dst
                    for n in range(NT):
                        eng.wait_ge(s_y, n + 1)
                        eng.tensor_tensor(dst[:, n, :], src[:, n, :], py[:, n % 4, 0:D], ALU.add).then_inc(s_a, 1)

    def load_context(self, cT):
        nc = self.nc
        s_c = self.sem("s_ctx")
        with nc.Block() as block:
            @block.sync
            def _(eng):
                for k in range(KD):
                    eng.dma_start(cT[:, k, :], self.t["ctx_1024"][k * P:(k + 1) * P, :]).then_inc(s_c, 16)
                eng.wait_ge(s_c, 16 * KD)

    def prepare_mask(self, mask):
        nc = self.nc
        with ExitStack() as ctx:
            raw = self.sb("raw", [P, 2, ST, S], I32, ctx=ctx)
            s_d = [self.sem("s_d", ctx) for _ in range(2)]
            bits = self.sb("bits", [P, 2, ST, S], BF16, ctx=ctx)
            s_m = self.sem("s_m", ctx)
            s_st = [self.sem("s_st", ctx) for _ in range(2)]
            with nc.Block() as block:
                def put(eng, b):
                    eng.wait_ge(s_m, b + 1)
                    eng.dma_start(mask[b], bits[:, b % 2]).then_inc(s_st[b % 2], 16)

                @block.sync
                def _(eng):
                    for b in range(B):
                        need(eng, s_m, b - 1)
                        eng.dma_start(raw[:, b % 2], self.t["mask_Bx1xSxS2_ik1"][b, 0].rearrange("(t p) k -> p t k", p=P))\
                           .then_inc(s_d[b % 2], 16)
                        if b:
                            put(eng, b - 1)
                    put(eng, B - 1)
                    for s in s_st:
                        eng.wait_ge(s, 16 * B // 2)

                @block.vector
                def _(eng):
                    for b in range(B):
                        eng.wait_ge(s_d[b % 2], 16 * (b // 2 + 1))
                        need(eng, s_st[b % 2], 16 * (b // 2))
                        eng.tensor_scalar(bits[:, b % 2], raw[:, b % 2], 0, None, ALU.not_equal).then_inc(s_m, 1)

    def store(self, x):
        nc = self.nc
        s_o = self.sem("s_out")
        with nc.Block() as block:
            @block.sync
            def _(eng):
                eng.dma_start(self.out.rearrange("b (t p) d -> p (b t) d", p=P), x[:]).then_inc(s_o, 16)
                eng.wait_ge(s_o, 16)

    def prepare_common(self, common):
        nc = self.nc
        with ExitStack() as ctx:
            am = self.sb("am", [P, ST, S], ctx=ctx)
            pad = self.sb("pad", [P, B, S], mybir.dt.uint8, ctx=ctx)
            low = self.sb("low", [P, B, S], ctx=ctx)
            s_d, s_l = self.sem("s_d", ctx), self.sem("s_l", ctx)
            with nc.Block() as block:
                @block.sync
                def _(eng):
                    eng.dma_start(am[:], self.t["fside_SxS2_0"].rearrange("(t p) k -> p t k", p=P)).then_inc(s_d, 16)
                    eng.dma_start(pad[:], self.t["mask_BxS2_bf0"].partition_broadcast(P)).then_inc(s_d, 16)

                @block.vector
                def _(eng):
                    eng.wait_ge(s_d, 32)
                    eng.tensor_scalar(low[:], pad[:], -3.0e38, 10.0, ALU.mult, ALU.mult).then_inc(s_l, 1)
                    eng.wait_ge(s_l, 1)
                    for b in range(B):
                        eng.scalar_tensor_tensor(out=common[:, b], in0=am[:], scalar=0.5,
                                                 in1=low[:, b].unsqueeze(1).to_broadcast([P, ST, S]), op0=ALU.mult, op1=ALU.add)

    def route_top1(self, src, xx, gain, shift, slot, tile_expert, XS):
        nc, t = self.nc, self.t
        with ExitStack() as ctx:
            grow, brow, rw = (self.sb(n, [P, D], ctx=ctx) for n in ("grow", "brow", "rw"))
            rb = self.sb("rb", [P, 1], ctx=ctx)
            junk = self.sb("junk", [P, D], ctx=ctx)
            key, kf, gt = (self.sb(n, [P, NT], ctx=ctx) for n in ("key", "kf", "gt"))
            ki = self.sb("ki", [P, NT], I32, ctx=ctx)
            oh = self.sb("oh", [P, E0, NT], ctx=ctx)
            ohb = self.sb("ohb", [P, E0, NT], BF16, ctx=ctx)
            tri = self.sb("tri", [P, P], BF16, ctx=ctx)
            ones = self.sb("ones", [P, P], BF16, ctx=ctx)
            tot, incl, w = (self.sb(n, [P, E0, NT], ctx=ctx) for n in ("tot", "incl", "w"))
            cnt, ends, base = (self.sb(n, [P, E0], ctx=ctx) for n in ("cnt", "ends", "base"))
            ci = self.sb("ci", [P, E0], I32, ctx=ctx)
            slotf = self.sb("slotf", [P, NT], ctx=ctx)
            starts = self.sb("starts", [P, L0_TILES], ctx=ctx)
            te = self.sb("te", [P, 3, L0_TILES], ctx=ctx)
            ps = self.ps("rt", [P, 2, 512], ctx)
            names = ("s_w", "s_ch", "s_mv", "s_rs", "s_z", "s_c", "s_oh", "s_p", "s_ix", "s_zero", "s_sc")
            s_w, s_ch, s_mv, s_rs, s_z, s_c, s_oh, s_p, s_ix, s_zero, s_sc = (self.sem(n, ctx) for n in names)
            s_ch2 = self.sem("s_ch2", ctx)
            with nc.Block() as block:
                @block.sync
                def _(eng):
                    for dst, srcd in ((grow, gain), (brow, shift), (rb, t["L0_ffn_router_b"])):
                        eng.dma_start(dst[:], srcd.partition_broadcast(P)).then_inc(s_w, 16)
                    eng.dma_start(rw[:], t["L0_ffn_router_w"].rearrange("d o -> (d o)").partition_broadcast(P)).then_inc(s_w, 16)
                    eng.dma_start(XS.rearrange("(p r) d -> p (r d)", p=P)[:, :], self.zero_rows(L0_SLOTS // P)).then_inc(s_zero, 16)

                @block.vector
                def _(eng):
                    eng.wait_ge(s_w, 64)
                rs = self.normalise(block, s_ch, s_mv, s_rs, s_z, xx, src, ctx, gain=grow, shift=brow)

                @block.scalar
                def _(eng):
                    self.deviations(eng, s_mv, s_rs, rs)

                @block.vector
                def _(eng):
                    do = Chain(eng, s_ch2)

                    def then(ins):
                        do(ins)
                        do.wait()

                    eng.wait_ge(s_z, B)
                    for n in range(NT):
                        then(eng.tensor_tensor_reduce(junk[:], xx[:, n, :], rw[:], 1.0, 0.0, ALU.mult, ALU.add, key[:, n:n + 1]))
                    then(eng.tensor_scalar(key[:], key[:], rb[:, 0:1], None, ALU.add))
                    then(eng.tensor_copy(ki[:], key[:]))
                    then(eng.tensor_copy(kf[:], ki[:]))
                    then(eng.tensor_tensor(gt[:], kf[:], key[:], ALU.is_gt))
                    then(eng.tensor_tensor(kf[:], kf[:], gt[:], ALU.subtract))
                    then(eng.tensor_copy(ki[:], kf[:]))
                    then(eng.tensor_scalar(ki[:], ki[:], E0 - 1, None, ALU.bitwise_and))
                    then(eng.tensor_copy(kf[:], ki[:]))
                    for e in range(E0):
                        do(eng.tensor_scalar(oh[:, e, :], kf[:], float(e), None, ALU.is_equal))
                    do.wait()
                    do(eng.tensor_copy(ohb[:], oh[:]))
                    do.wait()
                    eng.sem_inc(s_oh, 1)
                    eng.wait_ge(s_p, 1)
                    then(eng.tensor_copy(tot[:].rearrange("p e n -> p (e n)"), ps[:, 1, 0:E0 * NT]))
                    then(eng.tensor_reduce(cnt[:], tot[:], AX, ALU.add))
                    then(eng.tensor_scalar(cnt[:], cnt[:], float(P - 1), None, ALU.add))
                    then(eng.tensor_copy(ci[:], cnt[:]))
                    then(eng.tensor_scalar(ci[:], ci[:], 7, 7, ALU.logical_shift_right, ALU.logical_shift_left))
                    then(eng.tensor_copy(cnt[:], ci[:]))
                    then(eng.tensor_tensor_scan(ends[:], cnt[:], self.zeros[:, 0:E0], 0.0, ALU.add, ALU.add))
                    then(eng.tensor_tensor(base[:], ends[:], cnt[:], ALU.subtract))
                    for e in range(E0):
                        do(eng.tensor_tensor_scan(incl[:, e, :], tot[:, e, :], self.zeros[:, 0:NT], base[:, e:e + 1], ALU.add, ALU.add))
                    do.wait()
                    then(eng.tensor_tensor(incl[:], incl[:], tot[:], ALU.subtract))
                    then(eng.tensor_tensor(w[:].rearrange("p e n -> p (e n)"), incl[:].rearrange("p e n -> p (e n)"),
                                           ps[:, 0, 0:E0 * NT], ALU.add))
                    then(eng.tensor_tensor(w[:], w[:], oh[:], ALU.mult))
                    then(eng.tensor_reduce(slotf[:], w[:].rearrange("p e n -> p n e"), AX, ALU.add))
                    do(eng.tensor_copy(slot[:], slotf[:]))
                    eng.wait_ge(s_c, 5)
                    for e in range(E0 - 1):
                        do(eng.tensor_scalar(te[:, e, :], starts[:], ends[:, e:e + 1], None, ALU.is_ge))
                    do.wait()
                    then(eng.tensor_tensor(te[:, 0, :], te[:, 0, :], te[:, 1, :], ALU.add))
                    then(eng.tensor_tensor(te[:, 0, :], te[:, 0, :], te[:, 2, :], ALU.add))
                    do(eng.tensor_copy(tile_expert[:], te[:, 0, :]))
                    do.wait()
                    eng.sem_inc(s_ix, 1)

                @block.tensor
                def _(eng):
                    eng.wait_ge(s_c, 5)
                    eng.wait_ge(s_oh, 1)
                    rhs = ohb[:].rearrange("p e n -> p (e n)")
                    eng.matmul(ps[:, 0, 0:E0 * NT], tri[:], rhs, start=True, stop=True)
                    eng.matmul(ps[:, 1, 0:E0 * NT], ones[:], rhs, start=True, stop=True).then_inc(s_p, 1)

                @block.gpsimd
                def _(eng):
                    eng.memset(tri[:], 0.0).then_inc(s_c, 1)
                    eng.memset(ones[:], 1.0).then_inc(s_c, 1)
                    eng.wait_ge(s_c, 2)
                    eng.affine_select(out=tri[:], in_=tri[:], compare_op=ALU.is_ge, fill=1.0, base=0,
                                      pattern=[[-1, P]], channel_multiplier=1).then_inc(s_c, 1)
                    eng.iota(starts[:], pattern=[[P, L0_TILES]], base=0, channel_multiplier=0,
                             allow_small_or_imprecise_dtypes=True).then_inc(s_c, 2)
                    eng.wait_ge(s_ix, 1)
                    eng.wait_ge(s_zero, 16)
                    for n in range(NT):
                        eng.indirect_dma_start(out=XS, out_offset=bass.IndirectOffsetOnAxis(ap=slot[:, n:n + 1], axis=0),
                                               in_=xx[:, n, :], in_offset=None).then_inc(s_sc, 16)
                    eng.wait_ge(s_sc, 16 * NT)

    def zero_rows(self, rows):
        return self.zeros[:, 0:D].unsqueeze(1).to_broadcast([P, rows, D])

    def top1_tiles(self, tile_expert, XS, YS):
        nc, t = self.nc, self.t
        MF = FF0 // P
        with ExitStack() as ctx:
            w1 = self.sb("w1", [P, 2, KD, FF0], ctx=ctx)
            w2 = self.sb("w2", [P, 2, MF, D], ctx=ctx)
            b1 = self.sb("b1", [P, 2, MF], ctx=ctx)
            b2 = self.sb("b2", [P, 2, D], ctx=ctx)
            xs = self.sb("xs", [P, 2, D], ctx=ctx)
            xT = self.sb("xT", [P, 2, KD, P], ctx=ctx)
            hT = self.sb("hT", [P, 2, MF, P], ctx=ctx)
            ys = self.sb("ys", [P, 2, D], ctx=ctx)
            px = self.ps("px", [P, 2, 512], ctx)
            ph = self.ps("ph", [P, 4, 512], ctx)
            py = self.ps("py", [P, 2, 512], ctx)
            s_x, s_xt, s_h, s_hv, s_ha, s_y, s_yb = (self.sem(n, ctx) for n in ("s_x", "s_xt", "s_h", "s_hv", "s_ha", "s_y", "s_yb"))
            s_w = [self.sem("s_w", ctx) for _ in range(2)]
            s_st = [self.sem("s_st", ctx) for _ in range(2)]
            LOADS = 5 * 16
            with nc.Block() as block:
                @block.sync
                def _(eng):
                    def step(i, u, par):
                        if inside(i, L0_TILES):
                            need(eng, s_y, i - 1)
                            need(eng, s_yb, i - 1)
                            e = eng.value_load(tile_expert[0:1, bass.ds(i, 1)], min_val=0, max_val=E0 - 1)
                            one = bass.ds(e, 1)
                            eng.dma_start(xs[:, par, :], XS[bass.ds(i * P, P), :]).then_inc(s_w[par], 16)
                            eng.dma_start(w1[:, par], t["L0_ffn_W1"][one].rearrange("o (k p) f -> p (o k) f", p=P)).then_inc(s_w[par], 16)
                            eng.dma_start(b1[:, par], t["L0_ffn_b1"][one].rearrange("o p m -> (o p) m")).then_inc(s_w[par], 16)
                            eng.dma_start(b2[:, par], t["L0_ffn_b2"][one].rearrange("o d -> (o d)").partition_broadcast(P)).then_inc(s_w[par], 16)
                            eng.dma_start(w2[:, par], t["L0_ffn_W2"][one].rearrange("o (m p) d -> p (o m) d", p=P)).then_inc(s_w[par], 16)
                    steps(eng, step, L0_TILES, ahead=2, behind=0)

                @block.scalar
                def _(eng):
                    def step(i, u, par):
                        if inside(i, L0_TILES):
                            eng.wait_ge(s_x, i + 1)
                            need(eng, s_h, (i - 1) * 2)
                            eng.copy(xT[:, par].rearrange("p k n -> p (k n)"), px[:, par, 0:KD * P]).then_inc(s_xt, 1)
                            eng.wait_ge(s_h, i * 2 + 1)
                            need(eng, s_y, i - 1)
                            for m in range(MF // 2):
                                ins = eng.activation(hT[:, par, m, :], ph[:, par * 2, m * P:(m + 1) * P], ACT.Relu, bias=b1[:, par, m:m + 1])
                            ins.then_inc(s_ha, 1)
                            eng.wait_ge(s_yb, i + 1)
                            eng.dma_start(YS[bass.ds(i * P, P), :], ys[:, par, :]).then_inc(s_st[par], 16)
                    steps(eng, step, L0_TILES, ahead=2, behind=0)
                    for s in s_st:
                        eng.wait_ge(s, 16 * L0_TILES // 2)

                @block.vector
                def _(eng):
                    def step(i, u, par):
                        if inside(i, L0_TILES):
                            eng.wait_ge(s_h, i * 2 + 2)
                            need(eng, s_y, i - 1)
                            for m in range(MF // 2, MF):
                                at = m - MF // 2
                                ins = eng.tensor_scalar(hT[:, par, m, :], ph[:, par * 2 + 1, at * P:(at + 1) * P], b1[:, par, m:m + 1], 0.0,
                                                        ALU.add, ALU.max)
                            ins.then_inc(s_hv, 1)
                            eng.wait_ge(s_y, i + 1)
                            if not isinstance(i, int) or i >= 2:
                                eng.wait_ge(s_st[par], u * 16)
                            eng.tensor_tensor(ys[:, par, :], py[:, par, 0:D], b2[:, par, :], ALU.add).then_inc(s_yb, 1)
                    steps(eng, step, L0_TILES, ahead=2, behind=0)

                @block.tensor
                def _(eng):
                    def turn(i, u, par):
                        eng.wait_ge(s_w[par], (u + 1) * LOADS)
                        need(eng, s_xt, i - 1)
                        for k in range(KD):
                            ins = eng.transpose(px[:, par, k * P:(k + 1) * P], xs[:, par, k * P:(k + 1) * P], self.ident[:])
                        ins.then_inc(s_x, 1)

                    def step(i, u, par):
                        turn(i, u, par)
                        eng.wait_ge(s_xt, i + 1)
                        for half in range(2):
                            need(eng, (s_ha, s_hv)[half], i - 1)
                            for m in range(MF // 2):
                                f = (half * (MF // 2) + m) * P
                                for k in range(KD):
                                    ins = eng.matmul(ph[:, par * 2 + half, m * P:(m + 1) * P], w1[:, par, k, f:f + P], xT[:, par, k, :],
                                                     start=(k == 0), stop=(k == KD - 1))
                            ins.then_inc(s_h, 1)
                        need(eng, s_yb, i - 1)
                        for m in range(MF):
                            if m % (MF // 2) == 0:
                                eng.wait_ge((s_ha, s_hv)[m // (MF // 2)], i + 1)
                            ins = eng.matmul(py[:, par, 0:D], hT[:, par, m, :], w2[:, par, m, :], start=(m == 0), stop=(m == MF - 1))
                        ins.then_inc(s_y, 1)
                    steps(eng, step, L0_TILES, ahead=2, behind=0)

    def combine_top1(self, xx, slot, YS, gain, shift, x):
        nc = self.nc
        with ExitStack() as ctx:
            grow, brow = (self.sb(n, [P, D], ctx=ctx) for n in ("grow", "brow"))
            y = self.sb("y", [P, NT, D], ctx=ctx)
            s_w, s_g, s_ch, s_mv, s_rs, s_z, s_ch2 = (self.sem(n, ctx) for n in ("s_w", "s_g", "s_ch", "s_mv", "s_rs", "s_z", "s_ch2"))
            with nc.Block() as block:
                @block.sync
                def _(eng):
                    eng.dma_start(grow[:], gain.partition_broadcast(P)).then_inc(s_w, 16)
                    eng.dma_start(brow[:], shift.partition_broadcast(P)).then_inc(s_w, 16)

                @block.gpsimd
                def _(eng):
                    for n in range(NT):
                        eng.indirect_dma_start(out=y[:, n, :], out_offset=None, in_=YS,
                                               in_offset=bass.IndirectOffsetOnAxis(ap=slot[:, n:n + 1], axis=0)).then_inc(s_g, 16)

                @block.vector
                def _(eng):
                    do = Chain(eng, s_ch2)
                    eng.wait_ge(s_w, 32)
                    eng.wait_ge(s_g, 16 * NT)
                    do(eng.tensor_tensor(y[:], y[:], xx[:], ALU.add))
                    do.wait()
                rs = self.normalise(block, s_ch, s_mv, s_rs, s_z, y, y, ctx, gain=grow, shift=brow)

                @block.scalar
                def _(eng):
                    self.deviations(eng, s_mv, s_rs, rs)

                @block.vector
                def _(eng):
                    eng.wait_ge(s_z, B)
                    eng.tensor_tensor(x[:], x[:], y[:], ALU.add)

    def gate(self, zT, w_k, oh, lgT, asT):
        nc, t = self.nc, self.t
        G = [P, NT, E1]
        with ExitStack() as ctx:
            gw = self.sb("gw", [P, KD, E1], ctx=ctx)
            gb = self.sb("gb", [P, E1], ctx=ctx)
            rev = self.sb("rev", [P, E1], ctx=ctx)
            lg, sc, tmp = (self.sb(n, G, ctx=ctx) for n in ("lg", "sc", "tmp"))
            m = self.sb("m", [P, NT], ctx=ctx)
            pl = self.ps("pl", [P, 512], ctx)
            pt = self.ps("pt", [P, 4, 512], ctx)
            s_w, s_c, s_l, s_ch, s_d, s_e, s_as, s_t, s_tc = (self.sem(n, ctx) for n in
                                                             ("s_w", "s_c", "s_l", "s_ch", "s_d", "s_e", "s_as", "s_t", "s_tc"))

            def per_token(a):
                return a[:].unsqueeze(2).to_broadcast(G)

            def per_expert(a):
                return a[:].unsqueeze(1).to_broadcast(G)

            with nc.Block() as block:
                @block.sync
                def _(eng):
                    eng.dma_start(gw[:], t["L1_ffn_gate_w"].rearrange("(k p) e -> p k e", p=P)).then_inc(s_w, 16)
                    eng.dma_start(gb[:], t["L1_ffn_gate_b"].partition_broadcast(P)).then_inc(s_w, 16)

                @block.gpsimd
                def _(eng):
                    eng.iota(rev[:], pattern=[[-1, E1]], base=E1, channel_multiplier=0,
                             allow_small_or_imprecise_dtypes=True).then_inc(s_c, 1)

                @block.tensor
                def _(eng):
                    eng.wait_ge(s_w, 32)
                    for n in range(NT):
                        for k in range(KD):
                            ins = eng.matmul(pl[:, n * E1:(n + 1) * E1], zT[:, k, n * P:(n + 1) * P], gw[:, k, :],
                                             start=(k == 0), stop=(k == KD - 1))
                    ins.then_inc(s_l, 1)
                    eng.wait_ge(s_as, 1)
                    for x, src in enumerate((lg, sc)):
                        for c in range(4):
                            need(eng, s_tc, x * 4 + c - 3)
                            for j in range(ST):
                                ins = eng.transpose(pt[0:E1, c, j * P:(j + 1) * P], src[:, c * ST + j, :], self.ident[:])
                            ins.then_inc(s_t, 1)

                @block.scalar
                def _(eng):
                    eng.wait_ge(s_d, 1)
                    eng.activation(sc[:], tmp[:], ACT.Exp).then_inc(s_e, 1)
                    for x, dst in enumerate((lgT, asT)):
                        for c in range(4):
                            eng.wait_ge(s_t, x * 4 + c + 1)
                            eng.copy(dst[:, c * 512:(c + 1) * 512], pt[0:E1, c, :]).then_inc(s_tc, 1)

                @block.vector
                def _(eng):
                    do = Chain(eng, s_ch)

                    def then(ins):
                        do(ins)
                        do.wait()

                    eng.wait_ge(s_w, 32)
                    eng.wait_ge(s_c, 1)
                    eng.wait_ge(s_l, 1)
                    then(eng.tensor_copy(lg[:].rearrange("p n e -> p (n e)"), pl[:, 0:NT * E1]))
                    then(eng.tensor_reduce(m[:], lg[:], AX, ALU.max))
                    eng.tensor_tensor(tmp[:], lg[:], per_token(m), ALU.subtract).then_inc(s_d, 1)
                    eng.wait_ge(s_e, 1)
                    then(eng.tensor_reduce(m[:], sc[:], AX, ALU.add))
                    then(eng.reciprocal(m[:], m[:]))
                    then(eng.tensor_tensor(sc[:], sc[:], per_token(m), ALU.mult))
                    then(eng.tensor_tensor(sc[:], sc[:], per_expert(gb), ALU.add))
                    for k in range(TOPK):
                        then(eng.tensor_reduce(m[:], sc[:], AX, ALU.max))
                        then(eng.tensor_tensor(tmp[:], sc[:], per_token(m), ALU.is_equal))
                        then(eng.tensor_tensor(tmp[:], tmp[:], per_expert(rev), ALU.mult))
                        then(eng.tensor_reduce(m[:], tmp[:], AX, ALU.max))
                        then(eng.tensor_tensor(oh[:, k], per_expert(rev), per_token(m), ALU.is_equal))
                        then(eng.tensor_tensor(tmp[:], oh[:, k], lg[:], ALU.mult))
                        then(eng.tensor_reduce(w_k[:, k, :], tmp[:], AX, ALU.add))
                        if k + 1 < TOPK:
                            then(eng.scalar_tensor_tensor(out=sc[:], in0=oh[:, k], scalar=LOWEST, in1=sc[:], op0=ALU.mult, op1=ALU.add))
                    then(eng.tensor_tensor(sc[:], oh[:, 0], oh[:, 1], ALU.add))
                    eng.sem_inc(s_as, 1)

    def capacity(self, lgT, asT, oh, scatter, gather):
        nc = self.nc
        R = [E1, N]
        G = [P, NT, E1]
        with ExitStack() as ctx:
            flip = self.sb("flip", R, I32, ctx=ctx)
            hi, lo, t0, t1 = (self.sb(n, R, ctx=ctx) for n in ("hi", "lo", "t0", "t1"))
            thr, cand, bit, cnt, want, gain, first = (self.sb(n, [E1, 1], ctx=ctx) for n in
                                                      ("thr", "cand", "bit", "cnt", "want", "gain", "first"))
            own = self.sb("own", [P, TOPK, NT], ctx=ctx)
            pos, kept, tmp = (self.sb(n, G, ctx=ctx) for n in ("pos", "kept", "tmp"))
            pk, kk, idx = (self.sb(n, [P, TOPK, NT], ctx=ctx) for n in ("pk", "kk", "idx"))
            pt = self.ps("pt", [P, 2, 512], ctx)
            s_c, s_ch, s_k, s_t = (self.sem(n, ctx) for n in ("s_c", "s_ch", "s_k", "s_t"))
            with nc.Block() as block:
                @block.gpsimd
                def _(eng):
                    eng.iota(own[:], pattern=[[N, TOPK], [P, NT]], base=DROP_ROW, channel_multiplier=1,
                             allow_small_or_imprecise_dtypes=True).then_inc(s_c, 1)
                    eng.iota(first[:], pattern=[[0, 1]], base=-1, channel_multiplier=CAP,
                             allow_small_or_imprecise_dtypes=True).then_inc(s_c, 1)

                @block.tensor
                def _(eng):
                    eng.wait_ge(s_k, 1)
                    for x, src in enumerate((t1, t0)):
                        for n in range(NT):
                            ins = eng.transpose(pt[:, x, n * E1:(n + 1) * E1], src[:, n * P:(n + 1) * P], self.ident[0:E1, 0:E1])
                    ins.then_inc(s_t, 1)

                @block.vector
                def _(eng):
                    do = Chain(eng, s_ch)

                    def then(ins):
                        do(ins)
                        do.wait()

                    def count(src, than, op):
                        then(eng.tensor_scalar(t0[:], src[:], than, 0.0, op, ALU.add, accum_out=cnt[:]))

                    def search(src):
                        then(eng.memset(thr[:], 0.0))
                        then(eng.memset(bit[:], 32768.0))
                        with eng.Fori(0, 16) as i:
                            do.enter(i, 5)
                            then(eng.tensor_tensor(cand[:], thr[:], bit[:], ALU.add))
                            count(src, cand[:, 0:1], ALU.is_ge)
                            then(eng.tensor_scalar(gain[:], cnt[:], want[:, 0:1], bit[:, 0:1], ALU.is_ge, ALU.mult))
                            then(eng.tensor_tensor(thr[:], thr[:], gain[:], ALU.add))
                            then(eng.tensor_scalar(bit[:], bit[:], 0.5, None, ALU.mult))
                            do.leave(16)

                    bits = lgT[:].bitcast(I32)
                    then(eng.tensor_scalar(flip[:], bits, 31, None, ALU.arith_shift_right))
                    then(eng.tensor_scalar(flip[:], flip[:], -2147483648, None, ALU.bitwise_or))
                    then(eng.tensor_tensor(flip[:], flip[:], bits, ALU.bitwise_xor))
                    then(eng.tensor_scalar(t0[:].bitcast(I32), flip[:], 16, 0xffff, ALU.logical_shift_right, ALU.bitwise_and))
                    then(eng.tensor_copy(hi[:], t0[:].bitcast(I32)))
                    then(eng.tensor_scalar(t1[:].bitcast(I32), flip[:], 0xffff, None, ALU.bitwise_and))
                    then(eng.tensor_copy(lo[:], t1[:].bitcast(I32)))
                    then(eng.scalar_tensor_tensor(out=hi[:], in0=hi[:], scalar=1.0, in1=asT[:], op0=ALU.add, op1=ALU.mult))
                    then(eng.tensor_scalar(hi[:], hi[:], -1.0, None, ALU.add))
                    then(eng.memset(want[:], float(CAP)))
                    search(hi)
                    count(hi, thr[:, 0:1], ALU.is_gt)
                    then(eng.tensor_tensor(want[:], want[:], cnt[:], ALU.subtract))
                    then(eng.tensor_scalar(t1[:], hi[:], thr[:, 0:1], None, ALU.is_equal))
                    then(eng.scalar_tensor_tensor(out=lo[:], in0=lo[:], scalar=1.0, in1=t1[:], op0=ALU.add, op1=ALU.mult))
                    then(eng.tensor_scalar(lo[:], lo[:], -1.0, None, ALU.add))
                    then(eng.tensor_copy(hi[:], t0[:]))
                    search(lo)
                    count(lo, thr[:, 0:1], ALU.is_gt)
                    then(eng.tensor_tensor(want[:], want[:], cnt[:], ALU.subtract))
                    then(eng.tensor_tensor(hi[:], hi[:], t0[:], ALU.add))
                    then(eng.tensor_scalar(lo[:], lo[:], thr[:, 0:1], None, ALU.is_equal))
                    zeros = self.zeros[0:E1, 0:N]
                    then(eng.tensor_tensor_scan(t1[:], lo[:], zeros, 0.0, ALU.add, ALU.add))
                    then(eng.tensor_scalar(t1[:], t1[:], want[:, 0:1], None, ALU.is_le))
                    then(eng.tensor_tensor(t1[:], t1[:], lo[:], ALU.mult))
                    then(eng.tensor_tensor(t0[:], hi[:], t1[:], ALU.add))
                    eng.wait_ge(s_c, 2)
                    then(eng.tensor_tensor_scan(t1[:], t0[:], zeros, first[:, 0:1], ALU.add, ALU.add))
                    eng.sem_inc(s_k, 1)
                    eng.wait_ge(s_t, 1)
                    then(eng.tensor_copy(pos[:].rearrange("p n e -> p (n e)"), pt[:, 0, 0:NT * E1]))
                    then(eng.tensor_copy(kept[:].rearrange("p n e -> p (n e)"), pt[:, 1, 0:NT * E1]))
                    for k in range(TOPK):
                        then(eng.tensor_tensor(tmp[:], oh[:, k], pos[:], ALU.mult))
                        then(eng.tensor_reduce(pk[:, k, :], tmp[:], AX, ALU.add))
                        then(eng.tensor_tensor(tmp[:], oh[:, k], kept[:], ALU.mult))
                        then(eng.tensor_reduce(kk[:, k, :], tmp[:], AX, ALU.add))
                    then(eng.tensor_tensor(idx[:], pk[:], own[:], ALU.subtract))
                    then(eng.tensor_tensor(idx[:], idx[:], kk[:], ALU.mult))
                    then(eng.tensor_tensor(idx[:], idx[:], own[:], ALU.add))
                    then(eng.tensor_copy(scatter[:], idx[:]))
                    then(eng.tensor_scalar(idx[:], pk[:], float(-ZERO_ROW), None, ALU.add))
                    then(eng.tensor_tensor(idx[:], idx[:], kk[:], ALU.mult))
                    then(eng.tensor_scalar(idx[:], idx[:], float(ZERO_ROW), None, ALU.add))
                    then(eng.tensor_copy(gather[:], idx[:]))

    def dispatch(self, z, scatter, XS, YS):
        nc = self.nc
        with ExitStack() as ctx:
            s_z, s_s = self.sem("s_z", ctx), self.sem("s_s", ctx)
            with nc.Block() as block:
                @block.sync
                def _(eng):
                    eng.dma_start(XS[0:L1_SLOTS].rearrange("(p r) d -> p r d", p=P), self.zero_rows(L1_SLOTS // P)).then_inc(s_z, 16)
                    eng.dma_start(YS[ZERO_ROW:ZERO_ROW + P], self.zeros[:, 0:D]).then_inc(s_z, 16)
                    eng.wait_ge(s_z, 32)

                @block.gpsimd
                def _(eng):
                    eng.wait_ge(s_z, 32)
                    for n in range(NT):
                        for k in range(TOPK):
                            eng.indirect_dma_start(out=XS, out_offset=bass.IndirectOffsetOnAxis(ap=scatter[:, k, n:n + 1], axis=0),
                                                   in_=z[:, n, :], in_offset=None).then_inc(s_s, 16)
                    eng.wait_ge(s_s, 16 * NT * TOPK)

    def shared(self, zT, x):
        nc, t = self.nc, self.t
        MF = FSH // P
        with ExitStack() as ctx:
            w1, w3 = (self.sb(n, [P, KD, FSH], ctx=ctx) for n in ("w1", "w3"))
            w2 = self.sb("w2", [P, MF, D], ctx=ctx)
            act = self.sb("act", [P, 2, S], ctx=ctx)
            g = self.sb("g", [P, 2, MF, S], ctx=ctx)
            p1 = self.ps("p1", [P, 2, 512], ctx)
            p3 = self.ps("p3", [P, 2, 512], ctx)
            py = self.ps("py", [P, 2, 512], ctx)
            s_w, s_h, s_a, s_g, s_y, s_x = (self.sem(n, ctx) for n in ("s_w", "s_h", "s_a", "s_g", "s_y", "s_x"))
            with nc.Block() as block:
                @block.sync
                def _(eng):
                    for w, src in ((w1, t["L1_ffn_sw1"]), (w3, t["L1_ffn_sw3"])):
                        for k in range(KD):
                            eng.dma_start(w[:, k].rearrange("p (s f) -> p s f", s=NSH),
                                          src[:, k * P:(k + 1) * P, :].rearrange("s p f -> p s f")).then_inc(s_w, 16)
                    eng.dma_start(w2[:], t["L1_ffn_sw2"].rearrange("s (m p) d -> p (s m) d", p=P)).then_inc(s_w, 16)

                @block.tensor
                def _(eng):
                    eng.wait_ge(s_w, 80)

                    def down(c):
                        for j in range(ST):
                            n = c * ST + j
                            if j == 0:
                                eng.wait_ge(s_g, (c + 1) * MF)
                            need(eng, s_x, n - 1)
                            for m in range(MF):
                                ins = eng.matmul(py[:, n % 2, 0:D], g[:, c % 2, m, j * P:(j + 1) * P], w2[:, m, :],
                                                 start=(m == 0), stop=(m == MF - 1))
                            ins.then_inc(s_y, 1)

                    for c in range(B):
                        for m in range(MF):
                            q = c * MF + m
                            need(eng, s_g, q - 1)
                            for w, bank in ((w1, p1), (w3, p3)):
                                for k in range(KD):
                                    ins = eng.matmul(bank[:, q % 2, :], w[:, k, m * P:(m + 1) * P], zT[:, k, c * S:(c + 1) * S],
                                                     start=(k == 0), stop=(k == KD - 1))
                            ins.then_inc(s_h, 1)
                        if c:
                            down(c - 1)
                    down(B - 1)

                @block.scalar
                def _(eng):
                    for q in range(B * MF):
                        eng.wait_ge(s_h, q + 1)
                        need(eng, s_g, q - 1)
                        eng.activation(act[:, q % 2, :], p1[:, q % 2, :], ACT.Silu).then_inc(s_a, 1)

                @block.vector
                def _(eng):
                    def add(c):
                        for j in range(ST):
                            n = c * ST + j
                            eng.wait_ge(s_y, n + 1)
                            eng.scalar_tensor_tensor(out=x[:, n, :], in0=py[:, n % 2, 0:D], scalar=1.0 / NSH, in1=x[:, n, :],
                                                     op0=ALU.mult, op1=ALU.add).then_inc(s_x, 1)

                    for c in range(B):
                        for m in range(MF):
                            q = c * MF + m
                            eng.wait_ge(s_a, q + 1)
                            need(eng, s_y, (c - 1) * ST)
                            eng.tensor_tensor(g[:, c % 2, m, :], act[:, q % 2, :], p3[:, q % 2, :], ALU.mult).then_inc(s_g, 1)
                        if c:
                            add(c - 1)
                    add(B - 1)

    def experts(self, XS, YS):
        nc, t = self.nc, self.t
        MF = FF1 // P
        NTL = len(CAP_TILES)
        with ExitStack() as ctx:
            w1, w3 = (self.sb(n, [P, 2, KD, FF1], ctx=ctx) for n in ("w1", "w3"))
            w2 = self.sb("w2", [P, 2, MF, D], ctx=ctx)
            xs = self.sb("xs", [P, 2, NTL, D], ctx=ctx)
            xT = self.sb("xT", [P, 2, KD, CAP], ctx=ctx)
            act = self.sb("act", [P, 2, CAP], ctx=ctx)
            g = self.sb("g", [P, 2, MF, CAP], ctx=ctx)
            ys = self.sb("ys", [P, 2, NTL, D], ctx=ctx)
            px = self.ps("px", [P, KD, 512], ctx)
            p1 = self.ps("p1", [P, 2, 512], ctx)
            p3 = self.ps("p3", [P, 2, 512], ctx)
            py = self.ps("py", [P, 2, 512], ctx)
            s_x, s_xt, s_h, s_a, s_g, s_y, s_yb = (self.sem(n, ctx) for n in ("s_x", "s_xt", "s_h", "s_a", "s_g", "s_y", "s_yb"))
            s_w = [self.sem("s_w", ctx) for _ in range(2)]
            s_st = [self.sem("s_st", ctx) for _ in range(2)]
            LOADS = (3 + NTL) * 16
            with nc.Block() as block:
                @block.sync
                def _(eng):
                    def step(i, u, par):
                        if not inside(i, E1):
                            return
                        need(eng, s_y, (i - 1) * NTL)
                        one = bass.ds(i, 1)
                        for j, (s, rows) in enumerate(CAP_TILES):
                            eng.dma_start(xs[0:rows, par, j, :], XS[bass.ds(i * CAP + s, rows), :]).then_inc(s_w[par], 16)
                        for w, src in ((w1, "L1_ffn_ew1"), (w3, "L1_ffn_ew3"), (w2, "L1_ffn_ew2")):
                            eng.dma_start(w[:, par], t[src][one].rearrange("o (k p) f -> p (o k) f", p=P)).then_inc(s_w[par], 16)
                    steps(eng, step, E1, ahead=2, behind=0)

                @block.tensor
                def _(eng):
                    def step(i, u, par):
                        eng.wait_ge(s_w[par], (u + 1) * LOADS)
                        need(eng, s_xt, i * KD)
                        for k in range(KD):
                            for j, (s, rows) in enumerate(CAP_TILES):
                                ins = eng.transpose(px[:, k, s:s + rows], xs[0:rows, par, j, k * P:(k + 1) * P],
                                                    self.ident[0:rows, 0:rows])
                            ins.then_inc(s_x, 1)
                        eng.wait_ge(s_xt, (i + 1) * KD)
                        for m in range(MF):
                            if m < 2:
                                need(eng, s_g, i * MF + m - 1)
                            else:
                                eng.wait_ge(s_g, i * MF + m - 1)
                            for w, bank in ((w1, p1), (w3, p3)):
                                for k in range(KD):
                                    ins = eng.matmul(bank[:, m % 2, 0:CAP], w[:, par, k, m * P:(m + 1) * P], xT[:, par, k, :],
                                                     start=(k == 0), stop=(k == KD - 1))
                            ins.then_inc(s_h, 1)
                        eng.wait_ge(s_g, (i + 1) * MF)
                        for j, (s, rows) in enumerate(CAP_TILES):
                            if j < 2:
                                need(eng, s_yb, i * NTL + j - 1)
                            else:
                                eng.wait_ge(s_yb, i * NTL + j - 1)
                            for m in range(MF):
                                ins = eng.matmul(py[0:rows, (par + j) % 2, 0:D], g[:, par, m, s:s + rows], w2[:, par, m, :],
                                                 start=(m == 0), stop=(m == MF - 1))
                            ins.then_inc(s_y, 1)
                    steps(eng, step, E1, ahead=2, behind=0)

                @block.scalar
                def _(eng):
                    def step(i, u, par):
                        for k in range(KD):
                            eng.wait_ge(s_x, i * KD + k + 1)
                            eng.copy(xT[:, par, k, :], px[:, k, 0:CAP]).then_inc(s_xt, 1)
                        for m in range(MF):
                            eng.wait_ge(s_h, i * MF + m + 1)
                            need(eng, s_g, i * MF + m - 1)
                            eng.activation(act[:, m % 2, :], p1[:, m % 2, 0:CAP], ACT.Silu).then_inc(s_a, 1)
                        eng.wait_ge(s_yb, (i + 1) * NTL)
                        for j, (s, rows) in enumerate(CAP_TILES):
                            eng.dma_start(YS[bass.ds(i * CAP + s, rows), :], ys[0:rows, par, j, :]).then_inc(s_st[par], 16)
                    steps(eng, step, E1, ahead=2, behind=0)
                    for s in s_st:
                        eng.wait_ge(s, 16 * NTL * E1 // 2)

                @block.vector
                def _(eng):
                    def step(i, u, par):
                        for m in range(MF):
                            eng.wait_ge(s_a, i * MF + m + 1)
                            if m == 0:
                                need(eng, s_y, (i - 1) * NTL)
                            eng.tensor_tensor(g[:, par, m, :], act[:, m % 2, :], p3[:, m % 2, 0:CAP], ALU.mult).then_inc(s_g, 1)
                        if not isinstance(i, int) or i >= 2:
                            eng.wait_ge(s_st[par], u * 16 * NTL)
                        for j, (s, rows) in enumerate(CAP_TILES):
                            eng.wait_ge(s_y, i * NTL + j + 1)
                            eng.tensor_copy(ys[0:rows, par, j, :], py[0:rows, (par + j) % 2, 0:D]).then_inc(s_yb, 1)
                    steps(eng, step, E1, ahead=2, behind=0)

    def combine_top2(self, gather, w_k, YS, x):
        nc = self.nc
        with ExitStack() as ctx:
            y = self.sb("y", [P, NT, TOPK, D], ctx=ctx)
            s_g, s_ch = [self.sem("s_g", ctx) for _ in range(4)], self.sem("s_ch", ctx)
            with nc.Block() as block:
                @block.gpsimd
                def _(eng):
                    for n in range(NT):
                        for k in range(TOPK):
                            eng.indirect_dma_start(out=y[:, n, k, :], out_offset=None, in_=YS,
                                                   in_offset=bass.IndirectOffsetOnAxis(ap=gather[:, k, n:n + 1], axis=0))\
                               .then_inc(s_g[n // ST], 16)

                @block.vector
                def _(eng):
                    do = Chain(eng, s_ch)
                    for b in range(B):
                        eng.wait_ge(s_g[b], 16 * ST * TOPK)
                        for k in range(TOPK):
                            for n in range(b * ST, (b + 1) * ST):
                                do(eng.scalar_tensor_tensor(out=x[:, n, :], in0=y[:, n, k, :], scalar=w_k[:, k, n:n + 1], in1=x[:, n, :],
                                                            op0=ALU.mult, op1=ALU.add))
                            do.wait()


def build(nc, t, out):
    p = Program(nc, t, out)
    with p.ctx:
        p.load()
        QS = p.dram("q_stacks", [2, NBH, DK, S])
        KS = p.dram("k_stacks", [2, NBH, DK, S])
        with ExitStack() as ctx:
            V = p.sb("V", [P, NBH, ST, DK + 1], ctx=ctx)
            O = p.sb("O", [P, NBH, ST, DK], ctx=ctx)
            with ExitStack() as inner:
                z = p.sb("z", [P, NT, D], ctx=inner)
                zT = p.sb("zT", [P, KD, N], ctx=inner)
                cT = p.sb("cT", [P, KD, N], ctx=inner)
                p.norm_and_transpose(p.x, z, zT)
                p.load_context(cT)
                p.project(zT, cT, t["L0_xattn_Wq"], t["L0_xattn_Wk"], t["L0_xattn_Wv"], None, None, None, 1.0, QS, KS, V)
            with ExitStack() as inner:
                mask = p.dram("mask", [B, P, ST, S], BF16)
                p.prepare_mask(mask)
                p.attention("mask", QS, KS, V, O, DK ** -0.5, mask=mask, k_aux=-1e-9 * DK ** 0.5)
            p.output(O, t["L0_xattn_Wo"], None, p.x, p.x)
        with ExitStack() as ctx:
            f = {n[7:]: v for n, v in t.items() if n.startswith("L0_ffn_")}
            src = p.sb("src", [P, NT, D], ctx=ctx)
            xx = p.sb("xx", [P, NT, D], ctx=ctx)
            slot = p.sb("slot", [P, NT], U32, ctx=ctx)
            tile_expert = p.sb("tile_expert", [P, L0_TILES], I32, ctx=ctx)
            XS = p.dram("top1_in", [L0_SLOTS, D])
            YS = p.dram("top1_out", [L0_SLOTS, D])
            with ExitStack() as inner:
                V = p.sb("V", [P, NBH, ST, DK + 1], ctx=inner)
                O = p.sb("O", [P, NBH, ST, DK], ctx=inner)
                with ExitStack() as deep:
                    sT = p.sb("sT", [P, KD, N], ctx=deep)
                    p.norm_and_transpose(p.x, src, sT)
                    p.project(sT, sT, f["Wq"], f["Wk"], f["Wv"], f["bq"], f["bk"], f["bv"], DK ** -0.5, QS, KS, V)
                p.attention("self", QS, KS, V, O, 1.0)
                p.output(O, f["Wo"], f["bo"], src, src)
            p.route_top1(src, xx, f["ln1_g"], f["ln1_b"], slot, tile_expert, XS)
            p.top1_tiles(tile_expert, XS, YS)
            p.combine_top1(xx, slot, YS, f["ln2_g"], f["ln2_b"], p.x)
        p.recycle()
        with ExitStack() as ctx:
            f = {n[9:]: v for n, v in t.items() if n.startswith("L1_xattn_")}
            V = p.sb("V", [P, NBH, ST, DK + 1], ctx=ctx)
            O = p.sb("O", [P, NBH, ST, DK], ctx=ctx)
            with ExitStack() as inner:
                z = p.sb("z", [P, NT, D], ctx=inner)
                zT = p.sb("zT", [P, KD, N], ctx=inner)
                cT = p.sb("cT", [P, KD, N], ctx=inner)
                p.norm_and_transpose(p.x, z, zT)
                p.load_context(cT)
                p.project(zT, cT, f["Wq"], f["Wk"], f["Wv"], f["bq"], f["bk"], f["bv"], DK ** -0.5 / 2, QS, KS, V)
            with ExitStack() as inner:
                common = p.sb("common", [P, B, ST, S], ctx=inner)
                p.prepare_common(common)
                side = t["fside_Bx16xSxS2_0"].rearrange("b h (t p) k -> (b h) p t k", p=P)
                p.attention("side", QS, KS, V, O, 2.0, common=common, side=side)
            p.output(O, f["Wo"], f["bo"], p.x, p.x)
        with ExitStack() as ctx:
            w_k = p.sb("w_k", [P, TOPK, NT], ctx=ctx)
            oh = p.sb("oh", [P, TOPK, NT, E1], ctx=ctx)
            scatter = p.sb("scatter", [P, TOPK, NT], U32, ctx=ctx)
            gather = p.sb("gather", [P, TOPK, NT], U32, ctx=ctx)
            XS = p.dram("top2_in", [L1_ROWS, D])
            YS = p.dram("top2_out", [ZERO_ROW + P, D])
            with ExitStack() as inner:
                z = p.sb("z", [P, NT, D], ctx=inner)
                zT = p.sb("zT", [P, KD, N], ctx=inner)
                p.norm_and_transpose(p.x, z, zT)
                with ExitStack() as deep:
                    lgT = p.sb("lgT", [E1, N], ctx=deep)
                    asT = p.sb("asT", [E1, N], ctx=deep)
                    p.gate(zT, w_k, oh, lgT, asT)
                    p.capacity(lgT, asT, oh, scatter, gather)
                p.dispatch(z, scatter, XS, YS)
                p.shared(zT, p.x)
            p.experts(XS, YS)
            p.combine_top2(gather, w_k, YS, p.x)
        p.store(p.x)


_TRANSPOSED = ("L0_xattn_Wq", "L0_xattn_Wk", "L0_xattn_Wv", "L0_xattn_Wo", "L1_xattn_Wq", "L1_xattn_Wk", "L1_xattn_Wv",
               "L1_xattn_Wo", "ctx_1024")


def kernel(**inputs):
    import numpy as np
    import concourse.bacc as bacc
    from concourse.bass_utils import run_bass_kernel_spmd

    nc = bacc.Bacc("TRN2", target_bir_lowering=False, num_devices=1)
    arrays, t = {}, {}
    for name, a in inputs.items():
        a = np.asarray(a)
        if name in _TRANSPOSED:
            a = a.reshape(-1, a.shape[-1]).T
        if name == "L0_ffn_b1":
            a = a.reshape(E0, -1, P).transpose(0, 2, 1)
        if name[-3:] in ("_bq", "_bk"):
            a = a.reshape(KD, P).T
        a = np.ascontiguousarray(a)
        arrays[f"in_{name}"] = a
        t[name] = nc.dram_tensor(f"in_{name}", a.shape, mybir.dt.from_np(a.dtype), kind="ExternalInput").ap()
    out = nc.dram_tensor("out", [B, S, D], F32, kind="ExternalOutput").ap()
    build(nc, t, out)
    r = run_bass_kernel_spmd(nc, [arrays], core_ids=[0])
    return r.results[0]["out"]
```

```python
from contextlib import ExitStack

import concourse.bass as bass
from concourse import mybir
from concourse.alu_op_type import AluOpType as ALU

F32 = mybir.dt.float32
F32R = mybir.dt.float32r
BF16 = mybir.dt.bfloat16
I32 = mybir.dt.int32
U32 = mybir.dt.uint32
ACT = mybir.ActivationFunctionType
AX = mybir.AxisListType.X

P = 128
B, S, D, H = 4, 512, 256, 16
DK = D // H
VW = 2 * DK + 1
N = B * S
NT = N // P
ST = S // P
KD = D // P
NBH = B * H
SPLIT = 3
EPS = 1e-5
LOWEST = -3.0e38
E0, FF0 = 4, 1024
E1, FF1, TOPK = 16, 512, 2
CAP = -(-N * TOPK // E1 * 5 // 4)
NSH = 2
FSH = NSH * FF1

L0_TILES = 20
L0_SLOTS = L0_TILES * P
L1_SLOTS = E1 * CAP
ZERO_ROW = L1_SLOTS
DROP_ROW = L1_SLOTS + P
L1_ROWS = DROP_ROW + TOPK * N
CAP_TILES = [(s, min(P, CAP - s)) for s in range(0, CAP, P)]


class Step:

    def __init__(self, i, half, odd, quarter, slot):
        self.i, self.half, self.odd, self.quarter, self.slot = i, half, odd, quarter, slot


def steps(eng, step, trips, ahead=4, behind=2):
    assert ahead % 4 == 0 and trips % 4 == 0

    def plain(i):
        step(Step(i, i // 2, i % 2, i // 4, i % 4))

    for i in range(ahead):
        plain(i)
    with eng.Fori(ahead // 4, trips // 4) as v:
        for j in range(4):
            step(Step(v * 4 + j, v * 2 + j // 2, j % 2, v, j))
    for i in range(trips, trips + behind):
        plain(i)


def need(eng, sem, value):
    if not isinstance(value, int) or value > 0:
        eng.wait_ge(sem, value)


def unfused(eng, spare, i):
    if not isinstance(i, int):
        eng.sem_inc(spare, 1)


def inside(i, trips):
    return not isinstance(i, int) or 0 <= i < trips


class Chain:

    def __init__(self, eng, sem):
        self.eng, self.sem, self.base, self.k, self.loop, self.rate = eng, sem, 0, 0, None, 0

    def __call__(self, ins):
        ins.then_inc(self.sem, 1)
        self.k += 1
        return ins

    def wait(self):
        self.eng.wait_ge(self.sem, self.value())

    def value(self):
        at = self.base + self.k
        return at if self.loop is None else self.loop * self.rate + at

    def enter(self, loop, rate):
        self.base, self.k, self.loop, self.rate = self.base + self.k, 0, loop, rate

    def leave(self, trips):
        assert self.k == self.rate, (self.k, self.rate)
        self.base, self.k, self.loop = self.base + trips * self.rate, 0, None


class Program:
    def __init__(self, nc, t, out):
        self.nc, self.t, self.out, self.ctx = nc, t, out, ExitStack()
        self.n_sem, self.used = 0, []

    def sem(self, name, ctx=None):
        self.n_sem += 1
        self.used.append(self.nc.alloc_semaphore(f"{name}_{self.n_sem}"))
        return self.used[-1]

    def recycle(self):
        self.nc.clear_and_free_semaphores(self.used)
        self.nc.all_engine_barrier()
        self.used = []

    def sb(self, name, shape, dt=F32, ctx=None):
        self.n_sem += 1
        return (ctx or self.ctx).enter_context(self.nc.sbuf_tensor(f"{name}_{self.n_sem}", shape, dt))

    def ps(self, name, shape, ctx):
        self.n_sem += 1
        return ctx.enter_context(self.nc.psum_tensor(f"{name}_{self.n_sem}", shape, F32))

    def dram(self, name, shape, dt=F32):
        return self.nc.dram_tensor(name, shape, dt, kind="Internal").ap()

    def load(self):
        nc = self.nc
        self.x = self.sb("x", [P, NT, D])
        self.ident = self.sb("ident", [P, P])
        self.zeros = self.sb("zeros", [P, 2048])
        s_x, s_c = self.sem("s_x"), self.sem("s_c")
        with nc.Block() as block:
            @block.sync
            def _(eng):
                eng.dma_start(self.x[:], self.t["x"].rearrange("b (t p) d -> p (b t) d", p=P)).then_inc(s_x, 16)
                eng.wait_ge(s_x, 16)

            @block.gpsimd
            def _(eng):
                eng.memset(self.ident[:], 0.0).then_inc(s_c, 1)
                eng.memset(self.zeros[:], 0.0)
                eng.wait_ge(s_c, 1)
                eng.affine_select(out=self.ident[:], in_=self.ident[:], compare_op=ALU.not_equal, fill=1.0,
                                  base=0, pattern=[[-1, P]], channel_multiplier=1)

    def normalise(self, block, chain_sem, s_mv, s_rs, s_z, dst, src, ctx, gain=None, shift=None):
        st = self.sb("bn", [P, NT, 6], ctx=ctx)
        mv = self.sb("mv", [P, NT, 2], ctx=ctx)
        rs = self.sb("rs", [P, NT], ctx=ctx)

        @block.vector
        def _(eng):
            chain = Chain(eng, chain_sem)
            for n in range(NT):
                chain(eng.bn_stats(st[:, n, :], src[:, n, :]))
            chain.wait()
            for n in range(NT):
                chain(eng.bn_aggr(mv[:, n, :], st[:, n, :]))
            chain.wait()
            eng.tensor_scalar(rs[:], mv[:, :, 1], EPS, None, ALU.add).then_inc(s_mv, 1)
            eng.wait_ge(s_rs, 1)
            chain(eng.reciprocal(rs[:], rs[:]))
            chain.wait()
            for b in range(B):
                for j in range(ST):
                    n = b * ST + j
                    chain(eng.tensor_scalar(dst[:, n, :], src[:, n, :], mv[:, n, 0:1], rs[:, n:n + 1],
                                            ALU.subtract, ALU.mult))
                if gain is not None:
                    rows = dst[:, b * ST:(b + 1) * ST, :]
                    chain.wait()
                    chain(eng.tensor_tensor(rows, rows, gain[:].unsqueeze(1).to_broadcast([P, ST, D]), ALU.mult))
                    chain.wait()
                    chain(eng.tensor_tensor(rows, rows, shift[:].unsqueeze(1).to_broadcast([P, ST, D]), ALU.add))
                chain.wait()
                eng.sem_inc(s_z, 1)

        return rs

    @staticmethod
    def deviations(eng, s_mv, s_rs, rs):
        eng.wait_ge(s_mv, 1)
        eng.activation(rs[:], rs[:], ACT.Sqrt).then_inc(s_rs, 1)

    def norm_and_transpose(self, src, nat, featT):
        nc = self.nc
        with ExitStack() as ctx:
            bank = self.ps("tp", [P, 4, 512], ctx)
            s_ch, s_mv, s_rs, s_z, s_tr, s_ev = (self.sem(n, ctx) for n in ("s_ch", "s_mv", "s_rs", "s_z", "s_tr", "s_ev"))
            with nc.Block() as block:
                rs = self.normalise(block, s_ch, s_mv, s_rs, s_z, nat, src, ctx)

                @block.tensor
                def _(eng):
                    for b in range(B):
                        eng.wait_ge(s_z, b + 1)
                        self.transposes(eng, nat, bank, b, s_tr, s_ev)

                @block.scalar
                def _(eng):
                    self.deviations(eng, s_mv, s_rs, rs)
                    for n in range(B * KD):
                        eng.wait_ge(s_tr, n + 1)
                        b, k = divmod(n, KD)
                        eng.copy(featT[:, k, b * S:(b + 1) * S], bank[:, n % 4, :]).then_inc(s_ev, 1)

    def transposes(self, eng, nat, bank, b, s_tr, s_ev):
        for k in range(KD):
            n = b * KD + k
            need(eng, s_ev, n - 3)
            for j in range(ST):
                ins = eng.transpose(bank[:, n % 4, j * P:(j + 1) * P], nat[:, b * ST + j, k * P:(k + 1) * P], self.ident[:])
            ins.then_inc(s_tr, 1)

    def project(self, qT, kvT, wq, wk, wv, bq, bk, bv, q_scale, QS, KS, V):
        nc = self.nc
        with ExitStack() as ctx:
            W = [self.sb(n, [P, KD, D], ctx=ctx) for n in ("wq", "wk", "wv")]
            bias = self.sb("bias", [P, 2, KD], ctx=ctx)
            bvr = self.sb("bvr", [P, D], ctx=ctx)
            whole = self.sb("whole", [P, 2, 512], ctx=ctx)
            vw = self.sb("vw", [P, 2, H, DK], ctx=ctx)
            hi = self.sb("hi", [P, 4, 512], F32R, ctx=ctx)
            lo = self.sb("lo", [P, 4, 512], F32R, ctx=ctx)
            pj = self.ps("pj", [P, 4, 512], ctx)
            pv = self.ps("pv", [P, 4, 512], ctx)
            names = ("s_w", "s_z", "s_p", "s_t", "s_hi", "s_lo", "s_pv", "s_v", "s_one", "s_vh", "s_vl")
            s_w, s_z, s_p, s_t, s_hi, s_lo, s_pv, s_v, s_one, s_vh, s_vl = (self.sem(n, ctx) for n in names)
            s_st = [self.sem("s_st", ctx) for _ in range(4)]
            jobs = [(x, c, m) for x in range(2) for c in range(B) for m in range(KD)]
            n_bias = 3 if bq is not None else 0
            with nc.Block() as block:
                @block.sync
                def _(eng):
                    for w, src in zip(W, (wq, wk, wv)):
                        eng.dma_start(w[:], src.rearrange("(k p) n -> p k n", p=P)).then_inc(s_w, 16)
                    if n_bias:
                        eng.dma_start(bias[:, 0, :], bq).then_inc(s_w, 16)
                        eng.dma_start(bias[:, 1, :], bk).then_inc(s_w, 16)
                        eng.dma_start(bvr[:], bv.partition_broadcast(P)).then_inc(s_w, 16)
                    for n, (x, c, m) in enumerate(jobs):
                        rows = slice(c * H + m * (P // DK), c * H + (m + 1) * (P // DK))
                        for part, (s, buf) in enumerate(((s_hi, hi), (s_lo, lo))):
                            eng.wait_ge(s, n + 1)
                            eng.dma_start((QS, KS)[x][part, rows].rearrange("h d s -> (h d) s"), buf[:, n % 4, :].bitcast(F32)).then_inc(s_st[n % 4], 16)
                    for s in s_st:
                        eng.wait_ge(s, 32 * len(jobs) // 4)

                @block.tensor
                def _(eng):
                    eng.wait_ge(s_w, 16 * (3 + n_bias))
                    for n, (x, c, m) in enumerate(jobs):
                        need(eng, s_t, n - 3)
                        src = (qT, kvT)[x]
                        for k in range(KD):
                            ins = eng.matmul(pj[:, n % 4, :], W[x][:, k, m * P:(m + 1) * P], src[:, k, c * S:(c + 1) * S],
                                             start=(k == 0), stop=(k == KD - 1))
                        ins.then_inc(s_p, 1)
                        need(eng, s_v, n - 3)
                        for k in range(KD):
                            ins = eng.matmul(pv[:, n % 4, 0:D], kvT[:, k, n * P:(n + 1) * P], W[2][:, k, :],
                                             start=(k == 0), stop=(k == KD - 1))
                        ins.then_inc(s_pv, 1)

                @block.vector
                def _(eng):
                    eng.memset(V[:, :, :, DK:DK + 1].bitcast(F32), 1.0).then_inc(s_one, 1)
                    if not n_bias:
                        eng.memset(bias[:], 0.0).then_inc(s_one, 1)
                        eng.memset(bvr[:], 0.0).then_inc(s_one, 1)
                        eng.wait_ge(s_one, 3)
                    eng.wait_ge(s_w, 16 * (3 + n_bias))

                    def rest(n):
                        eng.wait_ge(s_hi, n + 1)
                        need(eng, s_st[n % 4], 32 * (n // 4))
                        eng.tensor_tensor(lo[:, n % 4, :], whole[:, n % 2, :], hi[:, n % 4, :].bitcast(F32), ALU.subtract)\
                           .then_inc(s_lo, 1)

                    for n, (x, c, m) in enumerate(jobs):
                        eng.wait_ge(s_p, n + 1)
                        need(eng, s_lo, n - 1)
                        eng.tensor_scalar(whole[:, n % 2, :], pj[:, n % 4, :], bias[:, x, m:m + 1], q_scale if x == 0 else 1.0,
                                          ALU.add, ALU.mult).then_inc(s_t, 1)
                        eng.wait_ge(s_pv, n + 1)
                        need(eng, s_vl, n - 1)
                        eng.tensor_tensor(vw[:, n % 2], pv[:, n % 4, 0:D].rearrange("p (h d) -> p h d", d=DK),
                                          bvr[:].rearrange("p (h d) -> p h d", d=DK), ALU.add).then_inc(s_v, 1)
                        rest(n)

                @block.scalar
                def _(eng):
                    for n in range(len(jobs)):
                        eng.wait_ge(s_t, n + 1)
                        need(eng, s_st[n % 4], 32 * (n // 4))
                        eng.copy(hi[:, n % 4, :], whole[:, n % 2, :]).then_inc(s_hi, 1)
                        eng.wait_ge(s_v, n + 1)
                        b, j = divmod(n, ST)
                        eng.copy(V[:, b * H:(b + 1) * H, j, 0:DK], vw[:, n % 2]).then_inc(s_vh, 1)

                @block.gpsimd
                def _(eng):
                    for n in range(NT):
                        eng.wait_ge(s_vh, n + 1)
                        b, j = divmod(n, ST)
                        heads = slice(b * H, (b + 1) * H)
                        eng.tensor_tensor(V[:, heads, j, DK + 1:VW], vw[:, n % 2], V[:, heads, j, 0:DK].bitcast(F32), ALU.subtract)\
                           .then_inc(s_vl, 1)

    def attention(self, kind, QS, KS, V, O, exp_scale, mask=None, common=None, side=None, k_aux=0.0):
        nc = self.nc
        with ExitStack() as ctx:
            q = self.sb("q", [P, 2, S], F32R, ctx=ctx)
            k = self.sb("k", [P, 2, S], F32R, ctx=ctx)
            v = self.sb("v", [P, 2, ST, VW], F32R, ctx=ctx)
            X = self.sb("X", [P, 2, ST, S], ctx=ctx)
            PH, PL = (self.sb(n, [P, 2, SPLIT, S], F32R, ctx=ctx) for n in ("PH", "PL"))
            PW = self.sb("PW", [P, 2, ST - SPLIT, S], ctx=ctx)
            OT = self.sb("OT", [VW, S], ctx=ctx)
            both = self.sb("both", [P, ST, DK], ctx=ctx)
            mx = self.sb("mx", [P, 2, ST], ctx=ctx)
            nm = self.sb("nm", [P, 2, ST], ctx=ctx)
            rec = self.sb("rec", [P, ST, 1], ctx=ctx)
            M = None if kind == "self" else self.sb("M", [P, 4, ST, S], BF16 if kind == "mask" else F32, ctx=ctx)
            pS = self.ps("pS", [P, 2, 512], ctx)
            pT = self.ps("pT", [P, 4, 512], ctx)
            pO = self.ps("pO", [P, 512], ctx)
            pB = self.ps("pB", [P, 512], ctx)
            names = ("s_c", "s_s", "s_x", "s_nm", "s_p", "s_t", "s_ea", "s_ed", "s_v", "s_o", "s_oc", "s_b", "s_r", "s_n",
                     "s_m", "s_z", "s_spv", "s_spt", "s_spg")
            (s_c, s_s, s_x, s_nm, s_p, s_t, s_ea, s_ed, s_v, s_o, s_oc, s_b, s_r, s_n, s_m, s_z, s_spv, s_spt, s_spg) = (self.sem(n, ctx) for n in names)
            s_ld = [self.sem("s_ld", ctx) for _ in range(2)]
            s_f = [self.sem("s_f", ctx) for _ in range(4)]
            PER = 6 * 16

            with nc.Block() as block:
                @block.sync
                def _(eng):
                    eng.wait_ge(s_c, 4)

                    def step(at):
                        i, par = at.i, at.odd
                        h = i - 2
                        if inside(h, NBH):
                            need(eng, s_s, (h - 1) * 4)
                            for r in range(4):
                                eng.dma_start(q[r * DK:(r + 1) * DK, par, :].bitcast(F32), QS[r // 2, bass.ds(h, 1)].rearrange("o d s -> (o d) s"))\
                                   .then_inc(s_ld[par], 16)
                            for r in range(2):
                                eng.dma_start(k[r * 2 * DK:(r + 1) * 2 * DK, par, :].bitcast(F32), KS[:, bass.ds(h, 1)].rearrange("r o d s -> r (o d) s"))\
                                   .then_inc(s_ld[par], 16)
                        if kind != "self" and inside(i, NBH):
                            need(eng, s_x, (i - 3) * 4)
                            src = side[bass.ds(i, 1)] if kind == "side" else mask[bass.ds(i // H, 1)]
                            eng.dma_start(M[:, at.slot], src.rearrange("o p t k -> (o p) t k")).then_inc(s_f[at.slot], 16)
                    steps(eng, step, NBH)

                @block.gpsimd
                def _(eng):
                    def bias(i, quarter, slot, b):
                        if kind == "side":
                            eng.wait_ge(s_f[slot], (quarter + 1) * 16)
                            unfused(eng, s_spg, i)
                            eng.tensor_tensor(M[:, slot], M[:, slot], common[:, bass.ds(b, 1)].rearrange("p o t k -> p (o t) k"),
                                              ALU.add).then_inc(s_m, 1)

                    def values(i, par):
                        need(eng, s_o, i - 1)
                        unfused(eng, s_spg, i)
                        eng.tensor_copy(v[:, par], V[:, bass.ds(i, 1)].rearrange("p o t d -> p (o t) d")).then_inc(s_v, 1)

                    eng.wait_ge(s_c, 4)
                    for i in range(4):
                        bias(i, 0, i, 0)
                        if i:
                            values(i - 1, 1 - i % 2)
                    with eng.Fori(1, H // 4) as w:
                        for slot in range(4):
                            bias(w * 4 + slot, w, slot, 0)
                            values(w * 4 + slot - 1, 1 - slot % 2)
                    with eng.Fori(1, B) as b:
                        with eng.Fori(0, H // 4) as w:
                            for slot in range(4):
                                i = b * H + w * 4 + slot
                                bias(i, b * (H // 4) + w, slot, b)
                                values(i - 1, 1 - slot % 2)
                    values(NBH - 1, 1)

                @block.tensor
                def _(eng):
                    eng.wait_ge(s_c, 4)

                    def scores(i, u, par, qts):
                        if not inside(i, NBH):
                            return
                        for qt in qts:
                            if qt == 0:
                                eng.wait_ge(s_ld[par], (u + 1) * PER)
                            if qt < 2:
                                need(eng, s_x, (i - 1) * 4 + qt + 3)
                            else:
                                eng.wait_ge(s_x, i * 4 + qt - 1)
                            eng.matmul(pS[:, qt % 2, :], q[:, par, qt * P:(qt + 1) * P], k[:, par, :], start=True, stop=True)\
                               .then_inc(s_s, 1)

                    def turn(t, par, kts):
                        if not inside(t, NBH):
                            return
                        for kt in kts:
                            if kt < SPLIT:
                                need(eng, s_ed, (t - 1) * SPLIT + kt + 1)
                            else:
                                need(eng, s_ea, t * ST)
                        for qt in range(ST):
                            if 0 in kts:
                                eng.wait_ge(s_p, t * 4 + qt + 1)
                            for kt in kts:
                                ins = eng.transpose(pT[:, kt, qt * P:(qt + 1) * P], X[:, par, qt, kt * P:(kt + 1) * P],
                                                    self.ident[:])
                                if qt == ST - 1:
                                    ins.then_inc(s_t, 1)

                    def step(at):
                        i, u, par = at.i, at.half, at.odd
                        scores(i, u, par, (0, 1))
                        turn(i - 1, 1 - par, (0, 1))
                        scores(i, u, par, (2,))
                        turn(i - 1, 1 - par, (2,))
                        scores(i, u, par, (3,))
                        turn(i - 1, 1 - par, (3,))
                        b = i - 3
                        if inside(b, NBH):
                            eng.wait_ge(s_oc, b + 1)
                            need(eng, s_n, b)
                            unfused(eng, s_spt, i)
                            for qt in range(ST):
                                ins = eng.transpose(pB[:, qt * VW:(qt + 1) * VW], OT[:, qt * P:(qt + 1) * P],
                                                    self.ident[0:VW, 0:VW])
                            ins.then_inc(s_b, 1)
                        a = i - 2
                        if inside(a, NBH):
                            eng.wait_ge(s_v, a + 1)
                            eng.wait_ge(s_ed, (a + 1) * SPLIT)
                            eng.wait_ge(s_ea, (a + 1) * ST)
                            need(eng, s_oc, a)
                            for kt in range(SPLIT):
                                for part in (PH, PL):
                                    eng.matmul(pO[0:VW, :], v[:, par, kt, :], part[:, par, kt, :],
                                               start=(kt == 0 and part is PH), stop=False)
                            for kt in range(SPLIT, ST):
                                ins = eng.matmul(pO[0:VW, :], v[:, par, kt, :].bitcast(F32), PW[:, par, kt - SPLIT, :],
                                                 start=False, stop=(kt == ST - 1))
                            ins.then_inc(s_o, 1)
                    steps(eng, step, NBH, behind=3)

                @block.vector
                def _(eng):
                    eng.memset(q[64:128, :, :].bitcast(F32), 0.0).then_inc(s_z, 1)
                    eng.memset(k[64:128, :, :].bitcast(F32), 0.0).then_inc(s_z, 1)
                    eng.wait_ge(s_z, 2)
                    eng.memset(q[64:65, :, :].bitcast(F32), 1.0).then_inc(s_c, 2)
                    eng.memset(k[64:65, :, :].bitcast(F32), k_aux).then_inc(s_c, 2)

                    def finish(b, part):
                        if not inside(b, NBH):
                            return
                        o = pB[:, 0:ST * VW].rearrange("p (t d) -> p t d", d=VW)
                        if part == 0:
                            eng.wait_ge(s_b, b + 1)
                            need(eng, s_n, b)
                            eng.tensor_copy(both[:], o[:, :, 0:DK]).then_inc(s_r, 1)
                        elif part == 1:
                            eng.wait_ge(s_r, b * 3 + 1)
                            eng.tensor_tensor(both[:], both[:], o[:, :, DK + 1:VW], ALU.add).then_inc(s_r, 1)
                        elif part == 2:
                            eng.reciprocal(rec[:], o[:, :, DK:DK + 1]).then_inc(s_r, 1)
                        else:
                            eng.wait_ge(s_r, b * 3 + 3)
                            eng.tensor_tensor(O[:, bass.ds(b, 1)].rearrange("p o t d -> p (o t) d"), both[:],
                                              rec[:].to_broadcast([P, ST, DK]), ALU.mult).then_inc(s_n, 1)

                    def maxima(at):
                        i, u, par = at.i, at.half, at.odd
                        if not inside(i, NBH):
                            return
                        if kind == "side":
                            eng.wait_ge(s_m, i + 1)
                        if kind == "mask":
                            eng.wait_ge(s_f[at.slot], (at.quarter + 1) * 16)
                        need(eng, s_t, (i - 1) * 4)
                        for qt in range(ST):
                            eng.wait_ge(s_s, i * 4 + qt + 1)
                            unfused(eng, s_spv, i)
                            eng.tensor_tensor_reduce(X[:, par, qt, :], pS[:, qt % 2, :],
                                                     self.zeros[:, 0:S] if kind == "self" else M[:, at.slot, qt, :], 1.0, LOWEST,
                                                     ALU.mult if kind == "mask" else ALU.add, ALU.max,
                                                     mx[:, par, qt:qt + 1]).then_inc(s_x, 1)
                        eng.wait_ge(s_x, (i + 1) * 4)
                        eng.tensor_scalar(nm[:, par, :], mx[:, par, :], -exp_scale, None, ALU.mult).then_inc(s_nm, 1)

                    def step(at):
                        i, u, par = at.i, at.half, at.odd
                        maxima(at)
                        t = i - 1
                        for kt in range(ST):
                            if kt < SPLIT and inside(t, NBH):
                                eng.wait_ge(s_ea, t * ST + kt + 1)
                                eng.tensor_tensor(PL[:, 1 - par, kt, :], pT[:, kt, :], PH[:, 1 - par, kt, :].bitcast(F32),
                                                  ALU.subtract).then_inc(s_ed, 1)
                            finish(i - 3, kt)
                    steps(eng, step, NBH, behind=3)

                @block.scalar
                def _(eng):
                    def step(at):
                        i, u, par = at.i, at.half, at.odd
                        t, a = i - 1, i - 2
                        if inside(t, NBH):
                            for kt in range(ST):
                                eng.wait_ge(s_t, t * 4 + kt + 1)
                                if kt == 0:
                                    need(eng, s_o, t - 1)
                                to = PH[:, 1 - par, kt, :] if kt < SPLIT else PW[:, 1 - par, kt - SPLIT, :]
                                eng.copy(to, pT[:, kt, :]).then_inc(s_ea, 1)
                        if inside(i, NBH):
                            for qt in range(ST):
                                if qt == 0:
                                    eng.wait_ge(s_nm, i + 1)
                                eng.activation(X[:, par, qt, :], X[:, par, qt, :], ACT.Exp,
                                               bias=nm[:, par, qt:qt + 1], scale=exp_scale).then_inc(s_p, 1)
                        if inside(a, NBH):
                            eng.wait_ge(s_o, a + 1)
                            need(eng, s_b, a)
                            eng.copy(OT[:], pO[0:VW, :]).then_inc(s_oc, 1)
                    steps(eng, step, NBH, behind=3)

    def output(self, O, wo, bo, base, dst):
        nc = self.nc
        with ExitStack() as ctx:
            w = self.sb("wo", [P, KD, D], ctx=ctx)
            brow = self.sb("bo", [P, D], ctx=ctx)
            OT = self.sb("oT", [P, 2, KD, S], ctx=ctx)
            nat = self.sb("nat", [P, 2, ST, D], ctx=ctx)
            bank = self.ps("tp", [P, 4, 512], ctx)
            py = self.ps("py", [P, 4, 512], ctx)
            s_w, s_g, s_tr, s_ev, s_y, s_a, s_b = (self.sem(n, ctx) for n in ("s_w", "s_g", "s_tr", "s_ev", "s_y", "s_a", "s_b"))
            with nc.Block() as block:
                @block.sync
                def _(eng):
                    eng.dma_start(w[:], wo.rearrange("(k p) n -> p k n", p=P)).then_inc(s_w, 16)
                    if bo is not None:
                        eng.dma_start(brow[:], bo.partition_broadcast(P)).then_inc(s_w, 16)

                @block.gpsimd
                def _(eng):
                    for b in range(B):
                        need(eng, s_tr, (b - 1) * KD)
                        eng.tensor_copy(nat[:, b % 2].rearrange("p t (h d) -> p t h d", d=DK),
                                        O[:, b * H:(b + 1) * H].rearrange("p h t d -> p t h d")).then_inc(s_g, 1)

                @block.tensor
                def _(eng):
                    eng.wait_ge(s_w, 16 if bo is None else 32)

                    def turn(b):
                        eng.wait_ge(s_g, b + 1)
                        for k in range(KD):
                            n = b * KD + k
                            need(eng, s_ev, n - 3)
                            for j in range(ST):
                                ins = eng.transpose(bank[:, n % 4, j * P:(j + 1) * P], nat[:, b % 2, j, k * P:(k + 1) * P],
                                                    self.ident[:])
                            ins.then_inc(s_tr, 1)

                    turn(0)
                    for b in range(B):
                        if b + 1 < B:
                            turn(b + 1)
                        eng.wait_ge(s_ev, (b + 1) * KD)
                        for j in range(ST):
                            n = b * ST + j
                            need(eng, s_a, n - 3)
                            for k in range(KD):
                                ins = eng.matmul(py[:, n % 4, 0:D], OT[:, b % 2, k, j * P:(j + 1) * P], w[:, k, :],
                                                 start=(k == 0), stop=(k == KD - 1))
                            ins.then_inc(s_y, 1)

                @block.scalar
                def _(eng):
                    for n in range(B * KD):
                        b, k = divmod(n, KD)
                        eng.wait_ge(s_tr, n + 1)
                        need(eng, s_y, (b - 1) * ST)
                        eng.copy(OT[:, b % 2, k, :], bank[:, n % 4, :]).then_inc(s_ev, 1)

                @block.vector
                def _(eng):
                    if bo is not None:
                        eng.wait_ge(s_w, 32)
                        for b in range(B):
                            rows = slice(b * ST, (b + 1) * ST)
                            eng.tensor_tensor(dst[:, rows, :], base[:, rows, :], brow[:].unsqueeze(1).to_broadcast([P, ST, D]),
                                              ALU.add).then_inc(s_b, 1)
                        eng.wait_ge(s_b, B)
                    src = base if bo is None else dst
                    for n in range(NT):
                        eng.wait_ge(s_y, n + 1)
                        eng.tensor_tensor(dst[:, n, :], src[:, n, :], py[:, n % 4, 0:D], ALU.add).then_inc(s_a, 1)

    def load_context(self, cT):
        nc = self.nc
        s_c = self.sem("s_ctx")
        with nc.Block() as block:
            @block.sync
            def _(eng):
                for k in range(KD):
                    eng.dma_start(cT[:, k, :], self.t["ctx_1024"][k * P:(k + 1) * P, :]).then_inc(s_c, 16)
                eng.wait_ge(s_c, 16 * KD)

    def prepare_mask(self, mask):
        nc = self.nc
        with ExitStack() as ctx:
            raw = self.sb("raw", [P, 2, ST, S], I32, ctx=ctx)
            s_d = [self.sem("s_d", ctx) for _ in range(2)]
            bits = self.sb("bits", [P, 2, ST, S], BF16, ctx=ctx)
            s_m = self.sem("s_m", ctx)
            s_st = [self.sem("s_st", ctx) for _ in range(2)]
            with nc.Block() as block:
                def put(eng, b):
                    eng.wait_ge(s_m, b + 1)
                    eng.dma_start(mask[b], bits[:, b % 2]).then_inc(s_st[b % 2], 16)

                @block.sync
                def _(eng):
                    for b in range(B):
                        need(eng, s_m, b - 1)
                        eng.dma_start(raw[:, b % 2], self.t["mask_Bx1xSxS2_ik1"][b, 0].rearrange("(t p) k -> p t k", p=P))\
                           .then_inc(s_d[b % 2], 16)
                        if b:
                            put(eng, b - 1)
                    put(eng, B - 1)
                    for s in s_st:
                        eng.wait_ge(s, 16 * B // 2)

                @block.vector
                def _(eng):
                    for b in range(B):
                        eng.wait_ge(s_d[b % 2], 16 * (b // 2 + 1))
                        need(eng, s_st[b % 2], 16 * (b // 2))
                        eng.tensor_scalar(bits[:, b % 2], raw[:, b % 2], 0, None, ALU.not_equal).then_inc(s_m, 1)

    def store(self, x):
        nc = self.nc
        s_o = self.sem("s_out")
        with nc.Block() as block:
            @block.sync
            def _(eng):
                eng.dma_start(self.out.rearrange("b (t p) d -> p (b t) d", p=P), x[:]).then_inc(s_o, 16)
                eng.wait_ge(s_o, 16)

    def prepare_common(self, common):
        nc = self.nc
        with ExitStack() as ctx:
            am = self.sb("am", [P, ST, S], ctx=ctx)
            pad = self.sb("pad", [P, B, S], mybir.dt.uint8, ctx=ctx)
            low = self.sb("low", [P, B, S], ctx=ctx)
            s_d, s_l = self.sem("s_d", ctx), self.sem("s_l", ctx)
            with nc.Block() as block:
                @block.sync
                def _(eng):
                    eng.dma_start(am[:], self.t["fside_SxS2_0"].rearrange("(t p) k -> p t k", p=P)).then_inc(s_d, 16)
                    eng.dma_start(pad[:], self.t["mask_BxS2_bf0"].partition_broadcast(P)).then_inc(s_d, 16)

                @block.vector
                def _(eng):
                    eng.wait_ge(s_d, 32)
                    eng.tensor_scalar(low[:], pad[:], -3.0e38, 10.0, ALU.mult, ALU.mult).then_inc(s_l, 1)
                    eng.wait_ge(s_l, 1)
                    for b in range(B):
                        eng.scalar_tensor_tensor(out=common[:, b], in0=am[:], scalar=0.5,
                                                 in1=low[:, b].unsqueeze(1).to_broadcast([P, ST, S]), op0=ALU.mult, op1=ALU.add)

    def route_top1(self, src, xx, gain, shift, slot, tile_expert, XS):
        nc, t = self.nc, self.t
        with ExitStack() as ctx:
            grow, brow, rw = (self.sb(n, [P, D], ctx=ctx) for n in ("grow", "brow", "rw"))
            rb = self.sb("rb", [P, 1], ctx=ctx)
            junk = self.sb("junk", [P, D], ctx=ctx)
            key, kf, gt = (self.sb(n, [P, NT], ctx=ctx) for n in ("key", "kf", "gt"))
            ki = self.sb("ki", [P, NT], I32, ctx=ctx)
            oh = self.sb("oh", [P, E0, NT], ctx=ctx)
            ohb = self.sb("ohb", [P, E0, NT], BF16, ctx=ctx)
            tri = self.sb("tri", [P, P], BF16, ctx=ctx)
            ones = self.sb("ones", [P, P], BF16, ctx=ctx)
            tot, incl, w = (self.sb(n, [P, E0, NT], ctx=ctx) for n in ("tot", "incl", "w"))
            cnt, ends, base = (self.sb(n, [P, E0], ctx=ctx) for n in ("cnt", "ends", "base"))
            ci = self.sb("ci", [P, E0], I32, ctx=ctx)
            slotf = self.sb("slotf", [P, NT], ctx=ctx)
            starts = self.sb("starts", [P, L0_TILES], ctx=ctx)
            te = self.sb("te", [P, 3, L0_TILES], ctx=ctx)
            ps = self.ps("rt", [P, 2, 512], ctx)
            names = ("s_w", "s_ch", "s_mv", "s_rs", "s_z", "s_c", "s_oh", "s_p", "s_ix", "s_zero", "s_sc")
            s_w, s_ch, s_mv, s_rs, s_z, s_c, s_oh, s_p, s_ix, s_zero, s_sc = (self.sem(n, ctx) for n in names)
            s_ch2 = self.sem("s_ch2", ctx)
            with nc.Block() as block:
                @block.sync
                def _(eng):
                    for dst, srcd in ((grow, gain), (brow, shift), (rb, t["L0_ffn_router_b"])):
                        eng.dma_start(dst[:], srcd.partition_broadcast(P)).then_inc(s_w, 16)
                    eng.dma_start(rw[:], t["L0_ffn_router_w"].rearrange("d o -> (d o)").partition_broadcast(P)).then_inc(s_w, 16)
                    eng.dma_start(XS.rearrange("(p r) d -> p (r d)", p=P)[:, :], self.zero_rows(L0_SLOTS // P)).then_inc(s_zero, 16)

                @block.vector
                def _(eng):
                    eng.wait_ge(s_w, 64)
                rs = self.normalise(block, s_ch, s_mv, s_rs, s_z, xx, src, ctx, gain=grow, shift=brow)

                @block.scalar
                def _(eng):
                    self.deviations(eng, s_mv, s_rs, rs)

                @block.vector
                def _(eng):
                    do = Chain(eng, s_ch2)

                    def then(ins):
                        do(ins)
                        do.wait()

                    eng.wait_ge(s_z, B)
                    for n in range(NT):
                        then(eng.tensor_tensor_reduce(junk[:], xx[:, n, :], rw[:], 1.0, 0.0, ALU.mult, ALU.add, key[:, n:n + 1]))
                    then(eng.tensor_scalar(key[:], key[:], rb[:, 0:1], None, ALU.add))
                    then(eng.tensor_copy(ki[:], key[:]))
                    then(eng.tensor_copy(kf[:], ki[:]))
                    then(eng.tensor_tensor(gt[:], kf[:], key[:], ALU.is_gt))
                    then(eng.tensor_tensor(kf[:], kf[:], gt[:], ALU.subtract))
                    then(eng.tensor_copy(ki[:], kf[:]))
                    then(eng.tensor_scalar(ki[:], ki[:], E0 - 1, None, ALU.bitwise_and))
                    then(eng.tensor_copy(kf[:], ki[:]))
                    for e in range(E0):
                        do(eng.tensor_scalar(oh[:, e, :], kf[:], float(e), None, ALU.is_equal))
                    do.wait()
                    do(eng.tensor_copy(ohb[:], oh[:]))
                    do.wait()
                    eng.sem_inc(s_oh, 1)
                    eng.wait_ge(s_p, 1)
                    then(eng.tensor_copy(tot[:].rearrange("p e n -> p (e n)"), ps[:, 1, 0:E0 * NT]))
                    then(eng.tensor_reduce(cnt[:], tot[:], AX, ALU.add))
                    then(eng.tensor_scalar(cnt[:], cnt[:], float(P - 1), None, ALU.add))
                    then(eng.tensor_copy(ci[:], cnt[:]))
                    then(eng.tensor_scalar(ci[:], ci[:], 7, 7, ALU.logical_shift_right, ALU.logical_shift_left))
                    then(eng.tensor_copy(cnt[:], ci[:]))
                    then(eng.tensor_tensor_scan(ends[:], cnt[:], self.zeros[:, 0:E0], 0.0, ALU.add, ALU.add))
                    then(eng.tensor_tensor(base[:], ends[:], cnt[:], ALU.subtract))
                    for e in range(E0):
                        do(eng.tensor_tensor_scan(incl[:, e, :], tot[:, e, :], self.zeros[:, 0:NT], base[:, e:e + 1], ALU.add, ALU.add))
                    do.wait()
                    then(eng.tensor_tensor(incl[:], incl[:], tot[:], ALU.subtract))
                    then(eng.tensor_tensor(w[:].rearrange("p e n -> p (e n)"), incl[:].rearrange("p e n -> p (e n)"),
                                           ps[:, 0, 0:E0 * NT], ALU.add))
                    then(eng.tensor_tensor(w[:], w[:], oh[:], ALU.mult))
                    then(eng.tensor_reduce(slotf[:], w[:].rearrange("p e n -> p n e"), AX, ALU.add))
                    do(eng.tensor_copy(slot[:], slotf[:]))
                    eng.wait_ge(s_c, 5)
                    for e in range(E0 - 1):
                        do(eng.tensor_scalar(te[:, e, :], starts[:], ends[:, e:e + 1], None, ALU.is_ge))
                    do.wait()
                    then(eng.tensor_tensor(te[:, 0, :], te[:, 0, :], te[:, 1, :], ALU.add))
                    then(eng.tensor_tensor(te[:, 0, :], te[:, 0, :], te[:, 2, :], ALU.add))
                    do(eng.tensor_copy(tile_expert[:], te[:, 0, :]))
                    do.wait()
                    eng.sem_inc(s_ix, 1)

                @block.tensor
                def _(eng):
                    eng.wait_ge(s_c, 5)
                    eng.wait_ge(s_oh, 1)
                    rhs = ohb[:].rearrange("p e n -> p (e n)")
                    eng.matmul(ps[:, 0, 0:E0 * NT], tri[:], rhs, start=True, stop=True)
                    eng.matmul(ps[:, 1, 0:E0 * NT], ones[:], rhs, start=True, stop=True).then_inc(s_p, 1)

                @block.gpsimd
                def _(eng):
                    eng.memset(tri[:], 0.0).then_inc(s_c, 1)
                    eng.memset(ones[:], 1.0).then_inc(s_c, 1)
                    eng.wait_ge(s_c, 2)
                    eng.affine_select(out=tri[:], in_=tri[:], compare_op=ALU.is_ge, fill=1.0, base=0,
                                      pattern=[[-1, P]], channel_multiplier=1).then_inc(s_c, 1)
                    eng.iota(starts[:], pattern=[[P, L0_TILES]], base=0, channel_multiplier=0,
                             allow_small_or_imprecise_dtypes=True).then_inc(s_c, 2)
                    eng.wait_ge(s_ix, 1)
                    eng.wait_ge(s_zero, 16)
                    for n in range(NT):
                        eng.indirect_dma_start(out=XS, out_offset=bass.IndirectOffsetOnAxis(ap=slot[:, n:n + 1], axis=0),
                                               in_=xx[:, n, :], in_offset=None).then_inc(s_sc, 16)
                    eng.wait_ge(s_sc, 16 * NT)

    def zero_rows(self, rows):
        return self.zeros[:, 0:D].unsqueeze(1).to_broadcast([P, rows, D])

    def top1_tiles(self, tile_expert, XS, YS):
        nc, t = self.nc, self.t
        MF = FF0 // P
        with ExitStack() as ctx:
            w1 = self.sb("w1", [P, 4, KD, FF0], ctx=ctx)
            w2 = self.sb("w2", [P, 4, MF, D], ctx=ctx)
            b1 = self.sb("b1", [P, 4, MF], ctx=ctx)
            b2 = self.sb("b2", [P, 4, D], ctx=ctx)
            xs = self.sb("xs", [P, 4, D], ctx=ctx)
            xT = self.sb("xT", [P, 2, KD, P], ctx=ctx)
            hT = self.sb("hT", [P, 2, MF, P], ctx=ctx)
            ys = self.sb("ys", [P, 2, D], ctx=ctx)
            px = self.ps("px", [P, 2, 512], ctx)
            ph = self.ps("ph", [P, 4, 512], ctx)
            py = self.ps("py", [P, 2, 512], ctx)
            s_x, s_xt, s_h, s_hv, s_ha, s_y, s_yb = (self.sem(n, ctx) for n in ("s_x", "s_xt", "s_h", "s_hv", "s_ha", "s_y", "s_yb"))
            s_w = [self.sem("s_w", ctx) for _ in range(4)]
            s_st = [self.sem("s_st", ctx) for _ in range(2)]
            LOADS = 5 * 16
            with nc.Block() as block:
                @block.sync
                def _(eng):
                    def step(at):
                        i, u, par = at.i, at.half, at.odd
                        if inside(i, L0_TILES):
                            need(eng, s_y, i - 3)
                            need(eng, s_yb, i - 3)
                            e = eng.value_load(tile_expert[0:1, bass.ds(i, 1)], min_val=0, max_val=E0 - 1)
                            one = bass.ds(e, 1)
                            eng.dma_start(xs[:, at.slot, :], XS[bass.ds(i * P, P), :]).then_inc(s_w[at.slot], 16)
                            eng.dma_start(w1[:, at.slot], t["L0_ffn_W1"][one].rearrange("o (k p) f -> p (o k) f", p=P)).then_inc(s_w[at.slot], 16)
                            eng.dma_start(b1[:, at.slot], t["L0_ffn_b1"][one].rearrange("o p m -> (o p) m")).then_inc(s_w[at.slot], 16)
                            eng.dma_start(b2[:, at.slot], t["L0_ffn_b2"][one].rearrange("o d -> (o d)").partition_broadcast(P)).then_inc(s_w[at.slot], 16)
                            eng.dma_start(w2[:, at.slot], t["L0_ffn_W2"][one].rearrange("o (m p) d -> p (o m) d", p=P)).then_inc(s_w[at.slot], 16)
                    steps(eng, step, L0_TILES, behind=0)

                @block.scalar
                def _(eng):
                    def step(at):
                        i, par = at.i, at.odd
                        if inside(i, L0_TILES):
                            eng.wait_ge(s_x, i + 1)
                            need(eng, s_h, (i - 1) * 2)
                            eng.copy(xT[:, par].rearrange("p k n -> p (k n)"), px[:, par, 0:KD * P]).then_inc(s_xt, 1)
                            eng.wait_ge(s_h, i * 2 + 1)
                            need(eng, s_y, i - 1)
                            for m in range(MF // 2):
                                ins = eng.activation(hT[:, par, m, :], ph[:, par * 2, m * P:(m + 1) * P], ACT.Relu, bias=b1[:, at.slot, m:m + 1])
                            ins.then_inc(s_ha, 1)
                        a = i - 1
                        if inside(a, L0_TILES):
                            eng.wait_ge(s_yb, a + 1)
                            eng.dma_start(YS[bass.ds(a * P, P), :], ys[:, 1 - par, :]).then_inc(s_st[1 - par], 16)
                    steps(eng, step, L0_TILES, behind=1)
                    for s in s_st:
                        eng.wait_ge(s, 16 * L0_TILES // 2)

                @block.vector
                def _(eng):
                    def step(at):
                        i, par = at.i, at.odd
                        a = i - 1
                        if inside(a, L0_TILES):
                            eng.wait_ge(s_y, a + 1)
                            if not isinstance(a, int) or a >= 2:
                                eng.wait_ge(s_st[1 - par], (at.half if par else at.half - 1) * 16)
                            eng.tensor_tensor(ys[:, 1 - par, :], py[:, 1 - par, 0:D], b2[:, (at.slot - 1) % 4, :], ALU.add).then_inc(s_yb, 1)
                        if inside(i, L0_TILES):
                            eng.wait_ge(s_h, i * 2 + 2)
                            need(eng, s_y, i - 1)
                            for m in range(MF // 2, MF):
                                q = m - MF // 2
                                ins = eng.tensor_scalar(hT[:, par, m, :], ph[:, par * 2 + 1, q * P:(q + 1) * P], b1[:, at.slot, m:m + 1], 0.0,
                                                        ALU.add, ALU.max)
                            ins.then_inc(s_hv, 1)
                    steps(eng, step, L0_TILES, behind=1)

                @block.tensor
                def _(eng):
                    def up(at, half):
                        i, par = at.i, at.odd
                        need(eng, (s_ha, s_hv)[half], i - 1)
                        for m in range(MF // 2):
                            f = (half * (MF // 2) + m) * P
                            for k in range(KD):
                                ins = eng.matmul(ph[:, par * 2 + half, m * P:(m + 1) * P], w1[:, at.slot, k, f:f + P], xT[:, par, k, :],
                                                 start=(k == 0), stop=(k == KD - 1))
                        ins.then_inc(s_h, 1)

                    def step(at):
                        i, par = at.i, at.odd
                        if inside(i, L0_TILES):
                            eng.wait_ge(s_w[at.slot], (at.quarter + 1) * LOADS)
                            need(eng, s_xt, i - 1)
                            for k in range(KD):
                                ins = eng.transpose(px[:, par, k * P:(k + 1) * P], xs[:, at.slot, k * P:(k + 1) * P], self.ident[:])
                            ins.then_inc(s_x, 1)
                            eng.wait_ge(s_xt, i + 1)
                            up(at, 0)
                        a = i - 1
                        if inside(a, L0_TILES):
                            need(eng, s_yb, a - 1)
                            for m in range(MF):
                                if m % (MF // 2) == 0:
                                    eng.wait_ge((s_ha, s_hv)[m // (MF // 2)], a + 1)
                                ins = eng.matmul(py[:, 1 - par, 0:D], hT[:, 1 - par, m, :], w2[:, (at.slot - 1) % 4, m, :],
                                                 start=(m == 0), stop=(m == MF - 1))
                            ins.then_inc(s_y, 1)
                        if inside(i, L0_TILES):
                            up(at, 1)
                    steps(eng, step, L0_TILES, behind=1)

    def combine_top1(self, xx, slot, YS, gain, shift, x):
        nc = self.nc
        with ExitStack() as ctx:
            grow, brow = (self.sb(n, [P, D], ctx=ctx) for n in ("grow", "brow"))
            y = self.sb("y", [P, NT, D], ctx=ctx)
            s_w, s_g, s_ch, s_mv, s_rs, s_z, s_ch2 = (self.sem(n, ctx) for n in ("s_w", "s_g", "s_ch", "s_mv", "s_rs", "s_z", "s_ch2"))
            with nc.Block() as block:
                @block.sync
                def _(eng):
                    eng.dma_start(grow[:], gain.partition_broadcast(P)).then_inc(s_w, 16)
                    eng.dma_start(brow[:], shift.partition_broadcast(P)).then_inc(s_w, 16)

                @block.gpsimd
                def _(eng):
                    for n in range(NT):
                        eng.indirect_dma_start(out=y[:, n, :], out_offset=None, in_=YS,
                                               in_offset=bass.IndirectOffsetOnAxis(ap=slot[:, n:n + 1], axis=0)).then_inc(s_g, 16)

                @block.vector
                def _(eng):
                    do = Chain(eng, s_ch2)
                    eng.wait_ge(s_w, 32)
                    eng.wait_ge(s_g, 16 * NT)
                    do(eng.tensor_tensor(y[:], y[:], xx[:], ALU.add))
                    do.wait()
                rs = self.normalise(block, s_ch, s_mv, s_rs, s_z, y, y, ctx, gain=grow, shift=brow)

                @block.scalar
                def _(eng):
                    self.deviations(eng, s_mv, s_rs, rs)

                @block.vector
                def _(eng):
                    eng.wait_ge(s_z, B)
                    eng.tensor_tensor(x[:], x[:], y[:], ALU.add)

    def route_and_share(self, zT, w_k, oh, scatter, gather, XS, YS, common_out):
        with ExitStack() as ctx:
            lgT, asT = (self.sb(n, [E1, N], ctx=ctx) for n in ("lgT", "asT"))
            pt = self.ps("pt", [P, 2, 512], ctx)
            with self.nc.Block() as block:
                choose, turn = self.top2_gate(block, ctx, pt, zT, w_k, oh, lgT, asT)
                shared = self.shared(block, ctx, zT, common_out, XS, YS)
                positions = self.top2_capacity(block, ctx, pt, lgT, asT, oh, scatter, gather)

                @block.tensor
                def _(eng):
                    choose(eng)
                    shared(eng, range(0, 1))
                    turn(eng)
                    shared(eng, range(1, B))
                    positions(eng)

    def top2_gate(self, block, ctx, pt, zT, w_k, oh, lgT, asT):
        nc, t = self.nc, self.t
        G = [P, NT, E1]
        gw = self.sb("gw", [P, KD, E1], ctx=ctx)
        gb = self.sb("gb", [P, E1], ctx=ctx)
        rev = self.sb("rev", [P, E1], ctx=ctx)
        lg, sc, tmp = (self.sb(n, G, ctx=ctx) for n in ("lg", "sc", "tmp"))
        m = self.sb("m", [P, NT], ctx=ctx)
        s_w, s_c, s_l, s_ch, s_d, s_e, s_as, s_t, s_tc = (self.sem(n, ctx) for n in
                                                         ("s_w", "s_c", "s_l", "s_ch", "s_d", "s_e", "s_as", "s_t", "s_tc"))

        def per_token(a):
            return a[:].unsqueeze(2).to_broadcast(G)

        def per_expert(a):
            return a[:].unsqueeze(1).to_broadcast(G)

        @block.sync
        def _(eng):
            eng.dma_start(gw[:], t["L1_ffn_gate_w"].rearrange("(k p) e -> p k e", p=P)).then_inc(s_w, 16)
            eng.dma_start(gb[:], t["L1_ffn_gate_b"].partition_broadcast(P)).then_inc(s_w, 16)

        @block.gpsimd
        def _(eng):
            eng.iota(rev[:], pattern=[[-1, E1]], base=E1, channel_multiplier=0,
                     allow_small_or_imprecise_dtypes=True).then_inc(s_c, 1)

        def choose(eng):
            eng.wait_ge(s_w, 32)
            for n in range(NT):
                for k in range(KD):
                    ins = eng.matmul(pt[:, 0, n * E1:(n + 1) * E1], zT[:, k, n * P:(n + 1) * P], gw[:, k, :],
                                     start=(k == 0), stop=(k == KD - 1))
            ins.then_inc(s_l, 1)

        def turn(eng):
            eng.wait_ge(s_as, 1)
            for x, src in enumerate((lg, sc)):
                for c in range(4):
                    need(eng, s_tc, x * 4 + c - 1)
                    for j in range(ST):
                        ins = eng.transpose(pt[0:E1, c % 2, j * P:(j + 1) * P], src[:, c * ST + j, :], self.ident[:])
                    ins.then_inc(s_t, 1)

        @block.scalar
        def _(eng):
            eng.wait_ge(s_d, 1)
            eng.activation(sc[:], tmp[:], ACT.Exp).then_inc(s_e, 1)

        @block.vector
        def _(eng):
            do = Chain(eng, s_ch)

            def then(ins):
                do(ins)
                do.wait()

            eng.wait_ge(s_w, 32)
            eng.wait_ge(s_c, 1)
            eng.wait_ge(s_l, 1)
            then(eng.tensor_copy(lg[:].rearrange("p n e -> p (n e)"), pt[:, 0, 0:NT * E1]))
            then(eng.tensor_reduce(m[:], lg[:], AX, ALU.max))
            eng.tensor_tensor(tmp[:], lg[:], per_token(m), ALU.subtract).then_inc(s_d, 1)
            eng.wait_ge(s_e, 1)
            then(eng.tensor_reduce(m[:], sc[:], AX, ALU.add))
            then(eng.reciprocal(m[:], m[:]))
            then(eng.tensor_tensor(sc[:], sc[:], per_token(m), ALU.mult))
            then(eng.tensor_tensor(sc[:], sc[:], per_expert(gb), ALU.add))
            for k in range(TOPK):
                then(eng.tensor_reduce(m[:], sc[:], AX, ALU.max))
                then(eng.tensor_tensor(tmp[:], sc[:], per_token(m), ALU.is_equal))
                then(eng.tensor_tensor(tmp[:], tmp[:], per_expert(rev), ALU.mult))
                then(eng.tensor_reduce(m[:], tmp[:], AX, ALU.max))
                then(eng.tensor_tensor(oh[:, k], per_expert(rev), per_token(m), ALU.is_equal))
                then(eng.tensor_tensor(tmp[:], oh[:, k], lg[:], ALU.mult))
                then(eng.tensor_reduce(w_k[:, k, :], tmp[:], AX, ALU.add))
                if k + 1 < TOPK:
                    then(eng.scalar_tensor_tensor(out=sc[:], in0=oh[:, k], scalar=LOWEST, in1=sc[:], op0=ALU.mult, op1=ALU.add))
            then(eng.tensor_tensor(sc[:], oh[:, 0], oh[:, 1], ALU.add))
            eng.sem_inc(s_as, 1)
            for x, dst in enumerate((lgT, asT)):
                for c in range(4):
                    eng.wait_ge(s_t, x * 4 + c + 1)
                    eng.tensor_copy(dst[:, c * 512:(c + 1) * 512], pt[0:E1, c % 2, :]).then_inc(s_tc, 1)
            eng.wait_ge(s_tc, 8)

        return choose, turn

    def top2_capacity(self, block, ctx, pt, lgT, asT, oh, scatter, gather):
        nc = self.nc
        R = [E1, N]
        G = [P, NT, E1]
        flip = self.sb("flip", R, I32, ctx=ctx)
        hi, lo, t0, t1 = (self.sb(n, R, ctx=ctx) for n in ("hi", "lo", "t0", "t1"))
        thr, cand, bit, cnt, want, gain, first = (self.sb(n, [E1, 1], ctx=ctx) for n in
                                                  ("thr", "cand", "bit", "cnt", "want", "gain", "first"))
        own = self.sb("own", [P, TOPK, NT], ctx=ctx)
        pos, kept, tmp = (self.sb(n, G, ctx=ctx) for n in ("pos", "kept", "tmp"))
        pk, kk, idx = (self.sb(n, [P, TOPK, NT], ctx=ctx) for n in ("pk", "kk", "idx"))
        s_c, s_ch, s_k, s_t = (self.sem(n, ctx) for n in ("s_c", "s_ch", "s_k", "s_t"))
        @block.gpsimd
        def _(eng):
            eng.iota(own[:], pattern=[[N, TOPK], [P, NT]], base=DROP_ROW, channel_multiplier=1,
                     allow_small_or_imprecise_dtypes=True).then_inc(s_c, 1)
            eng.iota(first[:], pattern=[[0, 1]], base=-1, channel_multiplier=CAP,
                     allow_small_or_imprecise_dtypes=True).then_inc(s_c, 1)

        def positions(eng):
            eng.wait_ge(s_k, 1)
            for x, src in enumerate((t1, t0)):
                for n in range(NT):
                    ins = eng.transpose(pt[:, x, n * E1:(n + 1) * E1], src[:, n * P:(n + 1) * P], self.ident[0:E1, 0:E1])
            ins.then_inc(s_t, 1)

        @block.vector
        def _(eng):
            do = Chain(eng, s_ch)

            def then(ins):
                do(ins)
                do.wait()

            def count(src, than, op):
                then(eng.tensor_scalar(t0[:], src[:], than, 0.0, op, ALU.add, accum_out=cnt[:]))

            def search(src):
                then(eng.memset(cand[:], 32768.0))
                then(eng.memset(bit[:], 32768.0))
                with eng.Fori(0, 16) as i:
                    do.enter(i, 4)
                    count(src, cand[:, 0:1], ALU.is_ge)
                    then(eng.tensor_scalar(gain[:], cnt[:], want[:, 0:1], 0.5, ALU.is_ge, ALU.subtract))
                    then(eng.scalar_tensor_tensor(out=cand[:], in0=gain[:], scalar=bit[:, 0:1], in1=cand[:], op0=ALU.mult, op1=ALU.add))
                    do(eng.tensor_scalar(bit[:], bit[:], 0.5, None, ALU.mult))
                    do.leave(16)
                do.wait()
                then(eng.tensor_scalar(thr[:], cand[:], -0.5, None, ALU.add))

            bits = lgT[:].bitcast(I32)
            then(eng.tensor_scalar(flip[:], bits, 31, None, ALU.arith_shift_right))
            then(eng.tensor_scalar(flip[:], flip[:], -2147483648, None, ALU.bitwise_or))
            then(eng.tensor_tensor(flip[:], flip[:], bits, ALU.bitwise_xor))
            then(eng.tensor_scalar(t0[:].bitcast(I32), flip[:], 16, 0xffff, ALU.logical_shift_right, ALU.bitwise_and))
            then(eng.tensor_copy(hi[:], t0[:].bitcast(I32)))
            then(eng.tensor_scalar(t1[:].bitcast(I32), flip[:], 0xffff, None, ALU.bitwise_and))
            then(eng.tensor_copy(lo[:], t1[:].bitcast(I32)))
            then(eng.scalar_tensor_tensor(out=hi[:], in0=hi[:], scalar=1.0, in1=asT[:], op0=ALU.add, op1=ALU.mult))
            then(eng.tensor_scalar(hi[:], hi[:], -1.0, None, ALU.add))
            then(eng.memset(want[:], float(CAP)))
            search(hi)
            count(hi, thr[:, 0:1], ALU.is_gt)
            then(eng.tensor_tensor(want[:], want[:], cnt[:], ALU.subtract))
            then(eng.tensor_scalar(t1[:], hi[:], thr[:, 0:1], None, ALU.is_equal))
            then(eng.scalar_tensor_tensor(out=lo[:], in0=lo[:], scalar=1.0, in1=t1[:], op0=ALU.add, op1=ALU.mult))
            then(eng.tensor_scalar(lo[:], lo[:], -1.0, None, ALU.add))
            then(eng.tensor_copy(hi[:], t0[:]))
            search(lo)
            count(lo, thr[:, 0:1], ALU.is_gt)
            then(eng.tensor_tensor(want[:], want[:], cnt[:], ALU.subtract))
            then(eng.tensor_tensor(hi[:], hi[:], t0[:], ALU.add))
            then(eng.tensor_scalar(lo[:], lo[:], thr[:, 0:1], None, ALU.is_equal))
            zeros = self.zeros[0:E1, 0:N]
            then(eng.tensor_tensor_scan(t1[:], lo[:], zeros, 0.0, ALU.add, ALU.add))
            then(eng.tensor_scalar(t1[:], t1[:], want[:, 0:1], None, ALU.is_le))
            then(eng.tensor_tensor(t1[:], t1[:], lo[:], ALU.mult))
            then(eng.tensor_tensor(t0[:], hi[:], t1[:], ALU.add))
            eng.wait_ge(s_c, 2)
            then(eng.tensor_tensor_scan(t1[:], t0[:], zeros, first[:, 0:1], ALU.add, ALU.add))
            eng.sem_inc(s_k, 1)
            eng.wait_ge(s_t, 1)
            then(eng.tensor_copy(pos[:].rearrange("p n e -> p (n e)"), pt[:, 0, 0:NT * E1]))
            then(eng.tensor_copy(kept[:].rearrange("p n e -> p (n e)"), pt[:, 1, 0:NT * E1]))
            for k in range(TOPK):
                then(eng.tensor_tensor(tmp[:], oh[:, k], pos[:], ALU.mult))
                then(eng.tensor_reduce(pk[:, k, :], tmp[:], AX, ALU.add))
                then(eng.tensor_tensor(tmp[:], oh[:, k], kept[:], ALU.mult))
                then(eng.tensor_reduce(kk[:, k, :], tmp[:], AX, ALU.add))
            then(eng.tensor_tensor(idx[:], pk[:], own[:], ALU.subtract))
            then(eng.tensor_tensor(idx[:], idx[:], kk[:], ALU.mult))
            then(eng.tensor_tensor(idx[:], idx[:], own[:], ALU.add))
            then(eng.tensor_copy(scatter[:], idx[:]))
            then(eng.tensor_scalar(idx[:], pk[:], float(-ZERO_ROW), None, ALU.add))
            then(eng.tensor_tensor(idx[:], idx[:], kk[:], ALU.mult))
            then(eng.tensor_scalar(idx[:], idx[:], float(ZERO_ROW), None, ALU.add))
            then(eng.tensor_copy(gather[:], idx[:]))

        return positions

    def dispatch(self, z, scatter, XS, YS):
        nc = self.nc
        with ExitStack() as ctx:
            s_s = self.sem("s_s", ctx)
            with nc.Block() as block:
                @block.gpsimd
                def _(eng):
                    for n in range(NT):
                        for k in range(TOPK):
                            eng.indirect_dma_start(out=XS, out_offset=bass.IndirectOffsetOnAxis(ap=scatter[:, k, n:n + 1], axis=0),
                                                   in_=z[:, n, :], in_offset=None).then_inc(s_s, 16)
                    eng.wait_ge(s_s, 16 * NT * TOPK)

    def shared(self, block, ctx, zT, out, XS, YS):
        t = self.t
        MF = FSH // P
        w1, w3 = (self.sb(n, [P, KD, FSH], ctx=ctx) for n in ("w1", "w3"))
        w2 = self.sb("w2", [P, MF, D], ctx=ctx)
        act, p3c = (self.sb(n, [P, 2, S], ctx=ctx) for n in ("act", "p3c"))
        g = self.sb("g", [P, 2, MF, S], ctx=ctx)
        p1, p3, py = (self.ps(n, [P, 2, 512], ctx) for n in ("p1", "p3", "py"))
        s_w, s_h, s_a, s_g, s_y, s_x, s_zero = (self.sem(n, ctx) for n in ("s_w", "s_h", "s_a", "s_g", "s_y", "s_x", "s_zero"))

        @block.sync
        def _(eng):
            for w, src in ((w1, t["L1_ffn_sw1"]), (w3, t["L1_ffn_sw3"])):
                for k in range(KD):
                    eng.dma_start(w[:, k].rearrange("p (s f) -> p s f", s=NSH),
                                  src[:, k * P:(k + 1) * P, :].rearrange("s p f -> p s f")).then_inc(s_w, 16)
            eng.dma_start(w2[:], t["L1_ffn_sw2"].rearrange("s (m p) d -> p (s m) d", p=P)).then_inc(s_w, 16)
            eng.dma_start(XS[0:L1_SLOTS].rearrange("(p r) d -> p r d", p=P), self.zero_rows(L1_SLOTS // P)).then_inc(s_zero, 16)
            eng.dma_start(YS[ZERO_ROW:ZERO_ROW + P], self.zeros[:, 0:D]).then_inc(s_zero, 16)
            eng.wait_ge(s_zero, 32)

        def down(eng, c):
            for j in range(ST):
                n = c * ST + j
                if j == 0:
                    eng.wait_ge(s_g, (c + 1) * MF)
                need(eng, s_x, n - 1)
                for m in range(MF):
                    ins = eng.matmul(py[:, n % 2, 0:D], g[:, c % 2, m, j * P:(j + 1) * P], w2[:, m, :],
                                     start=(m == 0), stop=(m == MF - 1))
                ins.then_inc(s_y, 1)

        def tensor(eng, batches):
            for c in batches:
                if c == 0:
                    eng.wait_ge(s_w, 80)
                for m in range(MF):
                    q = c * MF + m
                    need(eng, s_a, (q - 1) * 2)
                    for w, bank in ((w1, p1), (w3, p3)):
                        for k in range(KD):
                            ins = eng.matmul(bank[:, q % 2, :], w[:, k, m * P:(m + 1) * P], zT[:, k, c * S:(c + 1) * S],
                                             start=(k == 0), stop=(k == KD - 1))
                    ins.then_inc(s_h, 1)
                if c:
                    down(eng, c - 1)
                if c == B - 1:
                    down(eng, c)

        @block.scalar
        def _(eng):
            def take(c):
                for j in range(ST):
                    n = c * ST + j
                    eng.wait_ge(s_y, n + 1)
                    eng.copy(out[:, n, :], py[:, n % 2, 0:D]).then_inc(s_x, 1)

            for c in range(B):
                for m in range(MF):
                    q = c * MF + m
                    eng.wait_ge(s_h, q + 1)
                    need(eng, s_g, q - 1)
                    eng.activation(act[:, q % 2, :], p1[:, q % 2, :], ACT.Silu).then_inc(s_a, 1)
                    eng.copy(p3c[:, q % 2, :], p3[:, q % 2, :]).then_inc(s_a, 1)
                if c:
                    take(c - 1)
            take(B - 1)

        @block.gpsimd
        def _(eng):
            for c in range(B):
                for m in range(MF):
                    q = c * MF + m
                    eng.wait_ge(s_a, (q + 1) * 2)
                    need(eng, s_y, (c - 1) * ST)
                    eng.tensor_tensor(g[:, c % 2, m, :], act[:, q % 2, :], p3c[:, q % 2, :], ALU.mult).then_inc(s_g, 1)

        return tensor

    def experts(self, XS, YS):
        nc, t = self.nc, self.t
        MF = FF1 // P
        NTL = len(CAP_TILES)
        with ExitStack() as ctx:
            w1, w3 = (self.sb(n, [P, 4, KD, FF1], ctx=ctx) for n in ("w1", "w3"))
            w2 = self.sb("w2", [P, 4, MF, D], ctx=ctx)
            xs = self.sb("xs", [P, 4, NTL, D], ctx=ctx)
            xT = self.sb("xT", [P, 2, KD, CAP], ctx=ctx)
            act = self.sb("act", [P, 2, CAP], ctx=ctx)
            g = self.sb("g", [P, 2, MF, CAP], ctx=ctx)
            ys = self.sb("ys", [P, 2, NTL, D], ctx=ctx)
            px = self.ps("px", [P, KD, 512], ctx)
            p1 = self.ps("p1", [P, 2, 512], ctx)
            p3 = self.ps("p3", [P, 2, 512], ctx)
            py = self.ps("py", [P, 2, 512], ctx)
            s_x, s_xt, s_h, s_a, s_g, s_y, s_yb = (self.sem(n, ctx) for n in ("s_x", "s_xt", "s_h", "s_a", "s_g", "s_y", "s_yb"))
            s_w = [self.sem("s_w", ctx) for _ in range(4)]
            s_st = [self.sem("s_st", ctx) for _ in range(2)]
            LOADS = (3 + NTL) * 16
            with nc.Block() as block:
                @block.sync
                def _(eng):
                    def step(at):
                        i, u, par = at.i, at.half, at.odd
                        if not inside(i, E1):
                            return
                        need(eng, s_y, (i - 3) * NTL)
                        one = bass.ds(i, 1)
                        for j, (s, rows) in enumerate(CAP_TILES):
                            eng.dma_start(xs[0:rows, at.slot, j, :], XS[bass.ds(i * CAP + s, rows), :]).then_inc(s_w[at.slot], 16)
                        for w, src in ((w1, "L1_ffn_ew1"), (w3, "L1_ffn_ew3"), (w2, "L1_ffn_ew2")):
                            eng.dma_start(w[:, at.slot], t[src][one].rearrange("o (k p) f -> p (o k) f", p=P)).then_inc(s_w[at.slot], 16)
                    steps(eng, step, E1, behind=0)

                @block.tensor
                def _(eng):
                    def up(at, m):
                        i = at.i
                        need(eng, s_g, i * MF + m - 1)
                        for w, bank in ((w1, p1), (w3, p3)):
                            for k in range(KD):
                                ins = eng.matmul(bank[:, m % 2, 0:CAP], w[:, at.slot, k, m * P:(m + 1) * P], xT[:, at.odd, k, :],
                                                 start=(k == 0), stop=(k == KD - 1))
                        ins.then_inc(s_h, 1)

                    def step(at):
                        i, par = at.i, at.odd
                        if inside(i, E1):
                            eng.wait_ge(s_w[at.slot], (at.quarter + 1) * LOADS)
                            need(eng, s_xt, i * KD)
                            for k in range(KD):
                                for j, (s, rows) in enumerate(CAP_TILES):
                                    ins = eng.transpose(px[:, k, s:s + rows], xs[0:rows, at.slot, j, k * P:(k + 1) * P],
                                                        self.ident[0:rows, 0:rows])
                                ins.then_inc(s_x, 1)
                            eng.wait_ge(s_xt, (i + 1) * KD)
                            up(at, 0)
                        a = i - 1
                        if inside(a, E1):
                            eng.wait_ge(s_g, (a + 1) * MF)
                            for j, (s, rows) in enumerate(CAP_TILES):
                                need(eng, s_yb, a * NTL + j - 1)
                                for m in range(MF):
                                    ins = eng.matmul(py[0:rows, (1 - par + j) % 2, 0:D], g[:, 1 - par, m, s:s + rows], w2[:, (at.slot - 1) % 4, m, :],
                                                     start=(m == 0), stop=(m == MF - 1))
                                ins.then_inc(s_y, 1)
                        if inside(i, E1):
                            for m in range(1, MF):
                                up(at, m)
                    steps(eng, step, E1, behind=1)

                @block.scalar
                def _(eng):
                    def step(at):
                        i, par = at.i, at.odd
                        if inside(i, E1):
                            for k in range(KD):
                                eng.wait_ge(s_x, i * KD + k + 1)
                                if k == 0:
                                    need(eng, s_h, (i - 1) * MF)
                                eng.copy(xT[:, par, k, :], px[:, k, 0:CAP]).then_inc(s_xt, 1)
                            for m in range(MF):
                                eng.wait_ge(s_h, i * MF + m + 1)
                                need(eng, s_g, i * MF + m - 1)
                                eng.activation(act[:, m % 2, :], p1[:, m % 2, 0:CAP], ACT.Silu).then_inc(s_a, 1)
                        a = i - 1
                        if inside(a, E1):
                            eng.wait_ge(s_yb, (a + 1) * NTL)
                            for j, (s, rows) in enumerate(CAP_TILES):
                                eng.dma_start(YS[bass.ds(a * CAP + s, rows), :], ys[0:rows, 1 - par, j, :]).then_inc(s_st[1 - par], 16)
                    steps(eng, step, E1, behind=1)
                    for s in s_st:
                        eng.wait_ge(s, 16 * NTL * E1 // 2)

                @block.vector
                def _(eng):
                    def gated(i, par, m):
                        eng.wait_ge(s_a, i * MF + m + 1)
                        if m == 0:
                            need(eng, s_y, (i - 1) * NTL)
                        eng.tensor_tensor(g[:, par, m, :], act[:, m % 2, :], p3[:, m % 2, 0:CAP], ALU.mult).then_inc(s_g, 1)

                    def step(at):
                        i, par = at.i, at.odd
                        if inside(i, E1):
                            gated(i, par, 0)
                        a = i - 1
                        if inside(a, E1):
                            if not isinstance(a, int) or a >= 2:
                                eng.wait_ge(s_st[1 - par], (at.half if par else at.half - 1) * 16 * NTL)
                            for j, (s, rows) in enumerate(CAP_TILES):
                                eng.wait_ge(s_y, a * NTL + j + 1)
                                eng.tensor_copy(ys[0:rows, 1 - par, j, :], py[0:rows, (1 - par + j) % 2, 0:D]).then_inc(s_yb, 1)
                        if inside(i, E1):
                            for m in range(1, MF):
                                gated(i, par, m)
                    steps(eng, step, E1, behind=1)

    def combine_top2(self, gather, w_k, YS, common, x):
        nc = self.nc
        with ExitStack() as ctx:
            y = self.sb("y", [P, NT, TOPK, D], ctx=ctx)
            s_g, s_ch = [self.sem("s_g", ctx) for _ in range(4)], self.sem("s_ch", ctx)
            with nc.Block() as block:
                @block.gpsimd
                def _(eng):
                    for n in range(NT):
                        for k in range(TOPK):
                            eng.indirect_dma_start(out=y[:, n, k, :], out_offset=None, in_=YS,
                                                   in_offset=bass.IndirectOffsetOnAxis(ap=gather[:, k, n:n + 1], axis=0))\
                               .then_inc(s_g[n // ST], 16)

                @block.vector
                def _(eng):
                    do = Chain(eng, s_ch)
                    do(eng.scalar_tensor_tensor(out=x[:], in0=common[:], scalar=1.0 / NSH, in1=x[:], op0=ALU.mult, op1=ALU.add))
                    do.wait()
                    for b in range(B):
                        eng.wait_ge(s_g[b], 16 * ST * TOPK)
                        for k in range(TOPK):
                            for n in range(b * ST, (b + 1) * ST):
                                do(eng.scalar_tensor_tensor(out=x[:, n, :], in0=y[:, n, k, :], scalar=w_k[:, k, n:n + 1], in1=x[:, n, :],
                                                            op0=ALU.mult, op1=ALU.add))
                            do.wait()


def build(nc, t, out):
    p = Program(nc, t, out)
    with p.ctx:
        p.load()
        QS = p.dram("q_stacks", [2, NBH, DK, S])
        KS = p.dram("k_stacks", [2, NBH, DK, S])
        with ExitStack() as ctx:
            V = p.sb("V", [P, NBH, ST, VW], F32R, ctx=ctx)
            O = p.sb("O", [P, NBH, ST, DK], ctx=ctx)
            with ExitStack() as inner:
                z = p.sb("z", [P, NT, D], ctx=inner)
                zT = p.sb("zT", [P, KD, N], ctx=inner)
                cT = p.sb("cT", [P, KD, N], ctx=inner)
                p.norm_and_transpose(p.x, z, zT)
                p.load_context(cT)
                p.project(zT, cT, t["L0_xattn_Wq"], t["L0_xattn_Wk"], t["L0_xattn_Wv"], None, None, None, 1.0, QS, KS, V)
            with ExitStack() as inner:
                mask = p.dram("mask", [B, P, ST, S], BF16)
                p.prepare_mask(mask)
                p.attention("mask", QS, KS, V, O, DK ** -0.5, mask=mask, k_aux=-1e-9 * DK ** 0.5)
            p.output(O, t["L0_xattn_Wo"], None, p.x, p.x)
        with ExitStack() as ctx:
            f = {n[7:]: v for n, v in t.items() if n.startswith("L0_ffn_")}
            src = p.sb("src", [P, NT, D], ctx=ctx)
            xx = p.sb("xx", [P, NT, D], ctx=ctx)
            slot = p.sb("slot", [P, NT], U32, ctx=ctx)
            tile_expert = p.sb("tile_expert", [P, L0_TILES], I32, ctx=ctx)
            XS = p.dram("top1_in", [L0_SLOTS, D])
            YS = p.dram("top1_out", [L0_SLOTS, D])
            with ExitStack() as inner:
                V = p.sb("V", [P, NBH, ST, VW], F32R, ctx=inner)
                O = p.sb("O", [P, NBH, ST, DK], ctx=inner)
                with ExitStack() as deep:
                    sT = p.sb("sT", [P, KD, N], ctx=deep)
                    p.norm_and_transpose(p.x, src, sT)
                    p.project(sT, sT, f["Wq"], f["Wk"], f["Wv"], f["bq"], f["bk"], f["bv"], DK ** -0.5, QS, KS, V)
                p.attention("self", QS, KS, V, O, 1.0)
                p.output(O, f["Wo"], f["bo"], src, src)
            p.route_top1(src, xx, f["ln1_g"], f["ln1_b"], slot, tile_expert, XS)
            p.top1_tiles(tile_expert, XS, YS)
            p.combine_top1(xx, slot, YS, f["ln2_g"], f["ln2_b"], p.x)
        p.recycle()
        with ExitStack() as ctx:
            f = {n[9:]: v for n, v in t.items() if n.startswith("L1_xattn_")}
            V = p.sb("V", [P, NBH, ST, VW], F32R, ctx=ctx)
            O = p.sb("O", [P, NBH, ST, DK], ctx=ctx)
            with ExitStack() as inner:
                z = p.sb("z", [P, NT, D], ctx=inner)
                zT = p.sb("zT", [P, KD, N], ctx=inner)
                cT = p.sb("cT", [P, KD, N], ctx=inner)
                p.norm_and_transpose(p.x, z, zT)
                p.load_context(cT)
                p.project(zT, cT, f["Wq"], f["Wk"], f["Wv"], f["bq"], f["bk"], f["bv"], DK ** -0.5 / 2, QS, KS, V)
            with ExitStack() as inner:
                common = p.sb("common", [P, B, ST, S], ctx=inner)
                p.prepare_common(common)
                side = t["fside_Bx16xSxS2_0"].rearrange("b h (t p) k -> (b h) p t k", p=P)
                p.attention("side", QS, KS, V, O, 2.0, common=common, side=side)
            p.output(O, f["Wo"], f["bo"], p.x, p.x)
        with ExitStack() as ctx:
            w_k = p.sb("w_k", [P, TOPK, NT], ctx=ctx)
            oh = p.sb("oh", [P, TOPK, NT, E1], ctx=ctx)
            scatter = p.sb("scatter", [P, TOPK, NT], U32, ctx=ctx)
            gather = p.sb("gather", [P, TOPK, NT], U32, ctx=ctx)
            common = p.sb("common", [P, NT, D], ctx=ctx)
            XS = p.dram("top2_in", [L1_ROWS, D])
            YS = p.dram("top2_out", [ZERO_ROW + P, D])
            with ExitStack() as inner:
                z = p.sb("z", [P, NT, D], ctx=inner)
                zT = p.sb("zT", [P, KD, N], ctx=inner)
                p.norm_and_transpose(p.x, z, zT)
                p.route_and_share(zT, w_k, oh, scatter, gather, XS, YS, common)
                p.dispatch(z, scatter, XS, YS)
            p.experts(XS, YS)
            p.combine_top2(gather, w_k, YS, common, p.x)
        p.store(p.x)


_TRANSPOSED = ("L0_xattn_Wq", "L0_xattn_Wk", "L0_xattn_Wv", "L0_xattn_Wo", "L1_xattn_Wq", "L1_xattn_Wk", "L1_xattn_Wv",
               "L1_xattn_Wo", "ctx_1024")


def kernel(**inputs):
    import numpy as np
    import concourse.bacc as bacc
    from concourse.bass_utils import run_bass_kernel_spmd

    nc = bacc.Bacc("TRN2", target_bir_lowering=False, num_devices=1)
    arrays, t = {}, {}
    for name, a in inputs.items():
        a = np.asarray(a)
        if name in _TRANSPOSED:
            a = a.reshape(-1, a.shape[-1]).T
        if name == "L0_ffn_b1":
            a = a.reshape(E0, -1, P).transpose(0, 2, 1)
        if name[-3:] in ("_bq", "_bk"):
            a = a.reshape(KD, P).T
        a = np.ascontiguousarray(a)
        arrays[f"in_{name}"] = a
        t[name] = nc.dram_tensor(f"in_{name}", a.shape, mybir.dt.from_np(a.dtype), kind="ExternalInput").ap()
    out = nc.dram_tensor("out", [B, S, D], F32, kind="ExternalOutput").ap()
    build(nc, t, out)
    r = run_bass_kernel_spmd(nc, [arrays], core_ids=[0])
    return r.results[0]["out"]
```

```python
from contextlib import ExitStack

import concourse.bass as bass
from concourse import mybir
from concourse.alu_op_type import AluOpType as ALU

F32 = mybir.dt.float32
F32R = mybir.dt.float32r
BF16 = mybir.dt.bfloat16
I32 = mybir.dt.int32
U32 = mybir.dt.uint32
ACT = mybir.ActivationFunctionType
AX = mybir.AxisListType.X

P = 128
B, S, D, H = 4, 512, 256, 16
DK = D // H
VW = 2 * DK + 1
N = B * S
NT = N // P
ST = S // P
KD = D // P
NBH = B * H
AUX = 4 * DK
SPLIT = 3
EPS = 1e-5
LOWEST = -3.0e38
E0, FF0 = 4, 1024
E1, FF1, TOPK = 16, 512, 2
CAP = -(-N * TOPK // E1 * 5 // 4)
NSH = 2
FSH = NSH * FF1

L0_TILES = 20
L0_SLOTS = L0_TILES * P
L1_SLOTS = E1 * CAP
ZERO_ROW = L1_SLOTS
DROP_ROW = L1_SLOTS + P
L1_ROWS = DROP_ROW + TOPK * N
CAP_TILES = [(s, min(P, CAP - s)) for s in range(0, CAP, P)]


class Step:

    def __init__(self, i, half, odd, quarter, slot):
        self.i, self.half, self.odd, self.quarter, self.slot = i, half, odd, quarter, slot

    def back(self, n):
        return Step(self.i - n, self.half + (self.odd - n) // 2, (self.odd - n) % 2,
                    self.quarter + (self.slot - n) // 4, (self.slot - n) % 4)


def steps(eng, step, trips, behind=2, body=4):
    assert trips % body == 0 and body % 4 == 0

    def plain(i):
        step(Step(i, i // 2, i % 2, i // 4, i % 4))

    for i in range(body):
        plain(i)
    with eng.Fori(1, trips // body) as v:
        for j in range(body):
            step(Step(v * body + j, v * (body // 2) + j // 2, j % 2, v * (body // 4) + j // 4, j % 4))
    for i in range(trips, trips + behind):
        plain(i)


def need(eng, sem, value):
    if not isinstance(value, int) or value > 0:
        eng.wait_ge(sem, value)


def unfused(eng, spare, i):
    if not isinstance(i, int):
        eng.sem_inc(spare, 1)


def inside(i, trips):
    return not isinstance(i, int) or 0 <= i < trips


class Chain:

    def __init__(self, eng, sem):
        self.eng, self.sem, self.base, self.k, self.loop, self.rate = eng, sem, 0, 0, None, 0

    def __call__(self, ins):
        ins.then_inc(self.sem, 1)
        self.k += 1
        return ins

    def wait(self):
        self.eng.wait_ge(self.sem, self.value())

    def value(self):
        at = self.base + self.k
        return at if self.loop is None else self.loop * self.rate + at

    def enter(self, loop, rate):
        self.base, self.k, self.loop, self.rate = self.base + self.k, 0, loop, rate

    def leave(self, trips):
        assert self.k == self.rate, (self.k, self.rate)
        self.base, self.k, self.loop = self.base + trips * self.rate, 0, None


class Program:
    def __init__(self, nc, t, out):
        self.nc, self.t, self.out, self.ctx = nc, t, out, ExitStack()
        self.n_sem, self.used = 0, []

    def sem(self, name, ctx=None):
        self.n_sem += 1
        self.used.append(self.nc.alloc_semaphore(f"{name}_{self.n_sem}"))
        return self.used[-1]

    def recycle(self):
        self.nc.clear_and_free_semaphores(self.used)
        self.nc.all_engine_barrier()
        self.used = []

    def sb(self, name, shape, dt=F32, ctx=None):
        self.n_sem += 1
        return (ctx or self.ctx).enter_context(self.nc.sbuf_tensor(f"{name}_{self.n_sem}", shape, dt))

    def ps(self, name, shape, ctx):
        self.n_sem += 1
        return ctx.enter_context(self.nc.psum_tensor(f"{name}_{self.n_sem}", shape, F32))

    def dram(self, name, shape, dt=F32):
        return self.nc.dram_tensor(name, shape, dt, kind="Internal").ap()

    def place(self, ctx):
        self.x = self.sb("x", [P, NT, D])
        self.ident = self.sb("ident", [P, P])
        self.zeros = self.sb("zeros", [P, 2048])
        self.q = self.sb("q", [P, 2, S], F32R, ctx=ctx)
        self.k = self.sb("k", [P, 2, S], F32R, ctx=ctx)

    def load(self, block):
        s_x = [self.sem("s_x") for _ in range(B)]
        s_c, s_v = self.sem("s_c"), self.sem("s_v")

        @block.scalar
        def _(eng):
            for b in range(B):
                eng.dma_start(self.x[:, b * ST:(b + 1) * ST, :], self.t["x"][b].rearrange("(t p) d -> p t d", p=P)).then_inc(s_x[b], 16)

        @block.gpsimd
        def _(eng):
            eng.memset(self.ident[:], 0.0).then_inc(s_c, 1)
            eng.wait_ge(s_c, 1)
            eng.affine_select(out=self.ident[:], in_=self.ident[:], compare_op=ALU.not_equal, fill=1.0,
                              base=0, pattern=[[-1, P]], channel_multiplier=1).then_inc(s_c, 1)
            eng.memset(self.zeros[:], 0.0)

        @block.vector
        def _(eng):
            eng.memset(self.q[AUX:P, :, :].bitcast(F32), 0.0).then_inc(s_v, 1)
            eng.memset(self.k[AUX:P, :, :].bitcast(F32), 0.0).then_inc(s_v, 1)
            eng.wait_ge(s_v, 2)
            eng.memset(self.q[AUX:AUX + 1, :, :].bitcast(F32), 1.0)
            eng.memset(self.k[AUX:AUX + 1, :, :].bitcast(F32), -1e-9 * DK ** 0.5)

        def batch(eng, chain, b):
            eng.wait_ge(s_x[b], 16)

        return batch, s_c

    def normalise(self, block, chain_sem, s_mv, s_rs, s_z, dst, src, ctx, gain=None, shift=None, before=None, ready=None):
        st = self.sb("bn", [P, NT, 6], ctx=ctx)
        mv = self.sb("mv", [P, NT, 2], ctx=ctx)
        rs = self.sb("rs", [P, NT], ctx=ctx)

        @block.vector
        def _(eng):
            chain = Chain(eng, chain_sem)
            for n in range(NT):
                if before is not None and n % ST == 0:
                    before(eng, chain, n // ST)
                chain(eng.bn_stats(st[:, n, :], src[:, n, :]))
            chain.wait()
            for n in range(NT):
                chain(eng.bn_aggr(mv[:, n, :], st[:, n, :]))
            chain.wait()
            eng.tensor_scalar(rs[:], mv[:, :, 1], EPS, None, ALU.add).then_inc(s_mv, 1)
            eng.wait_ge(s_rs, 1)
            chain(eng.reciprocal(rs[:], rs[:]))
            chain.wait()
            for b in range(B):
                rows = range(b * ST, (b + 1) * ST)
                if gain is None:
                    for n in rows:
                        chain(eng.tensor_scalar(dst[:, n, :], src[:, n, :], mv[:, n, 0:1], rs[:, n:n + 1],
                                                ALU.subtract, ALU.mult))
                else:
                    if b == 0:
                        ready(eng)
                    for n in rows:
                        chain(eng.scalar_tensor_tensor(out=dst[:, n, :], in0=src[:, n, :], scalar=mv[:, n, 0:1], in1=gain[:],
                                                       op0=ALU.subtract, op1=ALU.mult))
                    chain.wait()
                    for n in rows:
                        chain(eng.scalar_tensor_tensor(out=dst[:, n, :], in0=dst[:, n, :], scalar=rs[:, n:n + 1], in1=shift[:],
                                                       op0=ALU.mult, op1=ALU.add))
                chain.wait()
                eng.sem_inc(s_z, 1)

        return rs

    @staticmethod
    def deviations(eng, s_mv, s_rs, rs):
        eng.wait_ge(s_mv, 1)
        eng.activation(rs[:], rs[:], ACT.Sqrt).then_inc(s_rs, 1)

    def norm_and_transpose(self, block, ctx, bank, banks, src, nat, featT, before=None):
        s_ch, s_mv, s_rs, s_z, s_tr, s_ev = (self.sem(n, ctx) for n in ("s_ch", "s_mv", "s_rs", "s_z", "s_tr", "s_ev"))
        rs = self.normalise(block, s_ch, s_mv, s_rs, s_z, nat, src, ctx, before=before)

        def tensor(eng, tenant_gone=None):
            for b in range(B):
                eng.wait_ge(s_z, b + 1)
                for k in range(KD):
                    n = b * KD + k
                    if tenant_gone is not None and n < banks:
                        tenant_gone(eng, n)
                    need(eng, s_ev, n - banks + 1)
                    for j in range(ST):
                        ins = eng.transpose(bank[:, n % banks, j * P:(j + 1) * P], nat[:, b * ST + j, k * P:(k + 1) * P], self.ident[:])
                    ins.then_inc(s_tr, 1)

        @block.scalar
        def _(eng):
            self.deviations(eng, s_mv, s_rs, rs)

        def scalar(eng):
            for n in range(B * KD):
                eng.wait_ge(s_tr, n + 1)
                b, k = divmod(n, KD)
                eng.copy(featT[:, k, b * S:(b + 1) * S], bank[:, n % banks, :]).then_inc(s_ev, 1)

        return tensor, scalar, s_ev

    def project(self, src, nat, qT, kvT, context, wq, wk, wv, bq, bk, bv, q_scale, QS, KS, V, mask=None, common=None, first=False):
        nc = self.nc
        with ExitStack() as ctx:
            W = [self.sb(n, [P, KD, D], ctx=ctx) for n in ("wq", "wk", "wv")]
            bias = self.sb("bias", [P, 2, KD], ctx=ctx)
            bvr = self.sb("bvr", [P, D], ctx=ctx)
            whole = self.sb("whole", [P, 2, 512], ctx=ctx)
            vw = self.sb("vw", [P, 2, H, DK], ctx=ctx)
            hi = self.sb("hi", [P, 4, 512], F32R, ctx=ctx)
            lo = self.sb("lo", [P, 4, 512], F32R, ctx=ctx)
            pj = self.ps("pj", [P, 4, 512], ctx)
            pv = self.ps("pv", [P, 4, 512], ctx)
            names = ("s_w", "s_p", "s_t", "s_hi", "s_lo", "s_pv", "s_v", "s_one", "s_vh", "s_vl")
            s_w, s_p, s_t, s_hi, s_lo, s_pv, s_v, s_one, s_vh, s_vl = (self.sem(n, ctx) for n in names)
            s_st = [self.sem("s_st", ctx) for _ in range(4)]
            if mask is not None:
                raw = self.sb("raw", [P, 2, ST, S], I32, ctx=ctx)
                bits = self.sb("bits", [P, 2, ST, S], BF16, ctx=ctx)
                s_m = self.sem("s_m", ctx)
                s_raw, s_bits = ([self.sem(n, ctx) for _ in range(2)] for n in ("s_raw", "s_bits"))
            order = (0, 1) if context is None else (1, 0)
            jobs = [(x, c, m) for x in order for c in range(B) for m in range(KD)]
            n_first = order.index(0) * B * KD
            if common is not None:
                am = self.sb("am", [P, ST, S], ctx=ctx)
                pad = self.sb("pad", [P, B, S], mybir.dt.uint8, ctx=ctx)
                low = self.sb("low", [P, B, S], ctx=ctx)
                s_am, s_low = self.sem("s_am", ctx), self.sem("s_low", ctx)
            n_bias = 3 if bq is not None else 0
            n_load = 3 + n_bias
            s_ctx = [self.sem("s_ctx", ctx) for _ in range(B)] if context is not None else None
            with nc.Block() as block:
                before, s_ident = self.load(block) if first else (None, None)
                turn, take, s_qT = self.norm_and_transpose(block, ctx, pj, 4, src, nat, qT, before)

                def load_mask(eng, b):
                    eng.dma_start(raw[:, b % 2], self.t["mask_Bx1xSxS2_ik1"][b, 0].rearrange("(t p) k -> p t k", p=P)).then_inc(s_raw[b % 2], 16)

                @block.sync
                def _(eng):
                    for w, of in zip(W, (wq, wk, wv)):
                        eng.dma_start(w[:], of.rearrange("(k p) n -> p k n", p=P)).then_inc(s_w, 16)
                    if n_bias:
                        eng.dma_start(bias[:, 0, :], bq).then_inc(s_w, 16)
                        eng.dma_start(bias[:, 1, :], bk).then_inc(s_w, 16)
                        eng.dma_start(bvr[:], bv.partition_broadcast(P)).then_inc(s_w, 16)
                    if context is not None:
                        for c in range(B):
                            eng.dma_start(kvT[:, :, c * S:(c + 1) * S], context[:, c * S:(c + 1) * S].rearrange("(k p) s -> p k s", p=P))\
                               .then_inc(s_ctx[c], 16)
                    if mask is not None:
                        load_mask(eng, 0)
                        load_mask(eng, 1)
                    if common is not None:
                        eng.dma_start(am[:], self.t["fside_SxS2_0"].rearrange("(t p) k -> p t k", p=P)).then_inc(s_am, 16)
                        eng.dma_start(pad[:], self.t["mask_BxS2_bf0"].partition_broadcast(P)).then_inc(s_am, 16)
                    for n, (x, c, m) in enumerate(jobs):
                        rows = slice(c * H + m * (P // DK), c * H + (m + 1) * (P // DK))
                        for part, (s, buf) in enumerate(((s_hi, hi), (s_lo, lo))):
                            eng.wait_ge(s, n + 1)
                            eng.dma_start((QS, KS)[x][part, rows].rearrange("h d s -> (h d) s"), buf[:, n % 4, :].bitcast(F32)).then_inc(s_st[n % 4], 16)
                        if mask is not None and n % ST == ST - 1:
                            b = n // ST
                            eng.wait_ge(s_m, b + 1)
                            eng.dma_start(mask[b], bits[:, b % 2]).then_inc(s_bits[b % 2], 16)
                            if b + 2 < B:
                                load_mask(eng, b + 2)
                    if mask is not None:
                        for sem in s_bits:
                            eng.wait_ge(sem, 16 * B // 2)
                    for s in s_st:
                        eng.wait_ge(s, 32 * len(jobs) // 4)

                @block.tensor
                def _(eng):
                    if n_first:
                        eng.wait_ge(s_w, 16 * n_load)
                    for n, (x, c, m) in enumerate(jobs):
                        if n == n_first:
                            if first:
                                eng.wait_ge(s_ident, 2)
                            turn(eng, lambda e, bank: need(e, s_t, n_first - 3 + bank if n_first else 0))
                            eng.wait_ge(s_w, 16 * n_load)
                            eng.wait_ge(s_qT, KD * B)
                        if n < n_first and n % KD == 0:
                            eng.wait_ge(s_ctx[c], 16)
                        need(eng, s_t, n - 3)
                        of = (qT, kvT)[x]
                        for k in range(KD):
                            ins = eng.matmul(pj[:, n % 4, :], W[x][:, k, m * P:(m + 1) * P], of[:, k, c * S:(c + 1) * S],
                                             start=(k == 0), stop=(k == KD - 1))
                        ins.then_inc(s_p, 1)
                        need(eng, s_v, n - 3)
                        for k in range(KD):
                            ins = eng.matmul(pv[:, n % 4, 0:D], kvT[:, k, n * P:(n + 1) * P], W[2][:, k, :],
                                             start=(k == 0), stop=(k == KD - 1))
                        ins.then_inc(s_pv, 1)

                @block.vector
                def _(eng):
                    eng.memset(V[:, :, :, DK:DK + 1].bitcast(F32), 1.0).then_inc(s_one, 1)
                    if not n_bias:
                        eng.memset(bias[:], 0.0).then_inc(s_one, 1)
                        eng.memset(bvr[:], 0.0).then_inc(s_one, 1)
                        eng.wait_ge(s_one, 3)
                    eng.wait_ge(s_w, 16 * n_load)

                    def rest(n):
                        eng.wait_ge(s_hi, n + 1)
                        need(eng, s_st[n % 4], 32 * (n // 4))
                        eng.tensor_tensor(lo[:, n % 4, :], whole[:, n % 2, :], hi[:, n % 4, :].bitcast(F32), ALU.subtract)\
                           .then_inc(s_lo, 1)

                    for n, (x, c, m) in enumerate(jobs):
                        eng.wait_ge(s_p, n + 1)
                        need(eng, s_lo, n - 1)
                        eng.tensor_scalar(whole[:, n % 2, :], pj[:, n % 4, :], bias[:, x, m:m + 1], q_scale if x == 0 else 1.0,
                                          ALU.add, ALU.mult).then_inc(s_t, 1)
                        eng.wait_ge(s_pv, n + 1)
                        need(eng, s_vl, n - 1)
                        eng.tensor_tensor(vw[:, n % 2], pv[:, n % 4, 0:D].rearrange("p (h d) -> p h d", d=DK),
                                          bvr[:].rearrange("p (h d) -> p h d", d=DK), ALU.add).then_inc(s_v, 1)
                        rest(n)
                        if mask is not None and n % ST == ST - 1:
                            b = n // ST
                            eng.wait_ge(s_raw[b % 2], 16 * (b // 2 + 1))
                            need(eng, s_bits[b % 2], 16 * (b // 2))
                            eng.tensor_scalar(bits[:, b % 2], raw[:, b % 2], 0, None, ALU.not_equal).then_inc(s_m, 1)
                        if common is not None and n % ST == ST - 1:
                            b = n // ST
                            if b == 0:
                                eng.wait_ge(s_am, 32)
                            eng.tensor_scalar(low[:, b], pad[:, b], -3.0e38, 10.0, ALU.mult, ALU.mult).then_inc(s_low, 1)
                            eng.wait_ge(s_low, b + 1)
                            eng.scalar_tensor_tensor(out=common[:, b], in0=am[:], scalar=0.5,
                                                     in1=low[:, b].unsqueeze(1).to_broadcast([P, ST, S]), op0=ALU.mult, op1=ALU.add)

                @block.scalar
                def _(eng):
                    for n in range(len(jobs)):
                        if n == n_first:
                            take(eng)
                        eng.wait_ge(s_t, n + 1)
                        need(eng, s_st[n % 4], 32 * (n // 4))
                        eng.copy(hi[:, n % 4, :], whole[:, n % 2, :]).then_inc(s_hi, 1)
                        eng.wait_ge(s_v, n + 1)
                        b, j = divmod(n, ST)
                        eng.copy(V[:, b * H:(b + 1) * H, j, 0:DK], vw[:, n % 2]).then_inc(s_vh, 1)

                @block.gpsimd
                def _(eng):
                    for n in range(NT):
                        eng.wait_ge(s_vh, n + 1)
                        b, j = divmod(n, ST)
                        heads = slice(b * H, (b + 1) * H)
                        eng.tensor_tensor(V[:, heads, j, DK + 1:VW], vw[:, n % 2], V[:, heads, j, 0:DK].bitcast(F32), ALU.subtract)\
                           .then_inc(s_vl, 1)

    def attention(self, kind, QS, KS, V, O, exp_scale, mask=None, common=None, side=None):
        nc = self.nc
        with ExitStack() as ctx:
            q, k = self.q, self.k
            v = self.sb("v", [P, 2, ST, VW], F32R, ctx=ctx)
            X = self.sb("X", [P, 2, ST, S], ctx=ctx)
            PH, PL = (self.sb(n, [P, 2, SPLIT, S], F32R, ctx=ctx) for n in ("PH", "PL"))
            PW = self.sb("PW", [P, 2, ST - SPLIT, S], ctx=ctx)
            OT = self.sb("OT", [VW, S], ctx=ctx)
            both = self.sb("both", [P, ST, DK], ctx=ctx)
            mx = self.sb("mx", [P, 2, ST], ctx=ctx)
            nm = self.sb("nm", [P, 2, ST], ctx=ctx)
            rec = self.sb("rec", [P, ST, 1], ctx=ctx)
            M = None if kind == "self" else self.sb("M", [P, 4, ST, S], BF16 if kind == "mask" else F32, ctx=ctx)
            pS = self.ps("pS", [P, 2, 512], ctx)
            pT = self.ps("pT", [P, 4, 512], ctx)
            pO = self.ps("pO", [P, 512], ctx)
            pB = self.ps("pB", [P, 512], ctx)
            names = ("s_c", "s_s", "s_x", "s_nm", "s_p", "s_t", "s_ea", "s_ed", "s_o", "s_oc", "s_b", "s_r", "s_n",
                     "s_m", "s_spv", "s_spt", "s_spg")
            (s_c, s_s, s_x, s_nm, s_p, s_t, s_ea, s_ed, s_o, s_oc, s_b, s_r, s_n, s_m, s_spv, s_spt, s_spg) = (self.sem(n, ctx) for n in names)
            s_ld = [self.sem("s_ld", ctx) for _ in range(2)]
            s_f = [self.sem("s_f", ctx) for _ in range(4)]
            s_v = [self.sem("s_v", ctx) for _ in range(2)]
            PER = 6 * 16

            with nc.Block() as block:
                @block.sync
                def _(eng):
                    def step(at):
                        i, par = at.i, at.odd
                        h = i - 2
                        if inside(h, NBH):
                            need(eng, s_s, (h - 1) * 4)
                            for r in range(4):
                                eng.dma_start(q[r * DK:(r + 1) * DK, par, :].bitcast(F32), QS[r // 2, bass.ds(h, 1)].rearrange("o d s -> (o d) s"))\
                                   .then_inc(s_ld[par], 16)
                            for r in range(2):
                                eng.dma_start(k[r * 2 * DK:(r + 1) * 2 * DK, par, :].bitcast(F32), KS[:, bass.ds(h, 1)].rearrange("r o d s -> r (o d) s"))\
                                   .then_inc(s_ld[par], 16)
                        if kind != "self" and inside(i, NBH):
                            need(eng, s_x, (i - 3) * 4)
                            src = side[bass.ds(i, 1)] if kind == "side" else mask[bass.ds(i // H, 1)]
                            eng.dma_start(M[:, at.slot], src.rearrange("o p t k -> (o p) t k")).then_inc(s_f[at.slot], 16)
                        a = i - 4
                        if inside(a, NBH):
                            need(eng, s_o, a - 1)
                            eng.dma_start(v[:, par].bitcast(F32), V[:, bass.ds(a, 1)].rearrange("p o t d -> p (o t) d").bitcast(F32))\
                               .then_inc(s_v[par], 16)
                    steps(eng, step, NBH, behind=4, body=8)

                @block.gpsimd
                def _(eng):
                    def bias(i, quarter, slot, b):
                        eng.wait_ge(s_f[slot], (quarter + 1) * 16)
                        unfused(eng, s_spg, i)
                        eng.tensor_tensor(M[:, slot], M[:, slot], common[:, bass.ds(b, 1)].rearrange("p o t k -> p (o t) k"),
                                          ALU.add).then_inc(s_m, 1)

                    if kind == "side":
                        for i in range(H):
                            bias(i, i // 4, i % 4, 0)
                        with eng.Fori(1, B) as b:
                            for h in range(H):
                                bias(b * H + h, b * (H // 4) + h // 4, h % 4, b)

                @block.tensor
                def _(eng):
                    if kind == "self":
                        eng.wait_ge(s_c, 1)

                    def scores(i, u, par, qts):
                        if not inside(i, NBH):
                            return
                        for qt in qts:
                            if qt == 0:
                                eng.wait_ge(s_ld[par], (u + 1) * PER)
                            if qt < 2:
                                need(eng, s_x, (i - 1) * 4 + qt + 3)
                            else:
                                eng.wait_ge(s_x, i * 4 + qt - 1)
                            eng.matmul(pS[:, qt % 2, :], q[:, par, qt * P:(qt + 1) * P], k[:, par, :], start=True, stop=True)\
                               .then_inc(s_s, 1)

                    def turn(t, par, kts):
                        if not inside(t, NBH):
                            return
                        for kt in kts:
                            if kt < SPLIT:
                                need(eng, s_ed, (t - 1) * SPLIT + kt + 1)
                            else:
                                need(eng, s_ea, t * ST)
                        for qt in range(ST):
                            if 0 in kts:
                                eng.wait_ge(s_p, t * 4 + qt + 1)
                            for kt in kts:
                                ins = eng.transpose(pT[:, kt, qt * P:(qt + 1) * P], X[:, par, qt, kt * P:(kt + 1) * P],
                                                    self.ident[:])
                                if qt == ST - 1:
                                    ins.then_inc(s_t, 1)

                    def step(at):
                        i, u, par = at.i, at.half, at.odd
                        scores(i, u, par, (0, 1))
                        turn(i - 1, 1 - par, (0, 1))
                        scores(i, u, par, (2,))
                        turn(i - 1, 1 - par, (2,))
                        scores(i, u, par, (3,))
                        turn(i - 1, 1 - par, (3,))
                        b = i - 3
                        if inside(b, NBH):
                            eng.wait_ge(s_oc, b + 1)
                            need(eng, s_n, b)
                            unfused(eng, s_spt, i)
                            for qt in range(ST):
                                ins = eng.transpose(pB[:, qt * VW:(qt + 1) * VW], OT[:, qt * P:(qt + 1) * P],
                                                    self.ident[0:VW, 0:VW])
                            ins.then_inc(s_b, 1)
                        a = i - 2
                        if inside(a, NBH):
                            eng.wait_ge(s_v[par], u * 16)
                            eng.wait_ge(s_ed, (a + 1) * SPLIT)
                            eng.wait_ge(s_ea, (a + 1) * ST)
                            need(eng, s_oc, a)
                            for kt in range(SPLIT):
                                for part in (PH, PL):
                                    eng.matmul(pO[0:VW, :], v[:, par, kt, :], part[:, par, kt, :],
                                               start=(kt == 0 and part is PH), stop=False)
                            for kt in range(SPLIT, ST):
                                ins = eng.matmul(pO[0:VW, :], v[:, par, kt, :].bitcast(F32), PW[:, par, kt - SPLIT, :],
                                                 start=False, stop=(kt == ST - 1))
                            ins.then_inc(s_o, 1)
                    steps(eng, step, NBH, behind=3, body=8)

                @block.vector
                def _(eng):
                    if kind == "self":
                        eng.memset(k[AUX:AUX + 1, :, :].bitcast(F32), 0.0).then_inc(s_c, 1)

                    def finish(b, part):
                        if not inside(b, NBH):
                            return
                        o = pB[:, 0:ST * VW].rearrange("p (t d) -> p t d", d=VW)
                        if part == 0:
                            eng.wait_ge(s_b, b + 1)
                            need(eng, s_n, b)
                            eng.tensor_copy(both[:], o[:, :, 0:DK]).then_inc(s_r, 1)
                            eng.reciprocal(rec[:], o[:, :, DK:DK + 1]).then_inc(s_r, 1)
                        elif part == 1:
                            eng.wait_ge(s_r, b * 3 + 2)
                            eng.tensor_tensor(both[:], both[:], o[:, :, DK + 1:VW], ALU.add).then_inc(s_r, 1)
                        else:
                            eng.wait_ge(s_r, b * 3 + 3)
                            to = O[:].rearrange("p (b t) (h d) -> p b h t d", b=B, d=DK)[:, bass.ds(b // H, 1), bass.ds(b % H, 1)]
                            eng.tensor_tensor(to.rearrange("p b h t d -> p (b h t) d"), both[:],
                                              rec[:].to_broadcast([P, ST, DK]), ALU.mult).then_inc(s_n, 1)

                    def maxima(at):
                        i, u, par = at.i, at.half, at.odd
                        if not inside(i, NBH):
                            return
                        if kind == "side":
                            eng.wait_ge(s_m, i + 1)
                        if kind == "mask":
                            eng.wait_ge(s_f[at.slot], (at.quarter + 1) * 16)
                        need(eng, s_t, (i - 1) * 4)
                        for qt in range(ST):
                            eng.wait_ge(s_s, i * 4 + qt + 1)
                            unfused(eng, s_spv, i)
                            eng.tensor_tensor_reduce(X[:, par, qt, :], pS[:, qt % 2, :],
                                                     self.zeros[:, 0:S] if kind == "self" else M[:, at.slot, qt, :], 1.0, LOWEST,
                                                     ALU.mult if kind == "mask" else ALU.add, ALU.max,
                                                     mx[:, par, qt:qt + 1]).then_inc(s_x, 1)
                        eng.wait_ge(s_x, (i + 1) * 4)
                        eng.tensor_scalar(nm[:, par, :], mx[:, par, :], -exp_scale, None, ALU.mult).then_inc(s_nm, 1)

                    def step(at):
                        i, u, par = at.i, at.half, at.odd
                        maxima(at)
                        t = i - 1
                        for kt in range(SPLIT):
                            if inside(t, NBH):
                                eng.wait_ge(s_ea, t * ST + kt + 1)
                                eng.tensor_tensor(PL[:, 1 - par, kt, :], pT[:, kt, :], PH[:, 1 - par, kt, :].bitcast(F32),
                                                  ALU.subtract).then_inc(s_ed, 1)
                            finish(i - 3, kt)
                    steps(eng, step, NBH, behind=3, body=8)

                @block.scalar
                def _(eng):
                    def step(at):
                        i, u, par = at.i, at.half, at.odd
                        t, a = i - 1, i - 2
                        if inside(t, NBH):
                            for kt in range(ST):
                                eng.wait_ge(s_t, t * 4 + kt + 1)
                                if kt == 0:
                                    need(eng, s_o, t - 1)
                                to = PH[:, 1 - par, kt, :] if kt < SPLIT else PW[:, 1 - par, kt - SPLIT, :]
                                eng.copy(to, pT[:, kt, :]).then_inc(s_ea, 1)
                        if inside(i, NBH):
                            for qt in range(ST):
                                if qt == 0:
                                    eng.wait_ge(s_nm, i + 1)
                                eng.activation(X[:, par, qt, :], X[:, par, qt, :], ACT.Exp,
                                               bias=nm[:, par, qt:qt + 1], scale=exp_scale).then_inc(s_p, 1)
                        if inside(a, NBH):
                            eng.wait_ge(s_o, a + 1)
                            need(eng, s_b, a)
                            eng.copy(OT[:], pO[0:VW, :]).then_inc(s_oc, 1)
                    steps(eng, step, NBH, behind=3, body=8)

    def output(self, O, wo, bo, base, dst):
        nc = self.nc
        with ExitStack() as ctx:
            w = self.sb("wo", [P, KD, D], ctx=ctx)
            brow = self.sb("bo", [P, D], ctx=ctx)
            OT = self.sb("oT", [P, 2, KD, S], ctx=ctx)
            bank = self.ps("tp", [P, 4, 512], ctx)
            py = self.ps("py", [P, 4, 512], ctx)
            s_w, s_tr, s_ev, s_y, s_a, s_b = (self.sem(n, ctx) for n in ("s_w", "s_tr", "s_ev", "s_y", "s_a", "s_b"))
            with nc.Block() as block:
                @block.sync
                def _(eng):
                    eng.dma_start(w[:], wo.rearrange("(k p) n -> p k n", p=P)).then_inc(s_w, 16)
                    if bo is not None:
                        eng.dma_start(brow[:], bo.partition_broadcast(P)).then_inc(s_w, 16)

                @block.tensor
                def _(eng):
                    def turn(b):
                        for k in range(KD):
                            n = b * KD + k
                            need(eng, s_ev, n - 3)
                            for j in range(ST):
                                ins = eng.transpose(bank[:, n % 4, j * P:(j + 1) * P], O[:, b * ST + j, k * P:(k + 1) * P],
                                                    self.ident[:])
                            ins.then_inc(s_tr, 1)

                    turn(0)
                    eng.wait_ge(s_w, 16 if bo is None else 32)
                    for b in range(B):
                        if b + 1 < B:
                            turn(b + 1)
                        eng.wait_ge(s_ev, (b + 1) * KD)
                        for j in range(ST):
                            n = b * ST + j
                            need(eng, s_a, n - 3)
                            for k in range(KD):
                                ins = eng.matmul(py[:, n % 4, 0:D], OT[:, b % 2, k, j * P:(j + 1) * P], w[:, k, :],
                                                 start=(k == 0), stop=(k == KD - 1))
                            ins.then_inc(s_y, 1)

                @block.scalar
                def _(eng):
                    for n in range(B * KD):
                        b, k = divmod(n, KD)
                        eng.wait_ge(s_tr, n + 1)
                        need(eng, s_y, (b - 1) * ST)
                        eng.copy(OT[:, b % 2, k, :], bank[:, n % 4, :]).then_inc(s_ev, 1)

                @block.vector
                def _(eng):
                    if bo is not None:
                        eng.wait_ge(s_w, 32)
                        for b in range(B):
                            rows = slice(b * ST, (b + 1) * ST)
                            eng.tensor_tensor(dst[:, rows, :], base[:, rows, :], brow[:].unsqueeze(1).to_broadcast([P, ST, D]),
                                              ALU.add).then_inc(s_b, 1)
                        eng.wait_ge(s_b, B)
                    src = base if bo is None else dst
                    for n in range(NT):
                        eng.wait_ge(s_y, n + 1)
                        eng.tensor_tensor(dst[:, n, :], src[:, n, :], py[:, n % 4, 0:D], ALU.add).then_inc(s_a, 1)

    def route_top1(self, src, xx, gain, shift, slot, tile_expert, XS):
        nc, t = self.nc, self.t
        with ExitStack() as ctx:
            grow, brow, rw = (self.sb(n, [P, D], ctx=ctx) for n in ("grow", "brow", "rw"))
            rb = self.sb("rb", [P, 1], ctx=ctx)
            junk = self.sb("junk", [P, NT, D], ctx=ctx)
            key, kf, gt = (self.sb(n, [P, NT], ctx=ctx) for n in ("key", "kf", "gt"))
            ki = self.sb("ki", [P, NT], I32, ctx=ctx)
            oh = self.sb("oh", [P, E0, NT], ctx=ctx)
            ohb = self.sb("ohb", [P, E0, NT], BF16, ctx=ctx)
            tri = self.sb("tri", [P, P], BF16, ctx=ctx)
            ones = self.sb("ones", [P, P], BF16, ctx=ctx)
            tot, incl, w = (self.sb(n, [P, E0, NT], ctx=ctx) for n in ("tot", "incl", "w"))
            cnt, ends, base = (self.sb(n, [P, E0], ctx=ctx) for n in ("cnt", "ends", "base"))
            ci = self.sb("ci", [P, E0], I32, ctx=ctx)
            slotf = self.sb("slotf", [P, NT], ctx=ctx)
            starts = self.sb("starts", [P, L0_TILES], ctx=ctx)
            te = self.sb("te", [P, 3, L0_TILES], ctx=ctx)
            ps = self.ps("rt", [P, 2, 512], ctx)
            names = ("s_w", "s_ch", "s_mv", "s_rs", "s_z", "s_c", "s_oh", "s_p", "s_ix", "s_zero", "s_sc")
            s_w, s_ch, s_mv, s_rs, s_z, s_c, s_oh, s_p, s_ix, s_zero, s_sc = (self.sem(n, ctx) for n in names)
            s_ch2 = self.sem("s_ch2", ctx)
            with nc.Block() as block:
                @block.sync
                def _(eng):
                    for dst, srcd in ((grow, gain), (brow, shift), (rb, t["L0_ffn_router_b"])):
                        eng.dma_start(dst[:], srcd.partition_broadcast(P)).then_inc(s_w, 16)
                    eng.dma_start(rw[:], t["L0_ffn_router_w"].rearrange("d o -> (d o)").partition_broadcast(P)).then_inc(s_w, 16)
                    eng.dma_start(XS.rearrange("(p r) d -> p (r d)", p=P)[:, :], self.zero_rows(L0_SLOTS // P)).then_inc(s_zero, 16)

                rs = self.normalise(block, s_ch, s_mv, s_rs, s_z, xx, src, ctx, gain=grow, shift=brow,
                                    ready=lambda eng: eng.wait_ge(s_w, 64))

                @block.scalar
                def _(eng):
                    self.deviations(eng, s_mv, s_rs, rs)

                @block.vector
                def _(eng):
                    do = Chain(eng, s_ch2)

                    def then(ins):
                        do(ins)
                        do.wait()

                    eng.wait_ge(s_z, B)
                    for n in range(NT):
                        do(eng.tensor_tensor_reduce(junk[:, n, :], xx[:, n, :], rw[:], 1.0, 0.0, ALU.mult, ALU.add, key[:, n:n + 1]))
                    do.wait()
                    then(eng.tensor_scalar(key[:], key[:], rb[:, 0:1], None, ALU.add))
                    then(eng.tensor_copy(ki[:], key[:]))
                    then(eng.tensor_copy(kf[:], ki[:]))
                    then(eng.tensor_tensor(gt[:], kf[:], key[:], ALU.is_gt))
                    then(eng.tensor_tensor(kf[:], kf[:], gt[:], ALU.subtract))
                    then(eng.tensor_copy(ki[:], kf[:]))
                    then(eng.tensor_scalar(ki[:], ki[:], E0 - 1, None, ALU.bitwise_and))
                    then(eng.tensor_copy(kf[:], ki[:]))
                    for e in range(E0):
                        do(eng.tensor_scalar(oh[:, e, :], kf[:], float(e), None, ALU.is_equal))
                    do.wait()
                    do(eng.tensor_copy(ohb[:], oh[:]))
                    do.wait()
                    eng.sem_inc(s_oh, 1)
                    eng.wait_ge(s_p, 1)
                    then(eng.tensor_copy(tot[:].rearrange("p e n -> p (e n)"), ps[:, 1, 0:E0 * NT]))
                    then(eng.tensor_reduce(cnt[:], tot[:], AX, ALU.add))
                    then(eng.tensor_scalar(cnt[:], cnt[:], float(P - 1), None, ALU.add))
                    then(eng.tensor_copy(ci[:], cnt[:]))
                    then(eng.tensor_scalar(ci[:], ci[:], 7, 7, ALU.logical_shift_right, ALU.logical_shift_left))
                    then(eng.tensor_copy(cnt[:], ci[:]))
                    then(eng.tensor_tensor_scan(ends[:], cnt[:], self.zeros[:, 0:E0], 0.0, ALU.add, ALU.add))
                    then(eng.tensor_tensor(base[:], ends[:], cnt[:], ALU.subtract))
                    for e in range(E0):
                        do(eng.tensor_tensor_scan(incl[:, e, :], tot[:, e, :], self.zeros[:, 0:NT], base[:, e:e + 1], ALU.add, ALU.add))
                    do.wait()
                    then(eng.tensor_tensor(incl[:], incl[:], tot[:], ALU.subtract))
                    then(eng.tensor_tensor(w[:].rearrange("p e n -> p (e n)"), incl[:].rearrange("p e n -> p (e n)"),
                                           ps[:, 0, 0:E0 * NT], ALU.add))
                    then(eng.tensor_tensor(w[:], w[:], oh[:], ALU.mult))
                    then(eng.tensor_reduce(slotf[:], w[:].rearrange("p e n -> p n e"), AX, ALU.add))
                    do(eng.tensor_copy(slot[:], slotf[:]))
                    eng.wait_ge(s_c, 5)
                    for e in range(E0 - 1):
                        do(eng.tensor_scalar(te[:, e, :], starts[:], ends[:, e:e + 1], None, ALU.is_ge))
                    do.wait()
                    then(eng.tensor_tensor(te[:, 0, :], te[:, 0, :], te[:, 1, :], ALU.add))
                    then(eng.tensor_tensor(te[:, 0, :], te[:, 0, :], te[:, 2, :], ALU.add))
                    do(eng.tensor_copy(tile_expert[:], te[:, 0, :]))
                    do.wait()
                    eng.sem_inc(s_ix, 1)

                @block.tensor
                def _(eng):
                    eng.wait_ge(s_c, 5)
                    eng.wait_ge(s_oh, 1)
                    rhs = ohb[:].rearrange("p e n -> p (e n)")
                    eng.matmul(ps[:, 0, 0:E0 * NT], tri[:], rhs, start=True, stop=True)
                    eng.matmul(ps[:, 1, 0:E0 * NT], ones[:], rhs, start=True, stop=True).then_inc(s_p, 1)

                @block.gpsimd
                def _(eng):
                    eng.memset(tri[:], 0.0).then_inc(s_c, 1)
                    eng.memset(ones[:], 1.0).then_inc(s_c, 1)
                    eng.wait_ge(s_c, 2)
                    eng.affine_select(out=tri[:], in_=tri[:], compare_op=ALU.is_ge, fill=1.0, base=0,
                                      pattern=[[-1, P]], channel_multiplier=1).then_inc(s_c, 1)
                    eng.iota(starts[:], pattern=[[P, L0_TILES]], base=0, channel_multiplier=0,
                             allow_small_or_imprecise_dtypes=True).then_inc(s_c, 2)
                    eng.wait_ge(s_ix, 1)
                    eng.wait_ge(s_zero, 16)
                    for n in range(NT):
                        eng.indirect_dma_start(out=XS, out_offset=bass.IndirectOffsetOnAxis(ap=slot[:, n:n + 1], axis=0),
                                               in_=xx[:, n, :], in_offset=None).then_inc(s_sc, 16)
                    eng.wait_ge(s_sc, 16 * NT)

    def zero_rows(self, rows):
        return self.zeros[:, 0:D].unsqueeze(1).to_broadcast([P, rows, D])

    def top1_tiles(self, tile_expert, XS, YS):
        nc, t = self.nc, self.t
        MF = FF0 // P
        with ExitStack() as ctx:
            w1 = self.sb("w1", [P, 4, KD, FF0], ctx=ctx)
            w2 = self.sb("w2", [P, 4, MF, D], ctx=ctx)
            b1 = self.sb("b1", [P, 4, MF], ctx=ctx)
            b2 = self.sb("b2", [P, 4, D], ctx=ctx)
            xs = self.sb("xs", [P, 4, D], ctx=ctx)
            xT = self.sb("xT", [P, 2, KD, P], ctx=ctx)
            hT = self.sb("hT", [P, 2, MF, P], ctx=ctx)
            ys = self.sb("ys", [P, 2, D], ctx=ctx)
            px = self.ps("px", [P, 2, 512], ctx)
            ph = self.ps("ph", [P, 4, 512], ctx)
            py = self.ps("py", [P, 2, 512], ctx)
            s_x, s_xt, s_h, s_hv, s_ha, s_y, s_yb = (self.sem(n, ctx) for n in ("s_x", "s_xt", "s_h", "s_hv", "s_ha", "s_y", "s_yb"))
            s_w = [self.sem("s_w", ctx) for _ in range(4)]
            s_st = [self.sem("s_st", ctx) for _ in range(2)]
            LOADS = 5 * 16
            with nc.Block() as block:
                @block.sync
                def _(eng):
                    def step(at):
                        i, u, par = at.i, at.half, at.odd
                        if inside(i, L0_TILES):
                            need(eng, s_y, i - 3)
                            need(eng, s_yb, i - 3)
                            e = eng.value_load(tile_expert[0:1, bass.ds(i, 1)], min_val=0, max_val=E0 - 1)
                            one = bass.ds(e, 1)
                            eng.dma_start(xs[:, at.slot, :], XS[bass.ds(i * P, P), :]).then_inc(s_w[at.slot], 16)
                            eng.dma_start(w1[:, at.slot], t["L0_ffn_W1"][one].rearrange("o (k p) f -> p (o k) f", p=P)).then_inc(s_w[at.slot], 16)
                            eng.dma_start(b1[:, at.slot], t["L0_ffn_b1"][one].rearrange("o p m -> (o p) m")).then_inc(s_w[at.slot], 16)
                            eng.dma_start(b2[:, at.slot], t["L0_ffn_b2"][one].rearrange("o d -> (o d)").partition_broadcast(P)).then_inc(s_w[at.slot], 16)
                            eng.dma_start(w2[:, at.slot], t["L0_ffn_W2"][one].rearrange("o (m p) d -> p (o m) d", p=P)).then_inc(s_w[at.slot], 16)
                    steps(eng, step, L0_TILES, behind=0)

                @block.scalar
                def _(eng):
                    def step(at):
                        i, par = at.i, at.odd
                        a = at.back(1)
                        if inside(a.i, L0_TILES):
                            eng.wait_ge(s_h, a.i * 2 + 1)
                            need(eng, s_y, a.i - 1)
                            for m in range(MF // 2):
                                ins = eng.activation(hT[:, a.odd, m, :], ph[:, a.odd * 2, m * P:(m + 1) * P], ACT.Relu, bias=b1[:, a.slot, m:m + 1])
                            ins.then_inc(s_ha, 1)
                        if inside(i, L0_TILES):
                            eng.wait_ge(s_x, i + 1)
                            need(eng, s_h, (i - 1) * 2)
                            eng.copy(xT[:, par].rearrange("p k n -> p (k n)"), px[:, par, 0:KD * P]).then_inc(s_xt, 1)
                        b = at.back(2)
                        if inside(b.i, L0_TILES):
                            eng.wait_ge(s_yb, b.i + 1)
                            eng.dma_start(YS[bass.ds(b.i * P, P), :], ys[:, b.odd, :]).then_inc(s_st[b.odd], 16)
                    steps(eng, step, L0_TILES)
                    for s in s_st:
                        eng.wait_ge(s, 16 * L0_TILES // 2)

                @block.vector
                def _(eng):
                    def step(at):
                        i, par = at.i, at.odd
                        a = i - 1
                        if inside(a, L0_TILES):
                            eng.wait_ge(s_y, a + 1)
                            if not isinstance(a, int) or a >= 2:
                                eng.wait_ge(s_st[1 - par], (at.half if par else at.half - 1) * 16)
                            eng.tensor_tensor(ys[:, 1 - par, :], py[:, 1 - par, 0:D], b2[:, (at.slot - 1) % 4, :], ALU.add).then_inc(s_yb, 1)
                        if inside(i, L0_TILES):
                            eng.wait_ge(s_h, i * 2 + 2)
                            need(eng, s_y, i - 1)
                            for m in range(MF // 2, MF):
                                q = m - MF // 2
                                ins = eng.tensor_scalar(hT[:, par, m, :], ph[:, par * 2 + 1, q * P:(q + 1) * P], b1[:, at.slot, m:m + 1], 0.0,
                                                        ALU.add, ALU.max)
                            ins.then_inc(s_hv, 1)
                    steps(eng, step, L0_TILES, behind=1)

                @block.tensor
                def _(eng):
                    def up(at, half):
                        i, par = at.i, at.odd
                        need(eng, (s_ha, s_hv)[half], i - 1)
                        for m in range(MF // 2):
                            f = (half * (MF // 2) + m) * P
                            for k in range(KD):
                                ins = eng.matmul(ph[:, par * 2 + half, m * P:(m + 1) * P], w1[:, at.slot, k, f:f + P], xT[:, par, k, :],
                                                 start=(k == 0), stop=(k == KD - 1))
                        ins.then_inc(s_h, 1)

                    def step(at):
                        i, par = at.i, at.odd
                        a, b = at.back(1), at.back(2)
                        if inside(a.i, L0_TILES):
                            eng.wait_ge(s_xt, a.i + 1)
                            up(a, 0)
                        if inside(b.i, L0_TILES):
                            need(eng, s_yb, b.i - 1)
                            for m in range(MF):
                                if m % (MF // 2) == 0:
                                    eng.wait_ge((s_ha, s_hv)[m // (MF // 2)], b.i + 1)
                                ins = eng.matmul(py[:, b.odd, 0:D], hT[:, b.odd, m, :], w2[:, b.slot, m, :],
                                                 start=(m == 0), stop=(m == MF - 1))
                            ins.then_inc(s_y, 1)
                        if inside(i, L0_TILES):
                            eng.wait_ge(s_w[at.slot], (at.quarter + 1) * LOADS)
                            need(eng, s_xt, i - 1)
                            for k in range(KD):
                                ins = eng.transpose(px[:, par, k * P:(k + 1) * P], xs[:, at.slot, k * P:(k + 1) * P], self.ident[:])
                            ins.then_inc(s_x, 1)
                        if inside(a.i, L0_TILES):
                            up(a, 1)
                    steps(eng, step, L0_TILES)

    def combine_top1(self, xx, slot, YS, gain, shift, x):
        nc = self.nc
        with ExitStack() as ctx:
            grow, brow = (self.sb(n, [P, D], ctx=ctx) for n in ("grow", "brow"))
            y = self.sb("y", [P, NT, D], ctx=ctx)
            s_w, s_ch, s_mv, s_rs, s_z = (self.sem(n, ctx) for n in ("s_w", "s_ch", "s_mv", "s_rs", "s_z"))
            s_g = [self.sem("s_g", ctx) for _ in range(B)]
            with nc.Block() as block:
                @block.sync
                def _(eng):
                    eng.dma_start(grow[:], gain.partition_broadcast(P)).then_inc(s_w, 16)
                    eng.dma_start(brow[:], shift.partition_broadcast(P)).then_inc(s_w, 16)

                @block.gpsimd
                def _(eng):
                    for n in range(NT):
                        eng.indirect_dma_start(out=y[:, n, :], out_offset=None, in_=YS,
                                               in_offset=bass.IndirectOffsetOnAxis(ap=slot[:, n:n + 1], axis=0)).then_inc(s_g[n // ST], 16)

                def before(eng, chain, b):
                    eng.wait_ge(s_g[b], 16 * ST)
                    rows = slice(b * ST, (b + 1) * ST)
                    chain(eng.tensor_tensor(y[:, rows], y[:, rows], xx[:, rows], ALU.add))
                    chain.wait()
                rs = self.normalise(block, s_ch, s_mv, s_rs, s_z, y, y, ctx, gain=grow, shift=brow, before=before,
                                    ready=lambda eng: eng.wait_ge(s_w, 32))

                @block.scalar
                def _(eng):
                    self.deviations(eng, s_mv, s_rs, rs)

                @block.vector
                def _(eng):
                    eng.wait_ge(s_z, B)
                    eng.tensor_tensor(x[:], x[:], y[:], ALU.add)

    def route_and_share(self, src, z, zT, w_k, oh, scatter, gather, XS, YS, common_out):
        with ExitStack() as ctx:
            lgG, asG = (self.sb(n, [P, 2, P], ctx=ctx) for n in ("lgG", "asG"))
            pt = self.ps("pt", [P, 2, 512], ctx)
            with self.nc.Block() as block:
                turn_rows, take_rows, s_zT = self.norm_and_transpose(block, ctx, pt, 2, src, z, zT)

                @block.scalar
                def _(eng):
                    take_rows(eng)

                choose, turn = self.top2_gate(block, ctx, pt, zT, w_k, oh, lgG, asG)
                counts, s_ix = self.top2_capacity(block, ctx, pt, lgG, asG, oh, scatter, gather)
                shared = self.shared(block, ctx, z, zT, common_out, scatter, s_ix, XS, YS)

                @block.tensor
                def _(eng):
                    def between():
                        if counts:
                            counts.pop(0)(eng)

                    turn_rows(eng)
                    eng.wait_ge(s_zT, KD * B)
                    choose(eng)
                    shared(eng, range(0, 1), lambda: None)
                    counts[:0] = [lambda eng: None] * 3 + [turn]
                    shared(eng, range(1, B), between)
                    while counts:
                        between()

    def top2_gate(self, block, ctx, pt, zT, w_k, oh, lgG, asG):
        nc, t = self.nc, self.t
        G = [P, NT, E1]
        gw = self.sb("gw", [P, KD, E1], ctx=ctx)
        gb = self.sb("gb", [P, E1], ctx=ctx)
        rev = self.sb("rev", [P, E1], ctx=ctx)
        lg, sc, tmp = (self.sb(n, G, ctx=ctx) for n in ("lg", "sc", "tmp"))
        m = self.sb("m", [P, NT], ctx=ctx)
        s_w, s_c, s_l, s_ch, s_d, s_e, s_as, s_t = (self.sem(n, ctx) for n in
                                                   ("s_w", "s_c", "s_l", "s_ch", "s_d", "s_e", "s_as", "s_t"))
        grouped = self.sb("grouped", [P, 2, 2, P], ctx=ctx)

        def per_token(a):
            return a[:].unsqueeze(2).to_broadcast(G)

        def per_expert(a):
            return a[:].unsqueeze(1).to_broadcast(G)

        @block.sync
        def _(eng):
            eng.dma_start(gw[:], t["L1_ffn_gate_w"].rearrange("(k p) e -> p k e", p=P)).then_inc(s_w, 16)
            eng.dma_start(gb[:], t["L1_ffn_gate_b"].partition_broadcast(P)).then_inc(s_w, 16)

        @block.gpsimd
        def _(eng):
            eng.iota(rev[:], pattern=[[-1, E1]], base=E1, channel_multiplier=0,
                     allow_small_or_imprecise_dtypes=True).then_inc(s_c, 1)

        def choose(eng):
            eng.wait_ge(s_w, 32)
            for n in range(NT):
                for k in range(KD):
                    ins = eng.matmul(pt[:, 0, n * E1:(n + 1) * E1], zT[:, k, n * P:(n + 1) * P], gw[:, k, :],
                                     start=(k == 0), stop=(k == KD - 1))
            ins.then_inc(s_l, 1)

        def turn(eng):
            eng.wait_ge(s_as, 1)
            for x in range(2):
                for h in range(2):
                    ins = eng.transpose(pt[:, x, h * P:(h + 1) * P], grouped[:, x, h, :], self.ident[:])
            ins.then_inc(s_t, 1)

        @block.scalar
        def _(eng):
            eng.wait_ge(s_d, 1)
            eng.activation(sc[:], tmp[:], ACT.Exp).then_inc(s_e, 1)

        @block.vector
        def _(eng):
            do = Chain(eng, s_ch)

            def then(ins):
                do(ins)
                do.wait()

            eng.wait_ge(s_w, 32)
            eng.wait_ge(s_c, 1)
            eng.wait_ge(s_l, 1)
            then(eng.tensor_copy(lg[:].rearrange("p n e -> p (n e)"), pt[:, 0, 0:NT * E1]))
            then(eng.tensor_reduce(m[:], lg[:], AX, ALU.max))
            eng.tensor_tensor(tmp[:], lg[:], per_token(m), ALU.subtract).then_inc(s_d, 1)
            eng.wait_ge(s_e, 1)
            then(eng.tensor_reduce(m[:], sc[:], AX, ALU.add))
            then(eng.reciprocal(m[:], m[:]))
            then(eng.tensor_tensor(sc[:], sc[:], per_token(m), ALU.mult))
            then(eng.tensor_tensor(sc[:], sc[:], per_expert(gb), ALU.add))
            for k in range(TOPK):
                then(eng.tensor_reduce(m[:], sc[:], AX, ALU.max))
                then(eng.tensor_tensor(tmp[:], sc[:], per_token(m), ALU.is_equal))
                then(eng.tensor_tensor(tmp[:], tmp[:], per_expert(rev), ALU.mult))
                then(eng.tensor_reduce(m[:], tmp[:], AX, ALU.max))
                then(eng.tensor_tensor(oh[:, k], per_expert(rev), per_token(m), ALU.is_equal))
                then(eng.tensor_tensor(tmp[:], oh[:, k], lg[:], ALU.mult))
                then(eng.tensor_reduce(w_k[:, k, :], tmp[:], AX, ALU.add))
                if k + 1 < TOPK:
                    then(eng.scalar_tensor_tensor(out=sc[:], in0=oh[:, k], scalar=LOWEST, in1=sc[:], op0=ALU.mult, op1=ALU.add))

            def of(a, h):
                return a.rearrange("p (g h) e -> p h g e", h=2)[:, h]

            for h in range(2):
                do(eng.tensor_copy(grouped[:, 0, h].rearrange("p (g e) -> p g e", e=E1), of(lg[:], h)))
                do(eng.tensor_tensor(grouped[:, 1, h].rearrange("p (g e) -> p g e", e=E1), of(oh[:, 0], h), of(oh[:, 1], h), ALU.add))
            do.wait()
            eng.sem_inc(s_as, 1)
            eng.wait_ge(s_t, 1)
            for x, dst in enumerate((lgG, asG)):
                do(eng.tensor_copy(dst[:].rearrange("p h t -> p (h t)"), pt[:, x, 0:2 * P]))
            do.wait()

        return choose, turn

    def top2_capacity(self, block, ctx, pt, lgG, asG, oh, scatter, gather):
        R = [P, 2 * P]
        G = [P, NT, E1]
        flip = self.sb("flip", R, I32, ctx=ctx)
        hi, lo, t0, t1 = (self.sb(n, R, ctx=ctx) for n in ("hi", "lo", "t0", "t1"))
        thr, cand, bit, cnt, want, gain, first, off = (self.sb(n, [P, 1], ctx=ctx) for n in
                                                       ("thr", "cand", "bit", "cnt", "want", "gain", "first", "off"))
        e_of = self.sb("e_of", [P, 1], I32, ctx=ctx)
        same = self.sb("same", [P, P], ctx=ctx)
        before = self.sb("before", [P, P], ctx=ctx)
        own = self.sb("own", [P, TOPK, NT], ctx=ctx)
        pos, kept, tmp = (self.sb(n, G, ctx=ctx) for n in ("pos", "kept", "tmp"))
        pk, kk, idx = (self.sb(n, [P, TOPK, NT], ctx=ctx) for n in ("pk", "kk", "idx"))
        s_c, s_ch, s_k, s_t, s_q, s_r, s_ix = (self.sem(n, ctx) for n in ("s_c", "s_ch", "s_k", "s_t", "s_q", "s_r", "s_ix"))
        BITS = 16
        total = pt[:, 0, 2 * P:2 * P + 1]

        @block.gpsimd
        def _(eng):
            do = Chain(eng, s_c)
            do(eng.iota(own[:], pattern=[[N, TOPK], [P, NT]], base=DROP_ROW, channel_multiplier=1,
                        allow_small_or_imprecise_dtypes=True))
            do(eng.iota(e_of[:], pattern=[[0, 1]], base=0, channel_multiplier=1))
            do(eng.memset(before[:], 0.0))

            def near(a, groups):
                do.wait()
                do(eng.affine_select(out=a[:], in_=a[:], compare_op=ALU.not_equal, fill=1.0, base=groups * E1,
                                     pattern=[[-1, P]], channel_multiplier=1))

            for groups in range(1, P // E1):
                near(before, groups)
            do.wait()
            do(eng.tensor_copy(same[:], before[:]))
            for groups in range(0, -(P // E1), -1):
                near(same, groups)
            self.n_setup = do.value()

        def add_up(matrix, n):
            def part(eng):
                eng.wait_ge(s_q, n + 1)
                eng.matmul(total, matrix[:], cnt[:], start=True, stop=True).then_inc(s_r, 1)
            return part

        def positions(eng):
            eng.wait_ge(s_k, 1)
            for x, src in enumerate((t1, t0)):
                for h in range(2):
                    ins = eng.transpose(pt[:, x, h * P:(h + 1) * P], src[:, h * P:(h + 1) * P], self.ident[:])
            ins.then_inc(s_t, 1)

        n_same = 2 * (BITS + 1)
        parts = [add_up(same if n < n_same else before, n) for n in range(n_same + 2)] + [positions]

        @block.vector
        def _(eng):
            do = Chain(eng, s_ch)

            def then(ins):
                do(ins)
                do.wait()

            asked = 0

            def add(ins, i=None):
                ins.then_inc(s_q, 1)
                eng.wait_ge(s_r, asked + 1 + (0 if i is None else i))

            def count(src, than, op, i=None):
                add(eng.tensor_scalar(t0[:], src[:], than, 0.0, op, ALU.add, accum_out=cnt[:]), i)

            def search(src):
                then(eng.memset(cand[:], 32768.0))
                then(eng.memset(bit[:], 32768.0))
                with eng.Fori(0, BITS) as i:
                    do.enter(i, 3)
                    count(src, cand[:, 0:1], ALU.is_ge, i)
                    then(eng.tensor_scalar(gain[:], total, want[:, 0:1], 0.5, ALU.is_ge, ALU.subtract))
                    then(eng.scalar_tensor_tensor(out=cand[:], in0=gain[:], scalar=bit[:, 0:1], in1=cand[:], op0=ALU.mult, op1=ALU.add))
                    then(eng.tensor_scalar(bit[:], bit[:], 0.5, None, ALU.mult))
                    do.leave(BITS)
                then(eng.tensor_scalar(thr[:], cand[:], -0.5, None, ALU.add))

            bits = lgG[:].rearrange("p h t -> p (h t)").bitcast(I32)
            chosen = asG[:].rearrange("p h t -> p (h t)")
            then(eng.tensor_scalar(flip[:], bits, 31, None, ALU.arith_shift_right))
            then(eng.tensor_scalar(flip[:], flip[:], -2147483648, None, ALU.bitwise_or))
            then(eng.tensor_tensor(flip[:], flip[:], bits, ALU.bitwise_xor))
            then(eng.tensor_scalar(t0[:].bitcast(I32), flip[:], 16, 0xffff, ALU.logical_shift_right, ALU.bitwise_and))
            then(eng.tensor_copy(hi[:], t0[:].bitcast(I32)))
            then(eng.tensor_scalar(t1[:].bitcast(I32), flip[:], 0xffff, None, ALU.bitwise_and))
            then(eng.tensor_copy(lo[:], t1[:].bitcast(I32)))
            then(eng.scalar_tensor_tensor(out=hi[:], in0=hi[:], scalar=1.0, in1=chosen, op0=ALU.add, op1=ALU.mult))
            then(eng.tensor_scalar(hi[:], hi[:], -1.0, None, ALU.add))
            then(eng.memset(want[:], float(CAP)))
            eng.wait_ge(s_c, self.n_setup)
            then(eng.tensor_scalar(e_of[:], e_of[:], E1 - 1, None, ALU.bitwise_and))
            then(eng.tensor_copy(first[:], e_of[:]))
            then(eng.tensor_scalar(first[:], first[:], float(CAP), -1.0, ALU.mult, ALU.add))
            search(hi)
            asked += BITS
            count(hi, thr[:, 0:1], ALU.is_gt)
            asked += 1
            then(eng.tensor_tensor(want[:], want[:], total, ALU.subtract))
            then(eng.tensor_scalar(t1[:], hi[:], thr[:, 0:1], None, ALU.is_equal))
            then(eng.scalar_tensor_tensor(out=lo[:], in0=lo[:], scalar=1.0, in1=t1[:], op0=ALU.add, op1=ALU.mult))
            then(eng.tensor_scalar(lo[:], lo[:], -1.0, None, ALU.add))
            then(eng.tensor_copy(hi[:], t0[:]))
            search(lo)
            asked += BITS
            count(lo, thr[:, 0:1], ALU.is_gt)
            asked += 1
            then(eng.tensor_tensor(want[:], want[:], total, ALU.subtract))
            then(eng.tensor_tensor(hi[:], hi[:], t0[:], ALU.add))
            add(eng.tensor_scalar(lo[:], lo[:], thr[:, 0:1], 0.0, ALU.is_equal, ALU.add, accum_out=cnt[:]))
            asked += 1
            then(eng.tensor_copy(off[:], total))
            zeros = self.zeros[:, 0:2 * P]
            then(eng.tensor_tensor_scan(t1[:], lo[:], zeros, off[:, 0:1], ALU.add, ALU.add))
            then(eng.tensor_scalar(t1[:], t1[:], want[:, 0:1], None, ALU.is_le))
            then(eng.tensor_tensor(t1[:], t1[:], lo[:], ALU.mult))
            then(eng.tensor_tensor(t0[:], hi[:], t1[:], ALU.add))
            add(eng.tensor_reduce(cnt[:], t0[:], AX, ALU.add))
            then(eng.tensor_tensor(off[:], first[:], total, ALU.add))
            then(eng.tensor_tensor_scan(t1[:], t0[:], zeros, off[:, 0:1], ALU.add, ALU.add))
            eng.sem_inc(s_k, 1)
            eng.wait_ge(s_t, 1)
            for x, dst in enumerate((pos, kept)):
                for h in range(2):
                    do(eng.tensor_copy(dst[:].rearrange("p (g h) e -> p h g e", h=2)[:, h],
                                       pt[:, x, h * P:(h + 1) * P].rearrange("p (g e) -> p g e", e=E1)))
            do.wait()
            for k in range(TOPK):
                then(eng.tensor_tensor(tmp[:], oh[:, k], pos[:], ALU.mult))
                then(eng.tensor_reduce(pk[:, k, :], tmp[:], AX, ALU.add))
                then(eng.tensor_tensor(tmp[:], oh[:, k], kept[:], ALU.mult))
                then(eng.tensor_reduce(kk[:, k, :], tmp[:], AX, ALU.add))
            then(eng.tensor_tensor(idx[:], pk[:], own[:], ALU.subtract))
            then(eng.tensor_tensor(idx[:], idx[:], kk[:], ALU.mult))
            then(eng.tensor_tensor(idx[:], idx[:], own[:], ALU.add))
            then(eng.tensor_copy(scatter[:], idx[:]))
            eng.sem_inc(s_ix, 1)
            then(eng.tensor_scalar(idx[:], pk[:], float(-ZERO_ROW), None, ALU.add))
            then(eng.tensor_tensor(idx[:], idx[:], kk[:], ALU.mult))
            then(eng.tensor_scalar(idx[:], idx[:], float(ZERO_ROW), None, ALU.add))
            then(eng.tensor_copy(gather[:], idx[:]))

        return parts, s_ix

    def shared(self, block, ctx, z, zT, out, scatter, s_ix, XS, YS):
        t = self.t
        MF = FSH // P
        w1, w3 = (self.sb(n, [P, KD, FSH], ctx=ctx) for n in ("w1", "w3"))
        w2 = self.sb("w2", [P, MF, D], ctx=ctx)
        act, p3c = (self.sb(n, [P, 2, S], ctx=ctx) for n in ("act", "p3c"))
        g = self.sb("g", [P, 2, MF, S], ctx=ctx)
        p1, p3, py = (self.ps(n, [P, 2, 512], ctx) for n in ("p1", "p3", "py"))
        s_w, s_h, s_a, s_g, s_y, s_x, s_zero = (self.sem(n, ctx) for n in ("s_w", "s_h", "s_a", "s_g", "s_y", "s_x", "s_zero"))
        s_s = self.sem("s_s", ctx)

        @block.sync
        def _(eng):
            for w, src in ((w1, t["L1_ffn_sw1"]), (w3, t["L1_ffn_sw3"])):
                for k in range(KD):
                    eng.dma_start(w[:, k].rearrange("p (s f) -> p s f", s=NSH),
                                  src[:, k * P:(k + 1) * P, :].rearrange("s p f -> p s f")).then_inc(s_w, 16)
            eng.dma_start(w2[:], t["L1_ffn_sw2"].rearrange("s (m p) d -> p (s m) d", p=P)).then_inc(s_w, 16)
            eng.dma_start(XS[0:L1_SLOTS].rearrange("(p r) d -> p r d", p=P), self.zero_rows(L1_SLOTS // P)).then_inc(s_zero, 16)
            eng.dma_start(YS[ZERO_ROW:ZERO_ROW + P], self.zeros[:, 0:D]).then_inc(s_zero, 16)
            eng.wait_ge(s_zero, 32)

        def down(eng, c, between):
            for j in range(ST):
                n = c * ST + j
                if j == 0:
                    eng.wait_ge(s_g, (c + 1) * MF)
                need(eng, s_x, n - 1)
                for m in range(MF):
                    ins = eng.matmul(py[:, n % 2, 0:D], g[:, c % 2, m, j * P:(j + 1) * P], w2[:, m, :],
                                     start=(m == 0), stop=(m == MF - 1))
                    if m == MF // 2:
                        between()
                ins.then_inc(s_y, 1)
                between()

        def tensor(eng, batches, between):
            for c in batches:
                if c == 0:
                    eng.wait_ge(s_w, 80)
                for m in range(MF):
                    q = c * MF + m
                    need(eng, s_a, (q - 1) * 2)
                    for w, bank in ((w1, p1), (w3, p3)):
                        for k in range(KD):
                            ins = eng.matmul(bank[:, q % 2, :], w[:, k, m * P:(m + 1) * P], zT[:, k, c * S:(c + 1) * S],
                                             start=(k == 0), stop=(k == KD - 1))
                        if w is w1:
                            between()
                    ins.then_inc(s_h, 1)
                    between()
                if c:
                    down(eng, c - 1, between)
                if c == B - 1:
                    down(eng, c, between)

        @block.scalar
        def _(eng):
            def take(c):
                for j in range(ST):
                    n = c * ST + j
                    eng.wait_ge(s_y, n + 1)
                    eng.copy(out[:, n, :], py[:, n % 2, 0:D]).then_inc(s_x, 1)

            for c in range(B):
                for m in range(MF):
                    q = c * MF + m
                    eng.wait_ge(s_h, q + 1)
                    need(eng, s_g, q - 1)
                    eng.activation(act[:, q % 2, :], p1[:, q % 2, :], ACT.Silu).then_inc(s_a, 1)
                    eng.copy(p3c[:, q % 2, :], p3[:, q % 2, :]).then_inc(s_a, 1)
                if c:
                    take(c - 1)
            take(B - 1)

        def dispatch(eng, n):
            if n == 0:
                eng.wait_ge(s_ix, 1)
                eng.wait_ge(s_zero, 32)
            for k in range(TOPK):
                eng.indirect_dma_start(out=XS, out_offset=bass.IndirectOffsetOnAxis(ap=scatter[:, k, n:n + 1], axis=0),
                                       in_=z[:, n, :], in_offset=None).then_inc(s_s, 16)

        @block.gpsimd
        def _(eng):
            for c in range(B):
                for m in range(MF):
                    q = c * MF + m
                    eng.wait_ge(s_a, (q + 1) * 2)
                    need(eng, s_y, (c - 1) * ST)
                    eng.tensor_tensor(g[:, c % 2, m, :], act[:, q % 2, :], p3c[:, q % 2, :], ALU.mult).then_inc(s_g, 1)
                    if c == B - 1:
                        dispatch(eng, m)
            for n in range(MF, NT):
                dispatch(eng, n)
            eng.wait_ge(s_s, 16 * NT * TOPK)

        return tensor

    def experts(self, XS, YS):
        nc, t = self.nc, self.t
        MF = FF1 // P
        NTL = len(CAP_TILES)
        with ExitStack() as ctx:
            w1, w3 = (self.sb(n, [P, 4, KD, FF1], ctx=ctx) for n in ("w1", "w3"))
            w2 = self.sb("w2", [P, 4, MF, D], ctx=ctx)
            xs = self.sb("xs", [P, 4, NTL, D], ctx=ctx)
            xT = self.sb("xT", [P, 2, KD, CAP], ctx=ctx)
            act = self.sb("act", [P, 2, CAP], ctx=ctx)
            g = self.sb("g", [P, 2, MF, CAP], ctx=ctx)
            ys = self.sb("ys", [P, 2, NTL, D], ctx=ctx)
            px = self.ps("px", [P, KD, 512], ctx)
            p1 = self.ps("p1", [P, 2, 512], ctx)
            p3 = self.ps("p3", [P, 2, 512], ctx)
            py = self.ps("py", [P, 2, 512], ctx)
            s_x, s_xt, s_h, s_a, s_g, s_y, s_yb = (self.sem(n, ctx) for n in ("s_x", "s_xt", "s_h", "s_a", "s_g", "s_y", "s_yb"))
            s_w = [self.sem("s_w", ctx) for _ in range(4)]
            s_st = [self.sem("s_st", ctx) for _ in range(2)]
            LOADS = (3 + NTL) * 16
            with nc.Block() as block:
                @block.sync
                def _(eng):
                    def step(at):
                        i, u, par = at.i, at.half, at.odd
                        if not inside(i, E1):
                            return
                        need(eng, s_y, (i - 3) * NTL)
                        one = bass.ds(i, 1)
                        for w, src in ((w1, "L1_ffn_ew1"), (w3, "L1_ffn_ew3"), (w2, "L1_ffn_ew2")):
                            eng.dma_start(w[:, at.slot], t[src][one].rearrange("o (k p) f -> p (o k) f", p=P)).then_inc(s_w[at.slot], 16)
                        for j, (s, rows) in enumerate(CAP_TILES):
                            eng.dma_start(xs[0:rows, at.slot, j, :], XS[bass.ds(i * CAP + s, rows), :]).then_inc(s_w[at.slot], 16)
                    steps(eng, step, E1, behind=0)

                @block.tensor
                def _(eng):
                    def up(at, m):
                        i = at.i
                        need(eng, s_g, i * MF + m - 1)
                        for w, bank in ((w1, p1), (w3, p3)):
                            for k in range(KD):
                                ins = eng.matmul(bank[:, m % 2, 0:CAP], w[:, at.slot, k, m * P:(m + 1) * P], xT[:, at.odd, k, :],
                                                 start=(k == 0), stop=(k == KD - 1))
                        ins.then_inc(s_h, 1)

                    def step(at):
                        i = at.i
                        a, b = at.back(1), at.back(2)
                        if inside(a.i, E1):
                            eng.wait_ge(s_xt, (a.i + 1) * KD)
                            up(a, 0)
                        if inside(b.i, E1):
                            eng.wait_ge(s_g, (b.i + 1) * MF)
                            for j, (s, rows) in enumerate(CAP_TILES):
                                need(eng, s_yb, b.i * NTL + j - 1)
                                for m in range(MF):
                                    ins = eng.matmul(py[0:rows, (b.odd + j) % 2, 0:D], g[:, b.odd, m, s:s + rows], w2[:, b.slot, m, :],
                                                     start=(m == 0), stop=(m == MF - 1))
                                ins.then_inc(s_y, 1)
                        if inside(a.i, E1):
                            for m in range(1, MF - 1):
                                up(a, m)
                        if inside(i, E1):
                            eng.wait_ge(s_w[at.slot], (at.quarter + 1) * LOADS)
                            need(eng, s_xt, i * KD)
                            for k in range(KD):
                                for j, (s, rows) in enumerate(CAP_TILES):
                                    ins = eng.transpose(px[:, k, s:s + rows], xs[0:rows, at.slot, j, k * P:(k + 1) * P],
                                                        self.ident[0:rows, 0:rows])
                                ins.then_inc(s_x, 1)
                        if inside(a.i, E1):
                            up(a, MF - 1)
                    steps(eng, step, E1)

                @block.scalar
                def _(eng):
                    def gate(a, m):
                        if inside(a.i, E1):
                            eng.wait_ge(s_h, a.i * MF + m + 1)
                            need(eng, s_g, a.i * MF + m - 1)
                            eng.activation(act[:, m % 2, :], p1[:, m % 2, 0:CAP], ACT.Silu).then_inc(s_a, 1)

                    def step(at):
                        i, par = at.i, at.odd
                        a, b = at.back(1), at.back(2)
                        for m in range(MF - 1):
                            gate(a, m)
                        if inside(i, E1):
                            for k in range(KD):
                                eng.wait_ge(s_x, i * KD + k + 1)
                                if k == 0:
                                    need(eng, s_h, (i - 1) * MF)
                                eng.copy(xT[:, par, k, :], px[:, k, 0:CAP]).then_inc(s_xt, 1)
                        gate(a, MF - 1)
                        if inside(b.i, E1):
                            eng.wait_ge(s_yb, (b.i + 1) * NTL)
                            for j, (s, rows) in enumerate(CAP_TILES):
                                eng.dma_start(YS[bass.ds(b.i * CAP + s, rows), :], ys[0:rows, b.odd, j, :]).then_inc(s_st[b.odd], 16)
                    steps(eng, step, E1)
                    for s in s_st:
                        eng.wait_ge(s, 16 * NTL * E1 // 2)

                @block.vector
                def _(eng):
                    def gated(i, par, m):
                        eng.wait_ge(s_a, i * MF + m + 1)
                        if m == 0:
                            need(eng, s_y, (i - 1) * NTL)
                        eng.tensor_tensor(g[:, par, m, :], act[:, m % 2, :], p3[:, m % 2, 0:CAP], ALU.mult).then_inc(s_g, 1)

                    def step(at):
                        i, par = at.i, at.odd
                        if inside(i, E1):
                            gated(i, par, 0)
                        a = i - 1
                        if inside(a, E1):
                            if not isinstance(a, int) or a >= 2:
                                eng.wait_ge(s_st[1 - par], (at.half if par else at.half - 1) * 16 * NTL)
                            for j, (s, rows) in enumerate(CAP_TILES):
                                eng.wait_ge(s_y, a * NTL + j + 1)
                                eng.tensor_copy(ys[0:rows, 1 - par, j, :], py[0:rows, (1 - par + j) % 2, 0:D]).then_inc(s_yb, 1)
                        if inside(i, E1):
                            for m in range(1, MF):
                                gated(i, par, m)
                    steps(eng, step, E1, behind=1)

    def combine_top2(self, gather, w_k, YS, common, x):
        nc = self.nc
        with ExitStack() as ctx:
            y = self.sb("y", [P, NT, TOPK, D], ctx=ctx)
            s_g, s_ch = [self.sem("s_g", ctx) for _ in range(4)], self.sem("s_ch", ctx)
            s_b, s_o = self.sem("s_b", ctx), self.sem("s_o", ctx)
            with nc.Block() as block:
                @block.sync
                def _(eng):
                    for b in range(B):
                        eng.wait_ge(s_b, b + 1)
                        eng.dma_start(self.out[b].rearrange("(t p) d -> p t d", p=P), x[:, b * ST:(b + 1) * ST, :]).then_inc(s_o, 16)
                    eng.wait_ge(s_o, 16 * B)

                @block.gpsimd
                def _(eng):
                    for n in range(NT):
                        for k in range(TOPK):
                            eng.indirect_dma_start(out=y[:, n, k, :], out_offset=None, in_=YS,
                                                   in_offset=bass.IndirectOffsetOnAxis(ap=gather[:, k, n:n + 1], axis=0))\
                               .then_inc(s_g[n // ST], 16)

                @block.vector
                def _(eng):
                    do = Chain(eng, s_ch)
                    do(eng.scalar_tensor_tensor(out=x[:], in0=common[:], scalar=1.0 / NSH, in1=x[:], op0=ALU.mult, op1=ALU.add))
                    do.wait()
                    for b in range(B):
                        eng.wait_ge(s_g[b], 16 * ST * TOPK)
                        for k in range(TOPK):
                            for n in range(b * ST, (b + 1) * ST):
                                do(eng.scalar_tensor_tensor(out=x[:, n, :], in0=y[:, n, k, :], scalar=w_k[:, k, n:n + 1], in1=x[:, n, :],
                                                            op0=ALU.mult, op1=ALU.add))
                            do.wait()
                        eng.sem_inc(s_b, 1)


def build(nc, t, out):
    p = Program(nc, t, out)
    with p.ctx:
        early = ExitStack()
        p.place(early)
        QS = p.dram("q_stacks", [2, NBH, DK, S])
        KS = p.dram("k_stacks", [2, NBH, DK, S])
        with ExitStack() as ctx:
            V = p.sb("V", [P, NBH, ST, VW], F32R, ctx=ctx)
            O = p.sb("O", [P, NT, D], ctx=ctx)
            with ExitStack() as inner:
                zT = p.sb("zT", [P, KD, N], ctx=inner)
                cT = p.sb("cT", [P, KD, N], ctx=inner)
                mask = p.dram("mask", [B, P, ST, S], BF16)
                p.project(p.x, O, zT, cT, t["ctx_1024"], t["L0_xattn_Wq"], t["L0_xattn_Wk"], t["L0_xattn_Wv"], None, None, None,
                          1.0, QS, KS, V, mask, first=True)
            p.attention("mask", QS, KS, V, O, DK ** -0.5, mask=mask)
            p.output(O, t["L0_xattn_Wo"], None, p.x, p.x)
        with ExitStack() as ctx:
            f = {n[7:]: v for n, v in t.items() if n.startswith("L0_ffn_")}
            src = p.sb("src", [P, NT, D], ctx=ctx)
            xx = p.sb("xx", [P, NT, D], ctx=ctx)
            slot = p.sb("slot", [P, NT], U32, ctx=ctx)
            tile_expert = p.sb("tile_expert", [P, L0_TILES], I32, ctx=ctx)
            XS = p.dram("top1_in", [L0_SLOTS, D])
            YS = p.dram("top1_out", [L0_SLOTS, D])
            with ExitStack() as inner:
                V = p.sb("V", [P, NBH, ST, VW], F32R, ctx=inner)
                O = p.sb("O", [P, NT, D], ctx=inner)
                with ExitStack() as deep:
                    sT = p.sb("sT", [P, KD, N], ctx=deep)
                    p.project(p.x, src, sT, sT, None, f["Wq"], f["Wk"], f["Wv"], f["bq"], f["bk"], f["bv"], DK ** -0.5, QS, KS, V)
                p.attention("self", QS, KS, V, O, 1.0)
                p.output(O, f["Wo"], f["bo"], src, src)
            p.route_top1(src, xx, f["ln1_g"], f["ln1_b"], slot, tile_expert, XS)
            p.top1_tiles(tile_expert, XS, YS)
            p.combine_top1(xx, slot, YS, f["ln2_g"], f["ln2_b"], p.x)
        p.recycle()
        with ExitStack() as ctx:
            f = {n[9:]: v for n, v in t.items() if n.startswith("L1_xattn_")}
            V = p.sb("V", [P, NBH, ST, VW], F32R, ctx=ctx)
            O = p.sb("O", [P, NT, D], ctx=ctx)
            common = p.sb("common", [P, B, ST, S], ctx=ctx)
            with ExitStack() as inner:
                zT = p.sb("zT", [P, KD, N], ctx=inner)
                cT = p.sb("cT", [P, KD, N], ctx=inner)
                p.project(p.x, O, zT, cT, t["ctx_1024"], f["Wq"], f["Wk"], f["Wv"], f["bq"], f["bk"], f["bv"], DK ** -0.5 / 2, QS, KS, V, common=common)
            side = t["fside_Bx16xSxS2_0"].rearrange("b h (t p) k -> (b h) p t k", p=P)
            p.attention("side", QS, KS, V, O, 2.0, common=common, side=side)
            p.output(O, f["Wo"], f["bo"], p.x, p.x)
        early.close()
        with ExitStack() as ctx:
            w_k = p.sb("w_k", [P, TOPK, NT], ctx=ctx)
            oh = p.sb("oh", [P, TOPK, NT, E1], ctx=ctx)
            scatter = p.sb("scatter", [P, TOPK, NT], U32, ctx=ctx)
            gather = p.sb("gather", [P, TOPK, NT], U32, ctx=ctx)
            common = p.sb("common", [P, NT, D], ctx=ctx)
            XS = p.dram("top2_in", [L1_ROWS, D])
            YS = p.dram("top2_out", [ZERO_ROW + P, D])
            with ExitStack() as inner:
                z = p.sb("z", [P, NT, D], ctx=inner)
                zT = p.sb("zT", [P, KD, N], ctx=inner)
                p.route_and_share(p.x, z, zT, w_k, oh, scatter, gather, XS, YS, common)
            p.experts(XS, YS)
            p.combine_top2(gather, w_k, YS, common, p.x)


_TRANSPOSED = ("L0_xattn_Wq", "L0_xattn_Wk", "L0_xattn_Wv", "L0_xattn_Wo", "L1_xattn_Wq", "L1_xattn_Wk", "L1_xattn_Wv",
               "L1_xattn_Wo", "ctx_1024")


def kernel(**inputs):
    import numpy as np
    import concourse.bacc as bacc
    from concourse.bass_utils import run_bass_kernel_spmd

    nc = bacc.Bacc("TRN2", target_bir_lowering=False, num_devices=1)
    arrays, t = {}, {}
    for name, a in inputs.items():
        a = np.asarray(a)
        if name in _TRANSPOSED:
            a = a.reshape(-1, a.shape[-1]).T
        if name == "L0_ffn_b1":
            a = a.reshape(E0, -1, P).transpose(0, 2, 1)
        if name[-3:] in ("_bq", "_bk"):
            a = a.reshape(KD, P).T
        a = np.ascontiguousarray(a)
        arrays[f"in_{name}"] = a
        t[name] = nc.dram_tensor(f"in_{name}", a.shape, mybir.dt.from_np(a.dtype), kind="ExternalInput").ap()
    out = nc.dram_tensor("out", [B, S, D], F32, kind="ExternalOutput").ap()
    build(nc, t, out)
    r = run_bass_kernel_spmd(nc, [arrays], core_ids=[0])
    return r.results[0]["out"]
```
